# Optimizing a Trainium2 kernel written in Bass

```python
import numpy as np
import jax
import jax.numpy as jnp

def _softmax(x, axis=-1):
    return jax.nn.softmax(x, axis=axis)

def _gelu(x):
    return jax.nn.gelu(x, approximate=True)

def _silu(x):
    return jax.nn.silu(x)

def _sigmoid(x):
    return jax.nn.sigmoid(x)

def _layernorm(x, axis=-1, eps=1e-05):
    m = jnp.mean(x, axis=axis, keepdims=True)
    v = jnp.var(x, axis=axis, keepdims=True)
    return (x - m) / jnp.sqrt(v + eps)

def _scatter_add(tgt, idx, src, axis=0):
    return tgt.at[idx].add(src)

def _segment_sum(src, seg, n):
    return jax.ops.segment_sum(src, seg, n)
kernel_name = 'mk_seq_preln_d2_jaxref_r8_327f8a'

def setup_inputs(seed: int=0):
    np.random.seed(seed)
    _w = jnp.asarray

    def _L0_attn_setup():
        import jax, jax.numpy as jnp
        import numpy as np
        B, T, H, NUM_LAYERS = (8, 512, 128, 2)

        def _log_g(x):
            return jnp.where(x >= 0.0, jnp.log(jax.nn.relu(x) + 0.5), -jax.nn.softplus(-x))

        def _heinsen_scan(log_coeffs, log_values):
            a_star = jnp.cumsum(log_coeffs, axis=1)
            return jnp.exp(a_star + jax.lax.cumlogsumexp(log_values - a_star, axis=1))
        key = jax.random.key(seed)
        k0, k1, k2 = jax.random.split(key, 3)
        scale = 1.0 / np.sqrt(H)
        return {'h': jax.random.normal(k0, (B, T, H), dtype=jnp.float32), 'W0': jax.random.normal(k1, (H, 3 * H), dtype=jnp.float32) * scale, 'W1': jax.random.normal(k2, (H, 3 * H), dtype=jnp.float32) * scale}
    _L0_attn_in = _L0_attn_setup()

    def _L0_ffn_setup():
        import jax, jax.numpy as jnp
        import numpy as np
        B, L, D, F, E = (2, 128, 128, 512, 8)
        key = jax.random.key(seed)
        ks = jax.random.split(key, 7)
        return {'x': jax.random.normal(ks[0], (B, L, D), dtype=jnp.float32), 'router_w': jax.random.normal(ks[1], (D, E), dtype=jnp.float32) * 0.02, 'router_b': jax.random.normal(ks[2], (E,), dtype=jnp.float32) * 0.02, 'W1': jax.random.normal(ks[3], (E, D, F), dtype=jnp.float32) * (1.0 / np.sqrt(D)), 'b1': jax.random.normal(ks[4], (E, F), dtype=jnp.float32) * 0.02, 'W2': jax.random.normal(ks[5], (E, F, D), dtype=jnp.float32) * (1.0 / np.sqrt(F)), 'b2': jax.random.normal(ks[6], (E, D), dtype=jnp.float32) * 0.02}
    _L0_ffn_in = _L0_ffn_setup()

    def _L1_attn_setup():
        import jax, jax.numpy as jnp
        import numpy as np
        from jax import lax
        D_MODEL = 128
        D_INNER = 2 * D_MODEL
        D_STATE = 16
        D_CONV = 4
        DT_RANK = (D_MODEL + 15) // 16
        B, L = (4, 256)
        EPS = 1e-06

        def _rmsnorm(h, w):
            var = jnp.mean(h.astype(jnp.float32) ** 2, axis=-1, keepdims=True)
            return (w * (h * lax.rsqrt(var + EPS))).astype(h.dtype)

        def _mamba(x, in_proj_w, conv_w, conv_b, x_proj_w, dt_proj_w, dt_proj_b, A_log, D_skip, out_proj_w):
            xz = jnp.einsum('bld,ed->ble', x, in_proj_w)
            u, z = jnp.split(xz, 2, axis=-1)
            u_t = jnp.transpose(u, (0, 2, 1))
            conv = lax.conv_general_dilated(u_t, conv_w[:, None, :], (1,), [(D_CONV - 1, 0)], dimension_numbers=('NCH', 'OIH', 'NCH'), feature_group_count=D_INNER)
            u = jax.nn.silu(jnp.transpose(conv + conv_b[None, :, None], (0, 2, 1)))
            dbc = jnp.einsum('bld,ed->ble', u, x_proj_w)
            dt, Bm, Cm = jnp.split(dbc, [DT_RANK, DT_RANK + D_STATE], axis=-1)
            dt = jax.nn.softplus(jnp.einsum('blr,dr->bld', dt, dt_proj_w) + dt_proj_b)
            A = -jnp.exp(A_log)

            def step(s, inp):
                d, u_i, b_i, c_i = inp
                s = s * jnp.exp(d[..., None] * A) + (d * u_i)[..., None] * b_i[:, None, :]
                y = jnp.einsum('bdn,bn->bd', s, c_i)
                return (s, y)
            s0 = jnp.zeros((u.shape[0], D_INNER, D_STATE), u.dtype)
            inputs = (jnp.moveaxis(dt, 1, 0), jnp.moveaxis(u, 1, 0), jnp.moveaxis(Bm, 1, 0), jnp.moveaxis(Cm, 1, 0))
            _, ys = lax.scan(step, s0, inputs)
            y = jnp.moveaxis(ys, 0, 1) + u * D_skip
            y = y * jax.nn.silu(z)
            return jnp.einsum('ble,de->bld', y, out_proj_w)

        def _mlp(x, fc1_w, fc1_b, fc2_w, fc2_b, fc3_w, fc3_b):
            h = jax.nn.relu(jnp.einsum('bld,hd->blh', x, fc1_w) + fc1_b)
            h = jax.nn.relu(jnp.einsum('blh,gh->blg', h, fc2_w) + fc2_b)
            return jnp.einsum('blg,dg->bld', h, fc3_w) + fc3_b
        key = jax.random.key(seed)
        ks = jax.random.split(key, 16)
        g = lambda k, shape, s=0.02: jax.random.normal(k, shape, jnp.float32) * s
        A_init = jnp.broadcast_to(jnp.arange(1, D_STATE + 1, dtype=jnp.float32), (D_INNER, D_STATE))
        return {'x': jax.random.normal(ks[0], (B, L, D_MODEL), jnp.float32), 'rms1_w': jnp.ones((D_MODEL,), jnp.float32), 'rms2_w': jnp.ones((D_MODEL,), jnp.float32), 'in_proj_w': g(ks[1], (2 * D_INNER, D_MODEL)), 'conv_w': g(ks[2], (D_INNER, D_CONV), 0.1), 'conv_b': jnp.zeros((D_INNER,), jnp.float32), 'x_proj_w': g(ks[3], (DT_RANK + 2 * D_STATE, D_INNER)), 'dt_proj_w': g(ks[4], (D_INNER, DT_RANK), 0.1), 'dt_proj_b': jnp.full((D_INNER,), -4.0, jnp.float32), 'A_log': jnp.log(A_init), 'D_skip': jnp.ones((D_INNER,), jnp.float32), 'out_proj_w': g(ks[5], (D_MODEL, D_INNER)), 'fc1_w': g(ks[6], (2 * D_MODEL, D_MODEL)), 'fc1_b': jnp.zeros((2 * D_MODEL,), jnp.float32), 'fc2_w': g(ks[7], (2 * D_MODEL, 2 * D_MODEL)), 'fc2_b': jnp.zeros((2 * D_MODEL,), jnp.float32), 'fc3_w': g(ks[8], (D_MODEL, 2 * D_MODEL)), 'fc3_b': jnp.zeros((D_MODEL,), jnp.float32)}
    _L1_attn_in = _L1_attn_setup()

    def _L1_ffn_setup():
        import jax, jax.numpy as jnp
        import numpy as np
        DIM = 128
        DEPTH = 2
        HEADS = 8
        DIM_HEAD = 64
        WINDOW = 64
        INNER = HEADS * DIM_HEAD
        HID = int(DIM * 4 * 2 / 3)
        B, N = (2, 1024)
        QK_SCALE = 8.0

        def shift_token(t):
            t1, t2 = jnp.split(t, 2, axis=-1)
            t2 = jnp.pad(t2, ((0, 0), (1, 0), (0, 0)))[:, :-1]
            return jnp.concatenate([t1, t2], axis=-1)

        def l2norm(t):
            return t / jnp.clip(jnp.linalg.norm(t, axis=-1, keepdims=True), 1e-12)

        def rotate_half(x):
            x1, x2 = jnp.split(x, 2, axis=-1)
            return jnp.concatenate([-x2, x1], axis=-1)

        def rotary_xpos(q, k):
            n = q.shape[-2]
            half_idx = jnp.arange(0, DIM_HEAD, 2, dtype=jnp.float32)
            inv_freq = 1.0 / 10000.0 ** (half_idx / DIM_HEAD)
            t = jnp.arange(n, dtype=jnp.float32)
            freqs = t[:, None] * inv_freq[None, :]
            freqs = jnp.concatenate([freqs, freqs], axis=-1)
            base = (half_idx + 0.4 * DIM_HEAD) / (1.4 * DIM_HEAD)
            power = (t - n // 2) / float(WINDOW // 2)
            scale = base[None, :] ** power[:, None]
            scale = jnp.concatenate([scale, scale], axis=-1)
            cos, sin = (jnp.cos(freqs), jnp.sin(freqs))
            q = q * cos * scale + rotate_half(q) * sin * scale
            k = k * cos / scale + rotate_half(k) * sin / scale
            return (q, k)

        def local_attention(q, k, v):
            b, h, n, d = q.shape
            w = n // WINDOW
            bq = q.reshape(b, h, w, WINDOW, d) * QK_SCALE
            bk = k.reshape(b, h, w, WINDOW, d)
            bv = v.reshape(b, h, w, WINDOW, d)

            def look_around(t):
                p = jnp.pad(t, ((0, 0), (0, 0), (1, 0), (0, 0), (0, 0)))
                return jnp.concatenate([p[:, :, :w], p[:, :, 1:]], axis=3)
            bk, bv = (look_around(bk), look_around(bv))
            bt = jnp.arange(n).reshape(w, WINDOW)
            btp = jnp.pad(bt, ((1, 0), (0, 0)), constant_values=-1)
            btk = jnp.concatenate([btp[:w], btp[1:]], axis=1)
            sim = jnp.einsum('bhwid,bhwjd->bhwij', bq, bk)
            i = bt[:, :, None]
            j = btk[:, None, :]
            mask = (i < j) | (i > j + WINDOW) | (j == -1)
            sim = jnp.where(mask, -jnp.finfo(sim.dtype).max, sim)
            attn = jax.nn.softmax(sim, axis=-1)
            out = jnp.einsum('bhwij,bhwjd->bhwid', attn, bv)
            return out.reshape(b, h, n, d)

        def _layer(x, wqkv, qs, ksc, wo, lg, lb, w1, b1, w2, b2):
            b, n, _ = x.shape
            h = shift_token(x)
            qkv = h @ wqkv
            q, k, v = jnp.split(qkv, 3, axis=-1)
            to_heads = lambda t: t.reshape(b, n, HEADS, DIM_HEAD).transpose(0, 2, 1, 3)
            q, k, v = (to_heads(q), to_heads(k), to_heads(v))
            q = l2norm(q) * qs
            k = l2norm(k) * ksc
            q, k = rotary_xpos(q, k)
            o = local_attention(q, k, v)
            o = o.transpose(0, 2, 1, 3).reshape(b, n, INNER)
            x = x + o @ wo
            h = shift_token(x)
            mu = h.mean(-1, keepdims=True)
            var = h.var(-1, keepdims=True)
            h = (h - mu) / jnp.sqrt(var + 1e-05) * lg + lb
            h = h @ w1 + b1
            a, g = jnp.split(h, 2, axis=-1)
            h = a * jax.nn.gelu(g, approximate=False)
            x = x + h @ w2 + b2
            return x
        key = jax.random.key(seed)
        ks = jax.random.split(key, 6)
        return {'x': jax.random.normal(ks[0], (B, N, DIM), jnp.float32), 'wqkv': jax.random.normal(ks[1], (DEPTH, DIM, 3 * INNER), jnp.float32) * 0.02, 'q_scale': jnp.ones((DEPTH, DIM_HEAD), jnp.float32), 'k_scale': jnp.ones((DEPTH, DIM_HEAD), jnp.float32), 'wo': jax.random.normal(ks[2], (DEPTH, INNER, DIM), jnp.float32) * 0.02, 'ln_g': jnp.ones((DEPTH, DIM), jnp.float32), 'ln_b': jnp.zeros((DEPTH, DIM), jnp.float32), 'w1': jax.random.normal(ks[3], (DEPTH, DIM, 2 * HID), jnp.float32) * 0.02, 'b1': jnp.zeros((DEPTH, 2 * HID), jnp.float32), 'w2': jax.random.normal(ks[4], (DEPTH, HID, DIM), jnp.float32) * 0.02, 'b2': jnp.zeros((DEPTH, DIM), jnp.float32)}
    _L1_ffn_in = _L1_ffn_setup()
    _d = {'L0_attn_h': _L0_attn_in['h'], 'L0_attn_W0': _L0_attn_in['W0'], 'L0_attn_W1': _L0_attn_in['W1'], 'L0_ffn_router_w': _L0_ffn_in['router_w'], 'L0_ffn_router_b': _L0_ffn_in['router_b'], 'L0_ffn_W1': _L0_ffn_in['W1'], 'L0_ffn_b1': _L0_ffn_in['b1'], 'L0_ffn_W2': _L0_ffn_in['W2'], 'L0_ffn_b2': _L0_ffn_in['b2'], 'L1_attn_rms1_w': _L1_attn_in['rms1_w'], 'L1_attn_rms2_w': _L1_attn_in['rms2_w'], 'L1_attn_in_proj_w': _L1_attn_in['in_proj_w'], 'L1_attn_conv_w': _L1_attn_in['conv_w'], 'L1_attn_conv_b': _L1_attn_in['conv_b'], 'L1_attn_x_proj_w': _L1_attn_in['x_proj_w'], 'L1_attn_dt_proj_w': _L1_attn_in['dt_proj_w'], 'L1_attn_dt_proj_b': _L1_attn_in['dt_proj_b'], 'L1_attn_A_log': _L1_attn_in['A_log'], 'L1_attn_D_skip': _L1_attn_in['D_skip'], 'L1_attn_out_proj_w': _L1_attn_in['out_proj_w'], 'L1_attn_fc1_w': _L1_attn_in['fc1_w'], 'L1_attn_fc1_b': _L1_attn_in['fc1_b'], 'L1_attn_fc2_w': _L1_attn_in['fc2_w'], 'L1_attn_fc2_b': _L1_attn_in['fc2_b'], 'L1_attn_fc3_w': _L1_attn_in['fc3_w'], 'L1_attn_fc3_b': _L1_attn_in['fc3_b'], 'L1_ffn_wqkv': _L1_ffn_in['wqkv'], 'L1_ffn_q_scale': _L1_ffn_in['q_scale'], 'L1_ffn_k_scale': _L1_ffn_in['k_scale'], 'L1_ffn_wo': _L1_ffn_in['wo'], 'L1_ffn_ln_g': _L1_ffn_in['ln_g'], 'L1_ffn_ln_b': _L1_ffn_in['ln_b'], 'L1_ffn_w1': _L1_ffn_in['w1'], 'L1_ffn_b1': _L1_ffn_in['b1'], 'L1_ffn_w2': _L1_ffn_in['w2'], 'L1_ffn_b2': _L1_ffn_in['b2']}
    _x0 = _d['L0_attn_h']
    _d['L0_attn_h'] = jax.random.normal(jax.random.fold_in(jax.random.key(seed), 1), (4, 1024, 128), dtype=_x0.dtype)
    del _x0
    return _d

def reference(L0_attn_h, L0_attn_W0, L0_attn_W1, L0_ffn_router_w, L0_ffn_router_b, L0_ffn_W1, L0_ffn_b1, L0_ffn_W2, L0_ffn_b2, L1_attn_rms1_w, L1_attn_rms2_w, L1_attn_in_proj_w, L1_attn_conv_w, L1_attn_conv_b, L1_attn_x_proj_w, L1_attn_dt_proj_w, L1_attn_dt_proj_b, L1_attn_A_log, L1_attn_D_skip, L1_attn_out_proj_w, L1_attn_fc1_w, L1_attn_fc1_b, L1_attn_fc2_w, L1_attn_fc2_b, L1_attn_fc3_w, L1_attn_fc3_b, L1_ffn_wqkv, L1_ffn_q_scale, L1_ffn_k_scale, L1_ffn_wo, L1_ffn_ln_g, L1_ffn_ln_b, L1_ffn_w1, L1_ffn_b1, L1_ffn_w2, L1_ffn_b2):

    def _L0_attn_ref(h, W0, W1):
        import jax, jax.numpy as jnp
        import numpy as np
        B, T, H, NUM_LAYERS = (8, 512, 128, 2)

        def _log_g(x):
            return jnp.where(x >= 0.0, jnp.log(jax.nn.relu(x) + 0.5), -jax.nn.softplus(-x))

        def _heinsen_scan(log_coeffs, log_values):
            a_star = jnp.cumsum(log_coeffs, axis=1)
            return jnp.exp(a_star + jax.lax.cumlogsumexp(log_values - a_star, axis=1))
        for W in (W0, W1):
            z = jnp.einsum('bth,hk->btk', h, W)
            hidden, gate, proj = jnp.split(z, 3, axis=-1)
            log_coeffs = -jax.nn.softplus(gate)
            log_values = -jax.nn.softplus(-gate) + _log_g(hidden)
            out = _heinsen_scan(log_coeffs, log_values)
            g = jax.nn.sigmoid(proj)
            h = g * out + (1.0 - g) * h
        return h

    def _L0_ffn_ref(x, router_w, router_b, W1, b1, W2, b2):
        import jax, jax.numpy as jnp
        import numpy as np
        B, L, D, F, E = (2, 128, 128, 512, 8)
        b, l, d = x.shape
        xf = x.reshape(b * l, d)
        logits = xf @ router_w + router_b
        top1 = jnp.argmax(logits, axis=-1)
        h = jax.nn.gelu(jnp.einsum('td,edf->etf', xf, W1) + b1[:, None, :], approximate=False)
        y_all = jnp.einsum('etf,efd->etd', h, W2) + b2[:, None, :]
        onehot = jax.nn.one_hot(top1, E, dtype=x.dtype)
        yf = jnp.einsum('te,etd->td', onehot, y_all)
        return yf.reshape(b, l, d)

    def _L1_attn_ref(x, rms1_w, rms2_w, in_proj_w, conv_w, conv_b, x_proj_w, dt_proj_w, dt_proj_b, A_log, D_skip, out_proj_w, fc1_w, fc1_b, fc2_w, fc2_b, fc3_w, fc3_b):
        import jax, jax.numpy as jnp
        import numpy as np
        from jax import lax
        D_MODEL = 128
        D_INNER = 2 * D_MODEL
        D_STATE = 16
        D_CONV = 4
        DT_RANK = (D_MODEL + 15) // 16
        B, L = (4, 256)
        EPS = 1e-06

        def _rmsnorm(h, w):
            var = jnp.mean(h.astype(jnp.float32) ** 2, axis=-1, keepdims=True)
            return (w * (h * lax.rsqrt(var + EPS))).astype(h.dtype)

        def _mamba(x, in_proj_w, conv_w, conv_b, x_proj_w, dt_proj_w, dt_proj_b, A_log, D_skip, out_proj_w):
            xz = jnp.einsum('bld,ed->ble', x, in_proj_w)
            u, z = jnp.split(xz, 2, axis=-1)
            u_t = jnp.transpose(u, (0, 2, 1))
            conv = lax.conv_general_dilated(u_t, conv_w[:, None, :], (1,), [(D_CONV - 1, 0)], dimension_numbers=('NCH', 'OIH', 'NCH'), feature_group_count=D_INNER)
            u = jax.nn.silu(jnp.transpose(conv + conv_b[None, :, None], (0, 2, 1)))
            dbc = jnp.einsum('bld,ed->ble', u, x_proj_w)
            dt, Bm, Cm = jnp.split(dbc, [DT_RANK, DT_RANK + D_STATE], axis=-1)
            dt = jax.nn.softplus(jnp.einsum('blr,dr->bld', dt, dt_proj_w) + dt_proj_b)
            A = -jnp.exp(A_log)

            def step(s, inp):
                d, u_i, b_i, c_i = inp
                s = s * jnp.exp(d[..., None] * A) + (d * u_i)[..., None] * b_i[:, None, :]
                y = jnp.einsum('bdn,bn->bd', s, c_i)
                return (s, y)
            s0 = jnp.zeros((u.shape[0], D_INNER, D_STATE), u.dtype)
            inputs = (jnp.moveaxis(dt, 1, 0), jnp.moveaxis(u, 1, 0), jnp.moveaxis(Bm, 1, 0), jnp.moveaxis(Cm, 1, 0))
            _, ys = lax.scan(step, s0, inputs)
            y = jnp.moveaxis(ys, 0, 1) + u * D_skip
            y = y * jax.nn.silu(z)
            return jnp.einsum('ble,de->bld', y, out_proj_w)

        def _mlp(x, fc1_w, fc1_b, fc2_w, fc2_b, fc3_w, fc3_b):
            h = jax.nn.relu(jnp.einsum('bld,hd->blh', x, fc1_w) + fc1_b)
            h = jax.nn.relu(jnp.einsum('blh,gh->blg', h, fc2_w) + fc2_b)
            return jnp.einsum('blg,dg->bld', h, fc3_w) + fc3_b
        x0 = _rmsnorm(x, rms1_w)
        x1 = _mamba(x0, in_proj_w, conv_w, conv_b, x_proj_w, dt_proj_w, dt_proj_b, A_log, D_skip, out_proj_w)
        x = x1 + x
        x2 = _rmsnorm(x, rms2_w)
        x3 = _mlp(x2, fc1_w, fc1_b, fc2_w, fc2_b, fc3_w, fc3_b)
        return x + x3

    def _L1_ffn_ref(x, wqkv, q_scale, k_scale, wo, ln_g, ln_b, w1, b1, w2, b2):
        import jax, jax.numpy as jnp
        import numpy as np
        DIM = 128
        DEPTH = 2
        HEADS = 8
        DIM_HEAD = 64
        WINDOW = 64
        INNER = HEADS * DIM_HEAD
        HID = int(DIM * 4 * 2 / 3)
        B, N = (2, 1024)
        QK_SCALE = 8.0

        def shift_token(t):
            t1, t2 = jnp.split(t, 2, axis=-1)
            t2 = jnp.pad(t2, ((0, 0), (1, 0), (0, 0)))[:, :-1]
            return jnp.concatenate([t1, t2], axis=-1)

        def l2norm(t):
            return t / jnp.clip(jnp.linalg.norm(t, axis=-1, keepdims=True), 1e-12)

        def rotate_half(x):
            x1, x2 = jnp.split(x, 2, axis=-1)
            return jnp.concatenate([-x2, x1], axis=-1)

        def rotary_xpos(q, k):
            n = q.shape[-2]
            half_idx = jnp.arange(0, DIM_HEAD, 2, dtype=jnp.float32)
            inv_freq = 1.0 / 10000.0 ** (half_idx / DIM_HEAD)
            t = jnp.arange(n, dtype=jnp.float32)
            freqs = t[:, None] * inv_freq[None, :]
            freqs = jnp.concatenate([freqs, freqs], axis=-1)
            base = (half_idx + 0.4 * DIM_HEAD) / (1.4 * DIM_HEAD)
            power = (t - n // 2) / float(WINDOW // 2)
            scale = base[None, :] ** power[:, None]
            scale = jnp.concatenate([scale, scale], axis=-1)
            cos, sin = (jnp.cos(freqs), jnp.sin(freqs))
            q = q * cos * scale + rotate_half(q) * sin * scale
            k = k * cos / scale + rotate_half(k) * sin / scale
            return (q, k)

        def local_attention(q, k, v):
            b, h, n, d = q.shape
            w = n // WINDOW
            bq = q.reshape(b, h, w, WINDOW, d) * QK_SCALE
            bk = k.reshape(b, h, w, WINDOW, d)
            bv = v.reshape(b, h, w, WINDOW, d)

            def look_around(t):
                p = jnp.pad(t, ((0, 0), (0, 0), (1, 0), (0, 0), (0, 0)))
                return jnp.concatenate([p[:, :, :w], p[:, :, 1:]], axis=3)
            bk, bv = (look_around(bk), look_around(bv))
            bt = jnp.arange(n).reshape(w, WINDOW)
            btp = jnp.pad(bt, ((1, 0), (0, 0)), constant_values=-1)
            btk = jnp.concatenate([btp[:w], btp[1:]], axis=1)
            sim = jnp.einsum('bhwid,bhwjd->bhwij', bq, bk)
            i = bt[:, :, None]
            j = btk[:, None, :]
            mask = (i < j) | (i > j + WINDOW) | (j == -1)
            sim = jnp.where(mask, -jnp.finfo(sim.dtype).max, sim)
            attn = jax.nn.softmax(sim, axis=-1)
            out = jnp.einsum('bhwij,bhwjd->bhwid', attn, bv)
            return out.reshape(b, h, n, d)

        def _layer(x, wqkv, qs, ksc, wo, lg, lb, w1, b1, w2, b2):
            b, n, _ = x.shape
            h = shift_token(x)
            qkv = h @ wqkv
            q, k, v = jnp.split(qkv, 3, axis=-1)
            to_heads = lambda t: t.reshape(b, n, HEADS, DIM_HEAD).transpose(0, 2, 1, 3)
            q, k, v = (to_heads(q), to_heads(k), to_heads(v))
            q = l2norm(q) * qs
            k = l2norm(k) * ksc
            q, k = rotary_xpos(q, k)
            o = local_attention(q, k, v)
            o = o.transpose(0, 2, 1, 3).reshape(b, n, INNER)
            x = x + o @ wo
            h = shift_token(x)
            mu = h.mean(-1, keepdims=True)
            var = h.var(-1, keepdims=True)
            h = (h - mu) / jnp.sqrt(var + 1e-05) * lg + lb
            h = h @ w1 + b1
            a, g = jnp.split(h, 2, axis=-1)
            h = a * jax.nn.gelu(g, approximate=False)
            x = x + h @ w2 + b2
            return x
        for l in range(DEPTH):
            x = _layer(x, wqkv[l], q_scale[l], k_scale[l], wo[l], ln_g[l], ln_b[l], w1[l], b1[l], w2[l], b2[l])
        return x
    x = L0_attn_h
    x = x + _L0_attn_ref(_layernorm(x, axis=-1), L0_attn_W0, L0_attn_W1)
    x = x + _L0_ffn_ref(_layernorm(x, axis=-1), L0_ffn_router_w, L0_ffn_router_b, L0_ffn_W1, L0_ffn_b1, L0_ffn_W2, L0_ffn_b2)
    x = x + _L1_attn_ref(_layernorm(x, axis=-1), L1_attn_rms1_w, L1_attn_rms2_w, L1_attn_in_proj_w, L1_attn_conv_w, L1_attn_conv_b, L1_attn_x_proj_w, L1_attn_dt_proj_w, L1_attn_dt_proj_b, L1_attn_A_log, L1_attn_D_skip, L1_attn_out_proj_w, L1_attn_fc1_w, L1_attn_fc1_b, L1_attn_fc2_w, L1_attn_fc2_b, L1_attn_fc3_w, L1_attn_fc3_b)
    x = x + _L1_ffn_ref(_layernorm(x, axis=-1), L1_ffn_wqkv, L1_ffn_q_scale, L1_ffn_k_scale, L1_ffn_wo, L1_ffn_ln_g, L1_ffn_ln_b, L1_ffn_w1, L1_ffn_b1, L1_ffn_w2, L1_ffn_b2)
    return x

_drawn_inputs = setup_inputs


def setup_inputs(seed=0):
    import zlib

    import numpy as np

    out = dict(_drawn_inputs(seed))
    spreads = {'L1_attn_rms1_w': (1.0, 0.2),
     'L1_attn_rms2_w': (1.0, 0.2),
     'L1_attn_conv_b': (0.0, 0.1),
     'L1_attn_dt_proj_b': (-4.0, 0.2),
     'L1_attn_D_skip': (1.0, 0.2),
     'L1_attn_fc1_b': (0.0, 0.1),
     'L1_attn_fc2_b': (0.0, 0.1),
     'L1_attn_fc3_b': (0.0, 0.1),
     'L1_ffn_q_scale': (1.0, 0.2),
     'L1_ffn_k_scale': (1.0, 0.2),
     'L1_ffn_ln_g': (1.0, 0.2),
     'L1_ffn_ln_b': (0.0, 0.1),
     'L1_ffn_b1': (0.0, 0.1),
     'L1_ffn_b2': (0.0, 0.1)}
    factors = {}
    for name, (base, spread) in spreads.items():
        noise = np.random.default_rng([zlib.crc32(name.encode()), seed]).standard_normal(out[name].shape)
        drawn = base * np.exp(spread * noise) if base else spread * noise
        out[name] = jnp.asarray(drawn.astype(out[name].dtype))
    for name, factor in factors.items():
        out[name] = (out[name] * factor).astype(out[name].dtype)
    return out
```

```python
from contextlib import ExitStack

import numpy as np

import concourse.bass as bass
from concourse import mybir

F32 = mybir.dt.float32
BF16 = mybir.dt.bfloat16
U32 = mybir.dt.uint32
ACT = mybir.ActivationFunctionType
ALU = mybir.AluOpType
AX_X = mybir.AxisListType.X

P = 128
SEQS = 4
T = 1024
CH = 512
CHUNKS = T // CH
ALL = SEQS * T
EPS_LN = 1e-5
EPS_RMS = 1e-6

PRIME = 2


def done(t):
    return t + 1 + PRIME


def freed(t):
    return t - 1 + PRIME


def cols(t, width=CH):
    return bass.ds(t * width, width)


def semaphores(ctx, nc, stage, names):
    made = [nc.alloc_semaphore(f"{stage}_{n}") for n in names.split()]
    ctx.callback(nc.clear_and_free_semaphores, made)
    return made


def load_constants(nc, mem, dram):
    with ExitStack() as ctx:
        (loaded,) = semaphores(ctx, nc, "init", "loaded")
        block = ctx.enter_context(nc.Block())

        @block.sync
        def _(sp):
            n = 0
            for name in ("centre", "mean", "ident"):
                sp.dma_start(mem[name][:], dram[name]).then_inc(loaded, 16)
                n += 16
            sp.dma_start(mem["x"][:], dram["x"]).then_inc(loaded, 16)
            sp.wait_ge(loaded, n + 16)


def min_gru(nc, mem, dram):
    x, centre, mean = mem["x"], mem["centre"], mem["mean"]
    with ExitStack() as ctx:
        def sb(name, shape, dt=F32):
            return ctx.enter_context(nc.sbuf_tensor(f"gru_{name}", shape, dt))

        w = sb("w", [P, 2, 3, P])
        square = sb("square", [P, 2, CH])
        log = sb("log", [P, 2, CH])
        rstd = sb("rstd", [P, 2, CH])
        h = [sb(f"h{n}", [P, 2, CH]) for n in range(3)]
        update = sb("update", [P, 2, CH])
        keep = sb("keep", [P, 2, CH])
        cand = sb("cand", [P, 2, CH])
        gate = sb("gate", [P, 2, CH])
        value = sb("value", [P, 2, CH])
        scan = sb("scan", [P, 2, 2, CH])
        mix = sb("mix", [P, 2, CH])
        bank = [ctx.enter_context(nc.psum_tensor(f"gru_bank{n}", [P, CH], F32)) for n in range(8)]
        centred, variance = bank[0:2], bank[2:4]
        (w_loaded, centred_ready, square_ready, variance_ready, log_ready, rstd_ready,
         h0_ready, x_done) = semaphores(
            ctx, nc, "gru", "w_loaded centred square variance log rstd normed x_done")
        gates_ready = semaphores(ctx, nc, "gru", "z0 z1")
        update_ready = semaphores(ctx, nc, "gru", "update0 update1")
        keep_ready = semaphores(ctx, nc, "gru", "keep0 keep1")
        cand_ready = semaphores(ctx, nc, "gru", "cand0 cand1")
        gate_ready = semaphores(ctx, nc, "gru", "gate0 gate1")
        (low_done, value_done, fed_done, scan_done, off_done, gated_done, h_done) = (
            semaphores(ctx, nc, "gru", f"{n}_0 {n}_1") for n in
            ("low", "value", "fed", "scan", "off", "gated", "h"))
        block = ctx.enter_context(nc.Block())

        @block.sync
        def _(sp):
            sp.dma_start(w[:, 0], dram["gru_w0"].rearrange("d (g n) -> d g n", g=3)).then_inc(w_loaded, 16)
            sp.dma_start(w[:, 1], dram["gru_w1"].rearrange("d (g n) -> d g n", g=3)).then_inc(w_loaded, 16)
            sp.wait_ge(w_loaded, 32)

        @block.tensor
        def _(pe):
            for s in [centred_ready, variance_ready] + gates_ready:
                pe.sem_inc(s, PRIME)
            pe.wait_ge(w_loaded, 32)
            with pe.Fori(0, SEQS) as b:
                for k in range(2):
                    t = b * 2 + k
                    pe.wait_ge(keep_ready[1], freed(t))
                    pe.wait_ge(h0_ready, freed(t))
                    nc.tensor.matmul(centred[k][:], centre[:], x[:, cols(t)], start=True, stop=True
                                     ).then_inc(centred_ready, 1)
                for k in range(2):
                    t = b * 2 + k
                    pe.wait_ge(square_ready, done(t))
                    pe.wait_ge(keep_ready[0], freed(t))
                    nc.tensor.matmul(variance[k][:], mean[:], square[:, k], start=True, stop=True
                                     ).then_inc(variance_ready, 1)
                for layer in range(2):
                    for k in range(2):
                        t = b * 2 + k
                        if layer == 0:
                            pe.wait_ge(h0_ready, done(t))
                            pe.wait_ge(fed_done[1], freed(t))
                            pe.wait_ge(gate_ready[1], freed(t))
                        else:
                            pe.wait_ge(h_done[0], done(t))
                            pe.wait_ge(fed_done[0], done(t))
                            pe.wait_ge(gate_ready[0], done(t))
                        for g, out in ((0, bank[4 + k]), (1, bank[6 + k]),
                                       (2, bank[2 + k] if layer == 0 else bank[k])):
                            last = nc.tensor.matmul(out[:], w[:, layer, g], h[layer][:, k],
                                                    start=True, stop=True)
                        last.then_inc(gates_ready[layer], 1)

        @block.scalar
        def _(act):
            for s in [square_ready, log_ready, rstd_ready] + update_ready + keep_ready + cand_ready + gate_ready:
                act.sem_inc(s, PRIME)
            with act.Fori(0, SEQS) as b:
                for k in range(2):
                    t = b * 2 + k
                    act.wait_ge(centred_ready, done(t))
                    nc.scalar.activation(square[:, k], centred[k][:], ACT.Square).then_inc(square_ready, 1)
                for k in range(2):
                    t = b * 2 + k
                    act.wait_ge(variance_ready, done(t))
                    nc.scalar.activation(log[:, k], variance[k][:], ACT.Ln, bias=EPS_LN).then_inc(log_ready, 1)
                for k in range(2):
                    t = b * 2 + k
                    act.wait_ge(log_ready, done(t))
                    act.wait_ge(h0_ready, freed(t))
                    nc.scalar.activation(rstd[:, k], log[:, k], ACT.Exp, scale=-0.5).then_inc(rstd_ready, 1)
                for layer in range(2):
                    for k in range(2):
                        t = b * 2 + k
                        act.wait_ge(gates_ready[layer], done(t))
                        if layer == 0:
                            act.wait_ge(h_done[1], freed(t))
                        else:
                            act.wait_ge(h_done[0], done(t))
                        nc.scalar.activation(cand[:, k], bank[4 + k][:], ACT.Sigmoid).then_inc(cand_ready[layer], 1)
                        nc.scalar.activation(update[:, k], bank[6 + k][:], ACT.Sigmoid).then_inc(update_ready[layer], 1)
                        nc.scalar.activation(gate[:, k], bank[6 + k][:], ACT.Sigmoid, scale=-1.0
                                             ).then_inc(gate_ready[layer], 1)
                        nc.scalar.activation(keep[:, k], (bank[2 + k] if layer == 0 else bank[k])[:], ACT.Sigmoid
                                             ).then_inc(keep_ready[layer], 1)

        @block.vector
        def _(dve):
            for s in ([h0_ready, x_done] + low_done + value_done + fed_done + scan_done + off_done
                      + gated_done + h_done):
                dve.sem_inc(s, PRIME)
            with dve.Fori(0, SEQS) as b:
                for k in range(2):
                    t = b * 2 + k
                    dve.wait_ge(rstd_ready, done(t))
                    dve.wait_ge(h_done[0], freed(t))
                    nc.vector.tensor_tensor(h[0][:, k], centred[k][:], rstd[:, k], ALU.mult).then_inc(h0_ready, 1)
                for layer in range(2):
                    for k in range(2):
                        t = b * 2 + k
                        hidden = bank[4 + k]
                        dve.wait_ge(cand_ready[layer], done(t))
                        nc.vector.tensor_scalar(cand[:, k], cand[:, k], 0.5, None, ALU.min
                                                ).then_inc(low_done[layer], 1)
                        dve.wait_ge(low_done[layer], done(t))
                        nc.vector.scalar_tensor_tensor(value[:, k], hidden[:], 0.0, cand[:, k],
                                                       ALU.max, ALU.add).then_inc(fed_done[layer], 1)
                        dve.wait_ge(fed_done[layer], done(t))
                        dve.wait_ge(update_ready[layer], done(t))
                        nc.vector.tensor_tensor(value[:, k], value[:, k], update[:, k], ALU.mult
                                                ).then_inc(value_done[layer], 1)
                        dve.wait_ge(value_done[layer], done(t))
                        dve.wait_ge(gate_ready[layer], done(t))
                        start = 0.0 if k == 0 else scan[:, layer, 0, CH - 1:CH]
                        if k == 1:
                            dve.wait_ge(scan_done[layer], done(t - 1))
                        nc.vector.tensor_tensor_scan(scan[:, layer, k], gate[:, k], value[:, k], start,
                                                     ALU.mult, ALU.add).then_inc(scan_done[layer], 1)
                        dve.wait_ge(scan_done[layer], done(t))
                        nc.vector.tensor_tensor(mix[:, k], scan[:, layer, k], h[layer][:, k], ALU.subtract
                                                ).then_inc(off_done[layer], 1)
                        dve.wait_ge(off_done[layer], done(t))
                        dve.wait_ge(keep_ready[layer], done(t))
                        nc.vector.tensor_tensor(mix[:, k], mix[:, k], keep[:, k], ALU.mult
                                                ).then_inc(gated_done[layer], 1)
                        dve.wait_ge(gated_done[layer], done(t))
                        nc.vector.tensor_tensor(h[layer + 1][:, k], mix[:, k], h[layer][:, k], ALU.add
                                                ).then_inc(h_done[layer], 1)
                for k in range(2):
                    t = b * 2 + k
                    dve.wait_ge(h_done[1], done(t))
                    nc.vector.tensor_tensor(x[:, cols(t)], x[:, cols(t)], h[2][:, k], ALU.add
                                            ).then_inc(x_done, 1)


MOE = ("weights_ready experts_ready cleared_tile cleared centred square variance log rstd normed logits biased best "
       "same preferred first chosen turned rows "
       "ranked totals totals_copied running ahead further blocks ends base based slot own_slot slots expert_no clipped "
       "block_expert scattered loaded0 loaded1 columns_turned columns picked up act down out stored0 stored1 "
       "back added")
E = 8
PARTS = 4
TOKEN_TILES = ALL // P
GROUP = 4
PAIRS = -(-(TOKEN_TILES + E - 1) // (2 * GROUP))
BLOCKS = PAIRS * 2 * GROUP


def experts(nc, mem, dram):
    x, centre, mean, ident = mem["x"], mem["centre"], mem["mean"], mem["ident"]
    with ExitStack() as ctx:
        def sb(name, shape, dt=F32):
            return ctx.enter_context(nc.sbuf_tensor(f"moe_{name}", shape, dt))

        router = sb("router", [P, E])
        router_b = sb("router_b", [P, E])
        order = sb("order", [P, E])
        before = sb("before", [P, P])
        index = sb("index", [P, BLOCKS])
        going = sb("going", [P, E * TOKEN_TILES])
        w1 = sb("w1", [P, E, PARTS * P])
        w2 = sb("w2", [P, E, PARTS * P])
        b1 = sb("b1", [P, E, PARTS])
        b2 = sb("b2", [1, E, P])
        zeros = sb("zeros", [P, GROUP * P])
        ones = sb("ones", [1, P])
        square = sb("square", [P, 2, CH])
        log = sb("log", [P, 2, CH])
        rstd = sb("rstd", [P, 2, CH])
        normed = sb("normed", [P, 2, CH])
        logits = sb("logits", [P, 2, 4, E])
        best = sb("best", [P, 2, 4])
        chosen = sb("chosen", [P, TOKEN_TILES, E])
        rows = sb("rows", [P, TOKEN_TILES, P])
        total = sb("total", [P, E, TOKEN_TILES])
        running = sb("running", [P, E, TOKEN_TILES])
        ahead = sb("ahead", [P, E, TOKEN_TILES])
        further = sb("further", [P, E, TOKEN_TILES])
        blocks = sb("blocks", [P, E])
        ends = sb("ends", [P, E])
        base = sb("base", [P, E])
        own_slot = sb("own_slot", [P, TOKEN_TILES])
        slots = sb("slots", [P, TOKEN_TILES], U32)
        passed = sb("passed", [1, BLOCKS, E])
        expert_no = sb("expert_no", [1, BLOCKS])
        block_expert = sb("block_expert", [1, BLOCKS], U32)
        slot_rows = sb("slot_rows", [P, 2, GROUP, P])
        columns = sb("columns", [P, 2, GROUP * P])
        w1_now = sb("w1_now", [P, 4, PARTS * P])
        w2_now = sb("w2_now", [P, 4, PARTS * P])
        b1_now = sb("b1_now", [P, 4, PARTS])
        b2_now = sb("b2_now", [1, 4, P])
        hidden = sb("hidden", [P, 2, PARTS, P])
        out_rows = sb("out_rows", [P, 2, GROUP, P])
        to_experts = nc.dram_tensor("moe_to_experts", (BLOCKS * P, P), F32, kind="Internal").ap()
        from_experts = nc.dram_tensor("moe_from_experts", (BLOCKS * P, P), F32, kind="Internal").ap()
        bank = [ctx.enter_context(nc.psum_tensor(f"moe_bank{n}", [P, CH], F32)) for n in range(8)]
        s = dict(zip(MOE.split(), semaphores(ctx, nc, "moe", MOE)))
        loaded, stored = (s["loaded0"], s["loaded1"]), (s["stored0"], s["stored1"])
        weights, expert_weights = semaphores(ctx, nc, "moe", "weights expert_weights")
        returned = semaphores(ctx, nc, "moe", " ".join(f"returned{n}" for n in range(2 * SEQS)))
        block = ctx.enter_context(nc.Block())

        def group_of(scratch, n):
            return scratch[n * GROUP * P:(n + 1) * GROUP * P].rearrange("(j p) d -> p j d", p=P)

        @block.sync
        def _(sp):
            first = [(router[:], dram["router_w"]), (router_b[:], dram["router_b"].partition_broadcast(P)),
                     (order[:], dram["order"].partition_broadcast(P)), (before[:], dram["before"]),
                     (index[:], dram["index"].partition_broadcast(P)),
                     (going[:], dram["going"].partition_broadcast(P))]
            for to, of in first:
                sp.dma_start(to, of).then_inc(weights, 16)
            sp.wait_ge(weights, 16 * len(first))
            sp.sem_inc(s["weights_ready"], 1)
            sp.wait_ge(s["cleared_tile"], 1)
            for n in range(2 * PAIRS):
                sp.dma_start(group_of(to_experts, n), zeros[:].rearrange("p (j d) -> p j d", j=GROUP)
                             ).then_inc(s["cleared"], 16)
            second = [(b1[:], dram["moe_b1"]), (b2[:], dram["moe_b2"])]
            for e in range(E):
                second += [(w1[:, e], dram["moe_w1"][e]),
                           (w2[:, e].rearrange("p (c n) -> p c n", n=P),
                            dram["moe_w2"][e].rearrange("(c p) n -> p c n", p=P))]
            for to, of in second:
                sp.dma_start(to, of).then_inc(expert_weights, 16)
            sp.wait_ge(expert_weights, 16 * len(second))
            sp.sem_inc(s["experts_ready"], 1)
            sp.wait_ge(s["scattered"], 16 * TOKEN_TILES)
            for n in range(2 * PAIRS + 2):
                if n < 2 * PAIRS:
                    if n >= 2:
                        sp.wait_ge(s["columns_turned"], n - 1 + PRIME)
                    sp.dma_start(slot_rows[:, n % 2], group_of(to_experts, n)).then_inc(loaded[n % 2], 16)
                if n >= 2:
                    sp.wait_ge(s["out"], n - 1 + PRIME)
                    sp.dma_start(group_of(from_experts, n - 2), out_rows[:, n % 2]).then_inc(stored[n % 2], 16)
            for n in range(2):
                sp.wait_ge(stored[n], 16 * (1 + PAIRS))

        @block.tensor
        def _(pe):
            for name in "centred variance logits turned columns_turned up down".split():
                pe.sem_inc(s[name], PRIME)
            pe.wait_ge(s["weights_ready"], 1)
            with pe.Fori(0, SEQS) as b:
                for k in range(2):
                    t = b * 2 + k
                    pe.wait_ge(s["normed"], freed(t))
                    nc.tensor.matmul(bank[k][:], centre[:], x[:, cols(t)], start=True, stop=True
                                     ).then_inc(s["centred"], 1)
                for k in range(2):
                    t = b * 2 + k
                    pe.wait_ge(s["square"], done(t))
                    nc.tensor.matmul(bank[2 + k][:], mean[:], square[:, k], start=True, stop=True
                                     ).then_inc(s["variance"], 1)
                for k in range(2):
                    t = b * 2 + k
                    pe.wait_ge(s["normed"], done(t))
                    pe.wait_ge(s["biased"], freed(t))
                    for j in range(4):
                        last = nc.tensor.matmul(bank[4 + k][:, j * E:(j + 1) * E], normed[:, k, j * P:(j + 1) * P],
                                                router[:], start=True, stop=True)
                    last.then_inc(s["logits"], 1)
                    pe.wait_ge(s["rows"], freed(t))
                    for j in range(4):
                        last = nc.tensor.transpose(bank[6 + k][:, j * P:(j + 1) * P],
                                                   normed[:, k, j * P:(j + 1) * P], ident[:])
                    last.then_inc(s["turned"], 1)
            pe.wait_ge(s["chosen"], done(2 * SEQS - 1))
            everyone = chosen[:].rearrange("p t e -> p (t e)")
            nc.tensor.matmul(bank[0][:, 0:TOKEN_TILES * E], before[:], everyone, start=True, stop=True
                             ).then_inc(s["ranked"], 1)
            nc.tensor.matmul(bank[1][:, 0:TOKEN_TILES * E], mean[:], everyone, start=True, stop=True
                             ).then_inc(s["totals"], 1)
            pe.wait_ge(s["slots"], 1)
            with pe.Fori(0, PAIRS) as b:
                for g in range(2):
                    n = b * 2 + g
                    pe.wait_ge(loaded[g], b * 16 + 16)
                    pe.wait_ge(s["columns"], freed(n))
                    for j in range(GROUP):
                        last = nc.tensor.transpose(bank[g][:, j * P:(j + 1) * P], slot_rows[:, g, j], ident[:])
                    last.then_inc(s["columns_turned"], 1)
                for m in range(2 * GROUP + 1):
                    if m < 2 * GROUP:
                        i = b * 2 * GROUP + m
                        g, j = divmod(m, GROUP)
                        if j == 0:
                            pe.wait_ge(s["columns"], done(b * 2 + g))
                        pe.wait_ge(s["picked"], done(i))
                        pe.wait_ge(s["act"], freed(i))
                        for c in range(PARTS):
                            last = nc.tensor.matmul(bank[2 + m % 2][:, c * P:(c + 1) * P],
                                                    w1_now[:, m % 4, c * P:(c + 1) * P],
                                                    columns[:, g, j * P:(j + 1) * P], start=True, stop=True)
                        last.then_inc(s["up"], 1)
                    if m >= 1:
                        i = b * 2 * GROUP + m - 1
                        g, j = divmod(m - 1, GROUP)
                        if j == 0:
                            pe.wait_ge(s["out"], freed(b * 2 + g))
                        pe.wait_ge(s["act"], done(i))
                        to = bank[4 + g][:, j * P:(j + 1) * P]
                        for c in range(PARTS):
                            nc.tensor.matmul(to, hidden[:, (m - 1) % 2, c], w2_now[:, (m - 1) % 4, c * P:(c + 1) * P],
                                             start=c == 0, stop=False)
                        nc.tensor.matmul(to, ones[:], b2_now[:, (m - 1) % 4], start=False, stop=True
                                         ).then_inc(s["down"], 1)
            for t in range(2 * SEQS):
                pe.wait_ge(returned[t], 16 * 4)
                if t >= 2:
                    pe.wait_ge(s["added"], t - 1)
                for j in range(4):
                    last = nc.tensor.transpose(bank[6 + t % 2][:, j * P:(j + 1) * P], rows[:, 4 * t + j], ident[:])
                last.then_inc(s["back"], 1)

        @block.scalar
        def _(act):
            for name in "square log rstd columns act out".split():
                act.sem_inc(s[name], PRIME)
            for n in range(2):
                act.sem_inc(stored[n], 16)
            act.preload_act_table_set("natural_log_exp_and_others")
            with act.Fori(0, SEQS) as b:
                for k in range(2):
                    t = b * 2 + k
                    act.wait_ge(s["centred"], done(t))
                    nc.scalar.activation(square[:, k], bank[k][:], ACT.Square).then_inc(s["square"], 1)
                for k in range(2):
                    t = b * 2 + k
                    act.wait_ge(s["variance"], done(t))
                    nc.scalar.activation(log[:, k], bank[2 + k][:], ACT.Ln, bias=EPS_LN).then_inc(s["log"], 1)
                for k in range(2):
                    t = b * 2 + k
                    act.wait_ge(s["log"], done(t))
                    act.wait_ge(s["normed"], freed(t))
                    nc.scalar.activation(rstd[:, k], log[:, k], ACT.Exp, scale=-0.5).then_inc(s["rstd"], 1)
            act.preload_act_table_set("gelu_and_others")
            with act.Fori(0, PAIRS) as b:
                def result(g):
                    act.wait_ge(s["down"], done(b * 2 * GROUP + g * GROUP + GROUP - 1))
                    act.wait_ge(stored[g], b * 16 + 16)
                    nc.scalar.activation(out_rows[:, g], bank[4 + g][:].rearrange("p (j d) -> p j d", j=GROUP),
                                         ACT.Copy).then_inc(s["out"], 1)

                for g in range(2):
                    act.wait_ge(s["columns_turned"], done(b * 2 + g))
                    nc.scalar.activation(columns[:, g], bank[g][:], ACT.Copy).then_inc(s["columns"], 1)
                for m in range(2 * GROUP):
                    i = b * 2 * GROUP + m
                    act.wait_ge(s["up"], done(i))
                    act.wait_ge(s["down"], freed(i))
                    for c in range(PARTS):
                        last = nc.scalar.activation(hidden[:, m % 2, c], bank[2 + m % 2][:, c * P:(c + 1) * P],
                                                    ACT.Gelu, bias=b1_now[:, m % 4, c:c + 1])
                    last.then_inc(s["act"], 1)
                    if m == GROUP + 1:
                        result(0)
                result(1)

        @block.gpsimd
        def _(pool):
            pool.wait_ge(s["slots"], 1)
            pool.wait_ge(s["cleared"], 16 * 2 * PAIRS)
            pool.wait_ge(s["rows"], done(2 * SEQS - 1))
            for n in range(TOKEN_TILES):
                nc.gpsimd.indirect_dma_start(to_experts, bass.IndirectOffsetOnAxis(slots[:, n:n + 1], 0),
                                             rows[:, n], None).then_inc(s["scattered"], 16)
            pool.wait_ge(s["scattered"], 16 * TOKEN_TILES)
            for n in range(2):
                pool.wait_ge(stored[n], 16 * (1 + PAIRS))
            for n in range(TOKEN_TILES):
                nc.gpsimd.indirect_dma_start(rows[:, n], None, from_experts,
                                             bass.IndirectOffsetOnAxis(slots[:, n:n + 1], 0)
                                             ).then_inc(returned[n // 4], 16)

        @block.vector
        def _(dve):
            for name in "normed biased best same preferred first chosen rows picked".split():
                dve.sem_inc(s[name], PRIME)
            nc.vector.memset(ones[:], 1.0)
            nc.vector.memset(zeros[:], 0.0).then_inc(s["cleared_tile"], 1)
            dve.wait_ge(s["weights_ready"], 1)
            with dve.Fori(0, SEQS) as b:
                for k in range(2):
                    t = b * 2 + k
                    dve.wait_ge(s["rstd"], done(t))
                    dve.wait_ge(s["turned"], freed(t))
                    nc.vector.tensor_tensor(normed[:, k], bank[k][:], rstd[:, k], ALU.mult).then_inc(s["normed"], 1)
                for k in range(2):
                    t = b * 2 + k
                    dve.wait_ge(s["logits"], done(t))
                    nc.vector.tensor_tensor(logits[:, k], bank[4 + k][:, 0:4 * E].rearrange("p (j e) -> p j e", e=E),
                                            router_b[:].unsqueeze(1).broadcast_to([P, 4, E]), ALU.add
                                            ).then_inc(s["biased"], 1)
                for k in range(2):
                    t = b * 2 + k
                    dve.wait_ge(s["biased"], done(t))
                    nc.vector.tensor_reduce(best[:, k], logits[:, k], AX_X, ALU.max).then_inc(s["best"], 1)
                for k in range(2):
                    t = b * 2 + k
                    dve.wait_ge(s["best"], done(t))
                    nc.vector.tensor_tensor(logits[:, k], logits[:, k], best[:, k].unsqueeze(2).broadcast_to([P, 4, E]),
                                            ALU.is_equal).then_inc(s["same"], 1)
                for k in range(2):
                    t = b * 2 + k
                    dve.wait_ge(s["same"], done(t))
                    nc.vector.tensor_tensor(logits[:, k], logits[:, k],
                                            order[:].unsqueeze(1).broadcast_to([P, 4, E]), ALU.mult
                                            ).then_inc(s["preferred"], 1)
                for k in range(2):
                    t = b * 2 + k
                    dve.wait_ge(s["preferred"], done(t))
                    nc.vector.tensor_reduce(best[:, k], logits[:, k], AX_X, ALU.max).then_inc(s["first"], 1)
                for k in range(2):
                    t = b * 2 + k
                    dve.wait_ge(s["first"], done(t))
                    nc.vector.tensor_tensor(chosen[:, bass.ds(t * 4, 4)], logits[:, k],
                                            best[:, k].unsqueeze(2).broadcast_to([P, 4, E]), ALU.is_equal
                                            ).then_inc(s["chosen"], 1)
                for k in range(2):
                    t = b * 2 + k
                    dve.wait_ge(s["turned"], done(t))
                    nc.vector.tensor_scalar(rows[:, bass.ds(t * 4, 4)],
                                            bank[6 + k][:].rearrange("p (j d) -> p j d", j=4), 1.0, None, ALU.mult
                                            ).then_inc(s["rows"], 1)

            def by_expert(ap):
                return ap.rearrange("p (t e) -> p e t", e=E)

            def flat(ap):
                return ap[:].rearrange("p e t -> p (e t)")

            dve.wait_ge(s["totals"], 1)
            nc.vector.tensor_copy(total[:], by_expert(bank[1][:, 0:TOKEN_TILES * E])).then_inc(s["totals_copied"], 1)
            dve.wait_ge(s["totals_copied"], 1)
            nc.vector.tensor_tensor_scan(flat(running), going[:], flat(total), 0.0, ALU.mult, ALU.add
                                         ).then_inc(s["running"], 1)
            dve.wait_ge(s["running"], 1)
            nc.vector.tensor_tensor(ahead[:], running[:], total[:], ALU.subtract).then_inc(s["ahead"], 1)
            nc.vector.tensor_tensor(further[:], running[:, :, TOKEN_TILES - 1:].broadcast_to([P, E, TOKEN_TILES]),
                                    index[:, 0:TOKEN_TILES].unsqueeze(1).broadcast_to([P, E, TOKEN_TILES]), ALU.is_gt
                                    ).then_inc(s["further"], 1)
            dve.wait_ge(s["further"], 1)
            nc.vector.tensor_reduce(blocks[:], further[:], AX_X, ALU.add).then_inc(s["blocks"], 1)
            dve.wait_ge(s["blocks"], 1)
            nc.vector.tensor_tensor_scan(ends[:], going[:, 1:1 + E], blocks[:], 0.0, ALU.mult, ALU.add
                                         ).then_inc(s["ends"], 1)
            dve.wait_ge(s["ends"], 1)
            nc.vector.tensor_tensor(base[:], ends[:], blocks[:], ALU.subtract).then_inc(s["base"], 1)
            dve.wait_ge(s["base"], 1)
            dve.wait_ge(s["ahead"], 1)
            nc.vector.tensor_tensor(ahead[:], ahead[:], base[:].unsqueeze(2).broadcast_to([P, E, TOKEN_TILES]),
                                    ALU.add).then_inc(s["based"], 1)
            dve.wait_ge(s["based"], 1)
            dve.wait_ge(s["ranked"], 1)
            nc.vector.scalar_tensor_tensor(ahead[:], ahead[:], float(P), by_expert(bank[0][:, 0:TOKEN_TILES * E]),
                                           ALU.mult, ALU.add).then_inc(s["slot"], 1)
            dve.wait_ge(s["slot"], 1)
            nc.vector.tensor_tensor(ahead[:], ahead[:], chosen[:].rearrange("p t e -> p e t"), ALU.mult
                                    ).then_inc(s["slot"], 1)
            dve.wait_ge(s["slot"], 2)
            nc.vector.tensor_reduce(own_slot[:], ahead[:].rearrange("p e t -> p t e"), AX_X, ALU.add
                                    ).then_inc(s["own_slot"], 1)
            dve.wait_ge(s["own_slot"], 1)
            nc.vector.tensor_copy(slots[:], own_slot[:]).then_inc(s["slots"], 1)
            nc.vector.tensor_tensor(passed[:], index[0:1].unsqueeze(2).broadcast_to([1, BLOCKS, E]),
                                    ends[0:1].unsqueeze(1).broadcast_to([1, BLOCKS, E]), ALU.is_ge
                                    ).then_inc(s["expert_no"], 1)
            dve.wait_ge(s["expert_no"], 1)
            nc.vector.tensor_reduce(expert_no[:], passed[:], AX_X, ALU.add).then_inc(s["expert_no"], 1)
            dve.wait_ge(s["expert_no"], 2)
            nc.vector.tensor_scalar(expert_no[:], expert_no[:], float(E - 1), None, ALU.min
                                    ).then_inc(s["clipped"], 1)
            dve.wait_ge(s["clipped"], 1)
            nc.vector.tensor_copy(block_expert[:], expert_no[:]).then_inc(s["block_expert"], 1)
            dve.wait_ge(s["block_expert"], 1)
            dve.wait_ge(s["experts_ready"], 1)
            with dve.Fori(0, PAIRS) as b:
                for m in range(2 * GROUP):
                    i = b * 2 * GROUP + m
                    half = m % 4
                    dve.wait_ge(s["up"], freed(i))
                    e = dve.value_load(block_expert[0:1, bass.ds(i, 1)], min_val=0, max_val=E - 1)
                    nc.vector.tensor_copy(w1_now[:, half], w1[:, bass.ds(e, 1)])
                    nc.vector.tensor_copy(b1_now[:, half], b1[:, bass.ds(e, 1)])
                    nc.vector.tensor_copy(b2_now[:, half], b2[:, bass.ds(e, 1)])
                    nc.vector.tensor_copy(w2_now[:, half], w2[:, bass.ds(e, 1)]).then_inc(s["picked"], 1)
            for t in range(2 * SEQS):
                dve.wait_ge(s["back"], t + 1)
                nc.vector.tensor_tensor(x[:, t * CH:(t + 1) * CH], x[:, t * CH:(t + 1) * CH], bank[6 + t % 2][:],
                                        ALU.add).then_inc(s["added"], 1)


SSM = ("weights_ready folded zeroed decay decay_ready centred square variance log rstd x0 uz raw tap z conv0 conv1 "
       "conv u dbc dt_low hi rest1 mid rest2 parts dtraw size small over dtlog dt dtu b c b_all da dbu "
       "state carried seen y summed gated out branch")


def mamba(nc, mem, dram):
    x, centre, mean, ident = mem["x"], mem["centre"], mem["mean"], mem["ident"]
    branch = mem["branch"]
    STATES = 16
    STEPS = 2 * STATES
    with ExitStack() as ctx:
        def sb(name, shape, dt=F32):
            return ctx.enter_context(nc.sbuf_tensor(f"ssm_{name}", shape, dt))

        in_w = sb("in_w", [P, 4 * P])
        dbc_w = sb("dbc_w", [P, 2, P])
        dt_w = sb("dt_w", [40, 2 * P])
        out_w = sb("out_w", [P, 2, P])
        pick = sb("pick", [P, 2 * STATES, P], BF16)
        rms_w = sb("rms_w", [P, 1])
        conv_w = sb("conv_w", [P, 2, 4])
        conv_b = sb("conv_b", [P, 2])
        dt_b = sb("dt_b", [P, 2])
        skip = sb("skip", [P, 2])
        a_log = sb("a_log", [P, 2, STATES])
        decay = sb("decay", [P, 2, STATES])
        u = sb("u", [P, 2, ALL])
        z = sb("z", [P, 2, ALL])
        dt = sb("dt", [P, 2, ALL])
        parts = sb("parts", [P, ALL], BF16)
        x0 = dt[:, 0]
        dtu = sb("dtu", [P, 2, 2, CH])
        b_all = sb("b_all", [P, 2, CH])
        da = sb("da", [P, 2, 2, CH])
        dbu = sb("dbu", [P, 2, 2, CH])
        state = sb("state", [P, 2, 2, CH])
        carry = sb("carry", [P, STATES, 2])
        shared = sb("shared", [P, 2, 4 * CH])
        seen = shared[:, 0].rearrange("p (a h c) -> p a h c", a=2, h=2)
        y = shared[:, 1].rearrange("p (a h c) -> p a h c", a=2, h=2)
        square = b_all
        log = da
        rstd = dbu
        raw = shared[:, :, 0:3 + T]
        conv = state
        dt_low = b_all[32:64]
        rest = dtu[:, 0]
        size = seen
        bank = [ctx.enter_context(nc.psum_tensor(f"ssm_bank{n}", [P, CH], F32)) for n in range(8)]
        s = dict(zip(SSM.split(), semaphores(ctx, nc, "ssm", SSM)))
        weights = semaphores(ctx, nc, "ssm", "weights")[0]
        block = ctx.enter_context(nc.Block())

        @block.sync
        def _(sp):
            loads = [(in_w[:], "in_w"), (dbc_w[:], "dbc_w"), (dt_w[32:40], "dt_w"), (out_w[:], "out_w"),
                     (pick[:], "pick"), (rms_w[:], "rms1"), (conv_w[:], "conv_w"), (conv_b[:], "conv_b"),
                     (dt_b[:], "dt_b"), (skip[:], "skip"), (a_log[:], "a_log")]
            for to, name in loads:
                sp.dma_start(to, dram[name]).then_inc(weights, 16)
            sp.wait_ge(weights, 16 * len(loads))
            sp.sem_inc(s["weights_ready"], 1)

        @block.tensor
        def _(pe):
            for name in "centred variance uz dbc dtraw b c y out".split():
                pe.sem_inc(s[name], PRIME)
            with pe.Fori(0, SEQS) as b:
                for k in range(2):
                    t = b * 2 + k
                    pe.wait_ge(s["x0"], freed(t))
                    nc.tensor.matmul(bank[k][:], centre[:], x[:, cols(t)], start=True, stop=True
                                     ).then_inc(s["centred"], 1)
                for k in range(2):
                    t = b * 2 + k
                    pe.wait_ge(s["square"], done(t))
                    nc.tensor.matmul(bank[2 + k][:], mean[:], square[:, k], start=True, stop=True
                                     ).then_inc(s["variance"], 1)
            pe.wait_ge(s["folded"], 1)
            pe.wait_ge(s["x0"], done(2 * SEQS - 1))
            with pe.Fori(0, SEQS) as b:
                for k in range(2):
                    t = b * 2 + k
                    pe.wait_ge(s["z"], freed(t))
                    for m in range(4):
                        last = nc.tensor.matmul(bank[4 * k + m][:], in_w[:, m * P:(m + 1) * P], x0[:, cols(t)],
                                                start=True, stop=True)
                    last.then_inc(s["uz"], 1)
            pe.wait_ge(s["z"], done(2 * SEQS - 1))
            pe.wait_ge(s["u"], done(2 * SEQS - 1))
            with pe.Fori(0, SEQS) as b:
                for k in range(2):
                    t = b * 2 + k
                    pe.wait_ge(s["rest1"], freed(t))
                    for half in range(2):
                        last = nc.tensor.matmul(bank[k][:], dbc_w[:, half], u[:, half, cols(t)],
                                                start=half == 0, stop=half == 1)
                    last.then_inc(s["dbc"], 1)
                for k in range(2):
                    t = b * 2 + k
                    pe.wait_ge(s["dt_low"], done(t))
                    pe.wait_ge(s["dt"], freed(t))
                    for half in range(2):
                        last = nc.tensor.matmul(bank[2 + 2 * k + half][:], dt_w[32:40, half * P:(half + 1) * P],
                                                dt_low[:, k][0:8], start=True, stop=True)
                    last.then_inc(s["dtraw"], 1)
            pe.wait_ge(s["parts"], done(2 * SEQS - 1))
            pe.wait_ge(s["dt"], done(2 * SEQS - 1))
            with pe.Fori(0, SEQS) as b:
                for m in range(STEPS + 3):
                    if m < STEPS:
                        i = b * STEPS + m
                        pe.wait_ge(s["b_all"], freed(i))
                        nc.tensor.matmul(bank[m % 2][:], pick[:, m % STATES], parts[:, cols(b * 2 + m // STATES)],
                                         start=True, stop=True).then_inc(s["b"], 1)
                    if 1 <= m <= STEPS:
                        i = b * STEPS + m - 1
                        pe.wait_ge(s["seen"], freed(i))
                        nc.tensor.matmul(bank[2 + (m - 1) % 2][:], pick[:, STATES + (m - 1) % STATES],
                                         parts[:, cols(b * 2 + (m - 1) // STATES)],
                                         start=True, stop=True).then_inc(s["c"], 1)
                    if m >= 3:
                        k, n = divmod(m - 3, STATES)
                        pe.wait_ge(s["seen"], done(b * STEPS + m - 3))
                        if n == 0:
                            pe.wait_ge(s["branch"], freed(b * 2 + k))
                        for half in range(2):
                            last = nc.tensor.matmul(bank[4 + 2 * k + half][:], ident[:], seen[:, n % 2, half],
                                                    start=n == 0, stop=n == STATES - 1)
                        last.then_inc(s["y"], 1)
                    for k in range(2):
                        if m == (STATES + 6 if k == 0 else STEPS + 2):
                            pe.wait_ge(s["gated"], done(b * 2 + k))
                            for half in range(2):
                                last = nc.tensor.matmul(bank[4 + 2 * k][:], out_w[:, half], y[:, k, half],
                                                        start=half == 0, stop=half == 1)
                            last.then_inc(s["out"], 1)

        @block.scalar
        def _(act):
            for name in "square log rstd raw tap z u dt_low hi size small dtlog b_all da".split():
                act.sem_inc(s[name], PRIME)
            act.preload_act_table_set("natural_log_exp_and_others")
            act.wait_ge(s["weights_ready"], 1)
            nc.scalar.activation(decay[:], a_log[:], ACT.Exp).then_inc(s["decay"], 1)
            with act.Fori(0, SEQS) as b:
                for k in range(2):
                    t = b * 2 + k
                    act.wait_ge(s["centred"], done(t))
                    nc.scalar.activation(square[:, k], bank[k][:], ACT.Square).then_inc(s["square"], 1)
                for k in range(2):
                    t = b * 2 + k
                    act.wait_ge(s["variance"], done(t))
                    nc.scalar.activation(log[:, k, 0], bank[2 + k][:], ACT.Ln, bias=EPS_LN)
                    nc.scalar.activation(log[:, k, 1], bank[2 + k][:], ACT.Ln, scale=1.0 + EPS_RMS,
                                         bias=EPS_RMS * EPS_LN).then_inc(s["log"], 1)
                for k in range(2):
                    t = b * 2 + k
                    act.wait_ge(s["log"], done(t))
                    act.wait_ge(s["x0"], freed(t))
                    nc.scalar.activation(rstd[:, k], log[:, k], ACT.Exp, scale=-0.5).then_inc(s["rstd"], 1)
            act.preload_act_table_set("silu_and_others")
            act.wait_ge(s["zeroed"], 1)
            with act.Fori(0, SEQS) as b:
                for k in range(2):
                    t = b * 2 + k
                    act.wait_ge(s["uz"], done(t))
                    act.wait_ge(s["conv"], freed(t + 1 - k))
                    for half in range(2):
                        last = nc.scalar.activation(raw[:, half, 3 + k * CH:3 + (k + 1) * CH],
                                                    bank[4 * k + half][:], ACT.Copy)
                    last.then_inc(s["raw"], 1)
                    act.wait_ge(s["u"], freed(t))
                    for half in range(2):
                        last = nc.scalar.activation(conv[:, k, half], bank[4 * k + half][:], ACT.Identity,
                                                    scale=conv_w[:, half, 3:4], bias=conv_b[:, half:half + 1])
                    last.then_inc(s["tap"], 1)
                    for half in range(2):
                        last = nc.scalar.activation(z[:, half, cols(t)], bank[4 * k + 2 + half][:], ACT.Silu)
                    last.then_inc(s["z"], 1)
                for k in range(2):
                    t = b * 2 + k
                    act.wait_ge(s["conv"], done(t))
                    act.wait_ge(s["zeroed"], 1)
                    for half in range(2):
                        last = nc.scalar.activation(u[:, half, cols(t)], conv[:, k, half], ACT.Silu)
                    last.then_inc(s["u"], 1)
            act.preload_act_table_set("natural_log_exp_and_others")
            with act.Fori(0, SEQS) as b:
                for k in range(2):
                    t = b * 2 + k
                    act.wait_ge(s["dbc"], done(t))
                    act.wait_ge(s["dtraw"], freed(t))
                    nc.scalar.activation(dt_low[:, k], bank[k][32:64, :], ACT.Copy).then_inc(s["dt_low"], 1)
                    nc.scalar.activation(parts[:, cols(t)], bank[k][:], ACT.Copy).then_inc(s["hi"], 1)
                for k in range(2):
                    t = b * 2 + k
                    act.wait_ge(s["dtraw"], done(t))
                    act.wait_ge(s["dt"], freed(t))
                    for half in range(2):
                        last = nc.scalar.activation(size[:, k, half], bank[2 + 2 * k + half][:], ACT.Abs,
                                                    bias=dt_b[:, half:half + 1])
                    last.then_inc(s["size"], 1)
                    act.wait_ge(s["size"], done(t))
                    nc.scalar.activation(size[:, k], size[:, k], ACT.Exp, scale=-1.0).then_inc(s["small"], 1)
                    act.wait_ge(s["small"], done(t))
                    nc.scalar.activation(size[:, k], size[:, k], ACT.Ln, bias=1.0).then_inc(s["dtlog"], 1)
            act.wait_ge(s["decay_ready"], 1)
            act.wait_ge(s["dtraw"], done(2 * SEQS - 1))
            with act.Fori(0, SEQS) as b:
                for m in range(STEPS):
                    i = b * STEPS + m
                    k, n = divmod(m, STATES)
                    act.wait_ge(s["b"], done(i))
                    act.wait_ge(s["dbu"], freed(i))
                    act.wait_ge(s["state"], freed(i))
                    nc.scalar.activation(b_all[:, m % 2], bank[m % 2][:], ACT.Copy).then_inc(s["b_all"], 1)
                    for half in range(2):
                        last = nc.scalar.activation(da[:, n % 2, half], dt[:, half, cols(b * 2 + k)],
                                                    ACT.Exp, scale=decay[:, half, n:n + 1])
                    last.then_inc(s["da"], 1)

        @block.gpsimd
        def _(pool):
            for name in "dtu dbu".split():
                pool.sem_inc(s[name], PRIME)
            pool.wait_ge(s["parts"], done(2 * SEQS - 1))
            pool.wait_ge(s["dt"], done(2 * SEQS - 1))
            with pool.Fori(0, SEQS) as b:
                def increments(k):
                    t = b * 2 + k
                    nc.gpsimd.tensor_tensor(dtu[:, k], dt[:, :, cols(t)], u[:, :, cols(t)], ALU.mult
                                            ).then_inc(s["dtu"], 1)

                pool.wait_ge(s["dbu"], freed(b * STEPS + 1))
                increments(0)
                for m in range(STEPS):
                    i = b * STEPS + m
                    k, n = divmod(m, STATES)
                    if n == 0:
                        pool.wait_ge(s["dtu"], done(b * 2 + k))
                    if m == STATES // 2:
                        increments(1)
                    pool.wait_ge(s["b_all"], done(i))
                    pool.wait_ge(s["state"], freed(i))
                    nc.gpsimd.tensor_tensor(dbu[:, n % 2], dtu[:, k],
                                            b_all[:, n % 2:n % 2 + 1, :].broadcast_to([P, 2, CH]), ALU.mult
                                            ).then_inc(s["dbu"], 1)

        @block.vector
        def _(dve):
            for name in ("x0 conv0 conv1 conv rest1 mid rest2 parts over dt state carried seen "
                         "summed gated branch").split():
                dve.sem_inc(s[name], PRIME)
            nc.vector.memset(raw[:, :, 0:3], 0.0).then_inc(s["zeroed"], 1)
            dve.wait_ge(s["weights_ready"], 1)
            nc.vector.tensor_scalar(in_w[:], in_w[:], rms_w[:, 0:1], None, ALU.mult).then_inc(s["folded"], 1)
            dve.wait_ge(s["decay"], 1)
            nc.vector.tensor_scalar(decay[:], decay[:], -1.0, None, ALU.mult).then_inc(s["decay_ready"], 1)
            with dve.Fori(0, SEQS) as b:
                for k in range(2):
                    t = b * 2 + k
                    dve.wait_ge(s["rstd"], done(t))
                    nc.vector.tensor_tensor(branch[:, cols(t)], bank[k][:], rstd[:, k, 0], ALU.mult)
                    nc.vector.tensor_tensor(x0[:, cols(t)], bank[k][:], rstd[:, k, 1], ALU.mult
                                            ).then_inc(s["x0"], 1)
            with dve.Fori(0, SEQS) as b:
                for k in range(2):
                    t = b * 2 + k
                    dve.wait_ge(s["tap"], done(t))
                    for tap, finished in ((2, "conv0"), (1, "conv1"), (0, "conv")):
                        for half in range(2):
                            at = raw[:, half, k * CH + tap:k * CH + tap + CH]
                            last = nc.vector.scalar_tensor_tensor(conv[:, k, half], at,
                                                                  conv_w[:, half, tap:tap + 1],
                                                                  conv[:, k, half], ALU.mult, ALU.add)
                        last.then_inc(s[finished], 1)
                        if tap:
                            dve.wait_ge(s[finished], done(t))
            with dve.Fori(0, SEQS) as b:
                for k in range(2):
                    t = b * 2 + k
                    dve.wait_ge(s["hi"], done(t))
                    nc.vector.tensor_tensor(rest[64:128, k], bank[k][64:128, :], parts[64:128, cols(t)], ALU.subtract
                                            ).then_inc(s["rest1"], 1)
                    dve.wait_ge(s["rest1"], done(t))
                    nc.vector.tensor_scalar(parts[64:128, cols(t)], rest[64:128, k], 1.0, None, ALU.mult).then_inc(s["mid"], 1)
                    dve.wait_ge(s["mid"], done(t))
                    nc.vector.tensor_tensor(rest[96:128, k], rest[96:128, k], parts[96:128, cols(t)], ALU.subtract
                                            ).then_inc(s["rest2"], 1)
                    dve.wait_ge(s["rest2"], done(t))
                    nc.vector.tensor_scalar(parts[96:128, cols(t)], rest[96:128, k], 1.0, None, ALU.mult).then_inc(s["parts"], 1)
                for k in range(2):
                    t = b * 2 + k
                    dve.wait_ge(s["size"], done(t))
                    for half in range(2):
                        last = nc.vector.tensor_scalar(dt[:, half, cols(t)], bank[2 + 2 * k + half][:],
                                                       dt_b[:, half:half + 1], 0.0, ALU.add, ALU.max)
                    last.then_inc(s["over"], 1)
                    dve.wait_ge(s["over"], done(t))
                    dve.wait_ge(s["dtlog"], done(t))
                    nc.vector.tensor_tensor(dt[:, :, cols(t)], dt[:, :, cols(t)], size[:, k], ALU.add
                                            ).then_inc(s["dt"], 1)
            with dve.Fori(0, SEQS) as b:
                def chunk_end(k):
                    t = b * 2 + k
                    dve.wait_ge(s["y"], done(b * STEPS + k * STATES + STATES - 1))
                    for half in range(2):
                        nc.vector.scalar_tensor_tensor(y[:, k, half], u[:, half, cols(t)], skip[:, half:half + 1],
                                                       bank[4 + 2 * k + half][:], ALU.mult, ALU.add
                                                       ).then_inc(s["summed"], 1)
                        dve.wait_ge(s["summed"], done(t * 2 + half))
                        last = nc.vector.tensor_tensor(y[:, k, half], y[:, k, half], z[:, half, cols(t)], ALU.mult)
                    last.then_inc(s["gated"], 1)

                def projected(k):
                    t = b * 2 + k
                    dve.wait_ge(s["out"], done(t))
                    nc.vector.tensor_tensor(branch[:, cols(t)], branch[:, cols(t)], bank[4 + 2 * k][:], ALU.add
                                            ).then_inc(s["branch"], 1)

                for m in range(STEPS):
                    k, n = divmod(m, STATES)
                    i = b * STEPS + m
                    if m == STATES + 4:
                        chunk_end(0)
                    if m == STATES + 8:
                        projected(0)
                    dve.wait_ge(s["da"], done(i))
                    dve.wait_ge(s["dbu"], done(i))
                    if k == 1:
                        dve.wait_ge(s["carried"], b * STATES + n + 1 + PRIME)
                    for half in range(2):
                        start = 0.0 if k == 0 else carry[:, n, half:half + 1]
                        last = nc.vector.tensor_tensor_scan(state[:, n % 2, half], da[:, n % 2, half],
                                                            dbu[:, n % 2, half], start, ALU.mult, ALU.add)
                    last.then_inc(s["state"], 1)
                    dve.wait_ge(s["state"], done(i))
                    dve.wait_ge(s["c"], done(i))
                    dve.wait_ge(s["y"], freed(i))
                    nc.vector.tensor_tensor(seen[:, n % 2], state[:, n % 2],
                                            bank[2 + n % 2][:].unsqueeze(1).broadcast_to([P, 2, CH]),
                                            ALU.mult).then_inc(s["seen"], 1)
                    if k == 0:
                        nc.vector.tensor_copy(carry[:, n], state[:, n % 2, :, CH - 1]).then_inc(s["carried"], 1)
                chunk_end(1)
                projected(1)


def mlp(nc, mem, dram):
    x, mean, branch = mem["x"], mem["mean"], mem["branch"]
    with ExitStack() as ctx:
        def sb(name, shape, dt=F32):
            return ctx.enter_context(nc.sbuf_tensor(f"mlp_{name}", shape, dt))

        fc1 = sb("fc1", [P, 2, P])
        fc2 = sb("fc2", [P, 2, 2, P])
        fc3 = sb("fc3", [P, 2, P])
        rms_w = sb("rms_w", [P, 1])
        bias = sb("bias", [P, 5])
        square = sb("square", [P, 2, CH])
        log = sb("log", [P, 2, CH])
        rstd = sb("rstd", [P, 2, CH])
        normed = sb("normed", [P, 2, CH])
        hidden = [sb(f"hidden{n}", [P, 2, 2, CH]) for n in range(2)]
        bank = [ctx.enter_context(nc.psum_tensor(f"mlp_bank{n}", [P, CH], F32)) for n in range(8)]
        (weights, folded, sq, power, lg, rs, nm, up, act1, mid, act2, down, first, xd) = semaphores(
            ctx, nc, "mlp", "weights folded square power log rstd normed up hidden0 mid hidden1 down first x")
        block = ctx.enter_context(nc.Block())

        @block.sync
        def _(sp):
            for to, name in ((fc1[:], "fc1"), (fc2[:], "fc2"), (fc3[:], "fc3"), (rms_w[:], "rms2"), (bias[:], "mlp_b")):
                sp.dma_start(to, dram[name]).then_inc(weights, 16)
            sp.wait_ge(weights, 80)

        @block.tensor
        def _(pe):
            for n in (power, up, mid, down):
                pe.sem_inc(n, PRIME)
            pe.wait_ge(folded, 1)
            with pe.Fori(0, SEQS) as b:
                for k in range(2):
                    t = b * 2 + k
                    pe.wait_ge(sq, done(t))
                    pe.wait_ge(xd, freed(t))
                    nc.tensor.matmul(bank[k][:], mean[:], square[:, k], start=True, stop=True).then_inc(power, 1)
                for k in range(2):
                    t = b * 2 + k
                    pe.wait_ge(nm, done(t))
                    pe.wait_ge(act2, freed(t))
                    for m in range(2):
                        last = nc.tensor.matmul(bank[2 + 2 * k + m][:], fc1[:, m], normed[:, k], start=True, stop=True)
                    last.then_inc(up, 1)
                for k in range(2):
                    t = b * 2 + k
                    pe.wait_ge(act1, done(t))
                    for m in range(2):
                        for c in range(2):
                            last = nc.tensor.matmul(bank[2 + 2 * k + m][:], fc2[:, c, m], hidden[0][:, k, c],
                                                    start=c == 0, stop=c == 1)
                    last.then_inc(mid, 1)
                for k in range(2):
                    t = b * 2 + k
                    pe.wait_ge(act2, done(t))
                    for c in range(2):
                        last = nc.tensor.matmul(bank[k][:], fc3[:, c], hidden[1][:, k, c], start=c == 0, stop=c == 1)
                    last.then_inc(down, 1)

        @block.scalar
        def _(act):
            for n in (sq, lg, rs, act1, act2):
                act.sem_inc(n, PRIME)
            act.wait_ge(weights, 80)
            with act.Fori(0, SEQS) as b:
                for k in range(2):
                    t = b * 2 + k
                    nc.scalar.activation(square[:, k], branch[:, cols(t)], ACT.Square).then_inc(sq, 1)
                for k in range(2):
                    t = b * 2 + k
                    act.wait_ge(power, done(t))
                    nc.scalar.activation(log[:, k], bank[k][:], ACT.Ln, bias=EPS_RMS).then_inc(lg, 1)
                for k in range(2):
                    t = b * 2 + k
                    act.wait_ge(lg, done(t))
                    act.wait_ge(nm, freed(t))
                    nc.scalar.activation(rstd[:, k], log[:, k], ACT.Exp, scale=-0.5).then_inc(rs, 1)
                for k in range(2):
                    t = b * 2 + k
                    act.wait_ge(up, done(t))
                    for m in range(2):
                        last = nc.scalar.activation(hidden[0][:, k, m], bank[2 + 2 * k + m][:], ACT.Relu,
                                                    bias=bias[:, m:m + 1])
                    last.then_inc(act1, 1)
                for k in range(2):
                    t = b * 2 + k
                    act.wait_ge(mid, done(t))
                    act.wait_ge(down, freed(t))
                    for m in range(2):
                        last = nc.scalar.activation(hidden[1][:, k, m], bank[2 + 2 * k + m][:], ACT.Relu,
                                                    bias=bias[:, 2 + m:3 + m])
                    last.then_inc(act2, 1)

        @block.vector
        def _(dve):
            for n in (nm, first, xd):
                dve.sem_inc(n, PRIME)
            dve.wait_ge(weights, 80)
            nc.vector.tensor_scalar(fc1[:], fc1[:], rms_w[:, 0:1], None, ALU.mult).then_inc(folded, 1)
            with dve.Fori(0, SEQS) as b:
                for k in range(2):
                    t = b * 2 + k
                    dve.wait_ge(rs, done(t))
                    dve.wait_ge(up, freed(t))
                    nc.vector.tensor_tensor(normed[:, k], branch[:, cols(t)], rstd[:, k], ALU.mult).then_inc(nm, 1)
                for k in range(2):
                    t = b * 2 + k
                    nc.vector.tensor_tensor(x[:, cols(t)], x[:, cols(t)], branch[:, cols(t)], ALU.add
                                            ).then_inc(first, 1)
                for k in range(2):
                    t = b * 2 + k
                    dve.wait_ge(down, done(t))
                    dve.wait_ge(first, done(t))
                    nc.vector.scalar_tensor_tensor(x[:, cols(t)], bank[k][:], bias[:, 4:5], x[:, cols(t)],
                                                   ALU.add, ALU.add).then_inc(xd, 1)


HEADS = 8
HEAD = 64
WINDOW = 64
INNER = HEADS * HEAD
TILE = 128
TILES = T // TILE
LAG = 3
HID = 341
HID_PARTS = [(0, 128), (128, 128), (256, 85)]


def normalise(nc, mem, dram):
    x, centre, mean, branch = mem["x"], mem["centre"], mem["mean"], mem["branch"]
    with ExitStack() as ctx:
        def sb(name, shape, dt=F32):
            return ctx.enter_context(nc.sbuf_tensor(f"norm_{name}", shape, dt))

        square = sb("square", [P, 2, CH])
        log = sb("log", [P, 2, CH])
        rstd = sb("rstd", [P, 2, CH])
        bank = [ctx.enter_context(nc.psum_tensor(f"norm_bank{n}", [P, CH], F32)) for n in range(4)]
        centred, sq, variance, lg, rs, out = semaphores(ctx, nc, "norm", "centred square variance log rstd out")
        block = ctx.enter_context(nc.Block())

        @block.tensor
        def _(pe):
            for n in (centred, variance):
                pe.sem_inc(n, PRIME)
            with pe.Fori(0, SEQS) as b:
                for k in range(2):
                    t = b * 2 + k
                    pe.wait_ge(out, freed(t))
                    nc.tensor.matmul(bank[k][:], centre[:], x[:, cols(t)], start=True, stop=True).then_inc(centred, 1)
                for k in range(2):
                    t = b * 2 + k
                    pe.wait_ge(sq, done(t))
                    nc.tensor.matmul(bank[2 + k][:], mean[:], square[:, k], start=True, stop=True).then_inc(variance, 1)

        @block.scalar
        def _(act):
            for n in (sq, lg, rs):
                act.sem_inc(n, PRIME)
            act.preload_act_table_set("natural_log_exp_and_others")
            with act.Fori(0, SEQS) as b:
                for k in range(2):
                    t = b * 2 + k
                    act.wait_ge(centred, done(t))
                    nc.scalar.activation(square[:, k], bank[k][:], ACT.Square).then_inc(sq, 1)
                for k in range(2):
                    t = b * 2 + k
                    act.wait_ge(variance, done(t))
                    nc.scalar.activation(log[:, k], bank[2 + k][:], ACT.Ln, bias=EPS_LN).then_inc(lg, 1)
                for k in range(2):
                    t = b * 2 + k
                    act.wait_ge(lg, done(t))
                    act.wait_ge(out, freed(t))
                    nc.scalar.activation(rstd[:, k], log[:, k], ACT.Exp, scale=-0.5).then_inc(rs, 1)

        @block.vector
        def _(dve):
            dve.sem_inc(out, PRIME)
            with dve.Fori(0, SEQS) as b:
                for k in range(2):
                    t = b * 2 + k
                    dve.wait_ge(rs, done(t))
                    nc.vector.tensor_tensor(branch[:, cols(t)], bank[k][:], rstd[:, k], ALU.mult).then_inc(out, 1)


ATTEND = ("qkv_loaded tables_loaded zeroed hs rotate0 rotate1 tables_ready proj qk_copied v_copied "
          "square sums floor log rnorm direct crossed added scaled qkT qkT_copied "
          "sim peak shifted prob total pT pT_copied av inv out oT oT_copied wo branch")


def attend(nc, mem, dram, layer):
    branch, ident = mem["branch"], mem["ident"]
    with ExitStack() as ctx:
        def sb(name, shape, dt=F32):
            return ctx.enter_context(nc.sbuf_tensor(f"at{layer}_{name}", shape, dt))

        w = sb("w", [P, 3 * INNER])
        wo = sb("wo", [P, 4, P])
        eye16 = sb("eye16", [P, P], BF16)
        mask = sb("mask", [P, 2, TILE], BF16)
        turn = sb("turn", [P, 2, TILES, 2, HEAD])
        scales = sb("scales", [P, 2, 2, HEAD])
        hs = sb("hs", [P, 1 + T])
        qk = sb("qk", [P, 2, 2 * INNER])
        square = sb("square", [P, 2, 2 * INNER])
        direct = sb("direct", [P, 4, 2 * INNER])
        crossed = square
        sums = sb("sums", [P, 2, 2 * HEADS])
        floor = sb("floor", [P, 2, 2 * HEADS])
        log = sb("log", [P, 2, 2 * HEADS])
        rnorm = sb("rnorm", [P, 2, 2 * HEADS])
        qT = sb("qT", [P, 4, T])
        kT = sb("kT", [P, 4, WINDOW + T])
        v = sb("v", [P, TILES, INNER])
        v_off = sb("v_off", [P, TILES, INNER])
        peak = sb("peak", [P, 2, HEADS])
        prob = sb("prob", [P, 2, HEADS, TILE])
        pT = sb("pT", [P, HEADS, TILE])
        total = sb("total", [P, 2, HEADS])
        inv = sb("inv", [P, 2, HEADS])
        out = sb("out", [P, 2, INNER])
        oT = sb("oT", [P, 2, 4, TILE])
        ps = ctx.enter_context(nc.psum_tensor(f"at{layer}_ps", [P, 8, CH], F32))
        s = dict(zip(ATTEND.split(), semaphores(ctx, nc, f"at{layer}", ATTEND)))
        v_moved = semaphores(ctx, nc, f"at{layer}", "moved0 moved1")
        block = ctx.enter_context(nc.Block())

        @block.sync
        def _(sp):
            sp.dma_start(w[:], dram["wqkv"][layer]).then_inc(s["qkv_loaded"], 16)
            sp.dma_start(wo[:], dram["wo"][layer].rearrange("(c p) n -> p c n", p=P)).then_inc(s["qkv_loaded"], 16)
            sp.dma_start(eye16[:], dram["eye16"]).then_inc(s["qkv_loaded"], 16)
            sp.dma_start(mask[:], dram["mask"]).then_inc(s["qkv_loaded"], 16)
            sp.dma_start(turn[:], dram["turn"]).then_inc(s["tables_loaded"], 16)
            for n, name in enumerate(("q_scale", "k_scale")):
                row = dram[name][layer:layer + 1]
                for half in range(2):
                    h0, h1 = half * 32, (1 - half) * 32
                    if half == 0:
                        sp.dma_start(scales[:, 0, n], row.partition_broadcast(P)).then_inc(s["tables_loaded"], 16)
                    sp.dma_start(scales[:, 1, n, h0:h0 + 32], row[:, h1:h1 + 32].partition_broadcast(P)
                                 ).then_inc(s["tables_loaded"], 16)
            sp.wait_ge(s["tables_loaded"], 16 * 7)

        @block.tensor
        def _(pe):
            for name in "proj qkT sim pT av oT wo".split():
                pe.sem_inc(s[name], PRIME)
            pe.wait_ge(s["qkv_loaded"], 64)
            with pe.Fori(0, SEQS) as b:
                for i in range(TILES + LAG):
                    if i < TILES:
                        g = b * TILES + i
                        p = i % 2
                        if i == 0:
                            pe.wait_ge(s["hs"], b + 1)
                        pe.wait_ge(s["qk_copied"], freed(g))
                        pe.wait_ge(s["v_copied"], freed(g))
                        if i < 2:
                            pe.wait_ge(s["branch"], b * TILES + PRIME)
                        for m, to in enumerate((2 * p, 2 * p + 1, 4 + p)):
                            last = nc.tensor.matmul(ps[:, to], hs[:, i * TILE:(i + 1) * TILE],
                                                    w[:, m * INNER:(m + 1) * INNER], start=True, stop=True)
                        last.then_inc(s["proj"], 1)
                    if i >= LAG:
                        g = b * TILES + i - LAG
                        pe.wait_ge(s["scaled"], done(g))
                        pe.wait_ge(s["qkT_copied"], freed(g + 1))
                        for m in range(8):
                            last = nc.tensor.transpose(ps[:, 6 + m // 4, (m % 4) * TILE:(m % 4 + 1) * TILE],
                                                       direct[:, (i - LAG) % 4, m * TILE:(m + 1) * TILE], ident[:])
                        last.then_inc(s["qkT"], 1)

                def similarities(i):
                    g = b * TILES + i
                    p = i % 2
                    pe.wait_ge(s["qkT_copied"], done(g))
                    pe.wait_ge(s["shifted"], freed(g))
                    for parity in range(2):
                        nc.tensor.matmul(ps[:, 2 * p + parity].rearrange("p (h j) -> p h j", h=4), eye16[:],
                                         mask[:, int(i == 0):int(i == 0) + 1].broadcast_to([P, 4, TILE]),
                                         start=True, stop=False, skip_group_check=True)
                    for h in range(HEADS):
                        at = slice(HEAD * (h % 2), HEAD * (h % 2) + HEAD)
                        for q in range(2):
                            last = nc.tensor.matmul(
                                ps[64 * q:64 * q + 64, 2 * p + h % 2, (h // 2) * TILE:(h // 2 + 1) * TILE],
                                qT[at, h // 2, i * TILE + 64 * q:i * TILE + 64 * q + 64],
                                kT[at, h // 2, i * TILE + 64 * q:i * TILE + 64 * q + TILE],
                                start=False, stop=True, skip_group_check=True)
                    last.then_inc(s["sim"], 1)

                pe.wait_ge(s["qk_copied"], done(b * TILES + TILES - 1))
                pe.wait_ge(s["v_copied"], done(b * TILES + TILES - 1))
                similarities(0)
                similarities(1)
                for i in range(TILES + 2):
                    g = b * TILES + i
                    p = i % 2
                    if i < TILES:
                        pe.wait_ge(s["prob"], done(g))
                        pe.wait_ge(s["pT_copied"], freed(g + 1))
                        for h in range(HEADS):
                            last = nc.tensor.transpose(ps[:, 4 + h // 4, (h % 4) * TILE:(h % 4 + 1) * TILE],
                                                       prob[:, p, h], ident[:])
                        last.then_inc(s["pT"], 1)
                    if i >= 2:
                        pe.wait_ge(s["oT_copied"], done(g - 2))
                        for m in range(4):
                            last = nc.tensor.matmul(ps[:, 7, 0:TILE], wo[:, m], oT[:, p, m],
                                                    start=m == 0, stop=m == 3)
                        last.then_inc(s["wo"], 1)
                    if i + 2 < TILES:
                        similarities(i + 2)
                    if i < TILES:
                        if i == 0:
                            pe.wait_ge(s["qkT_copied"], done(b * TILES + TILES - 1))
                        pe.wait_ge(s["pT_copied"], done(g))
                        pe.wait_ge(v_moved[i // 4], 32 * b + 32)
                        pe.wait_ge(s["out"], freed(g + 1))
                        for j in range(HEADS):
                            h = 2 * (j % 4) + j // 4
                            at = slice(h * HEAD, (h + 1) * HEAD)
                            for q, values in ((0, v_off), (1, v)):
                                last = nc.tensor.matmul(ps[64 * q:64 * q + 64, 6, at], pT[:, j, 64 * q:64 * q + 64],
                                                        values[:, i, at], start=True, stop=True)
                        last.then_inc(s["av"], 1)
                    if 1 <= i <= TILES:
                        pe.wait_ge(s["out"], done(g - 1))
                        if i >= 2:
                            pe.wait_ge(s["branch"], done(g - 2))
                        for m in range(4):
                            last = nc.tensor.transpose(ps[:, 7, m * TILE:(m + 1) * TILE],
                                                       out[:, 1 - p, m * TILE:(m + 1) * TILE], ident[:])
                        last.then_inc(s["oT"], 1)

        @block.scalar
        def _(act):
            for name in "qk_copied v_copied square log rnorm qkT_copied prob pT_copied oT_copied".split():
                act.sem_inc(s[name], PRIME)
            act.preload_act_table_set("natural_log_exp_and_others")
            act.wait_ge(s["zeroed"], 3)
            with act.Fori(0, SEQS) as b:
                act.wait_ge(s["proj"], b * TILES + PRIME)
                nc.scalar.activation(hs[0:64, 0:T], branch[0:64, bass.ds(b * T, T)], ACT.Copy)
                nc.scalar.activation(hs[64:128, 1:1 + T], branch[64:128, bass.ds(b * T, T)], ACT.Copy
                                     ).then_inc(s["hs"], 1)
                for i in range(TILES + LAG):
                    if i < TILES:
                        g = b * TILES + i
                        p = i % 2
                        act.wait_ge(s["proj"], done(g))
                        act.wait_ge(s["crossed"], freed(g))
                        nc.scalar.activation(qk[:, p], ps[:, 2 * p:2 * p + 2].rearrange("p a n -> p (a n)"), ACT.Copy
                                             ).then_inc(s["qk_copied"], 1)
                        if i == 0:
                            act.wait_ge(s["av"], b * TILES + PRIME)
                        nc.scalar.activation(v[:, i], ps[:, 4 + p], ACT.Copy).then_inc(s["v_copied"], 1)
                        act.wait_ge(s["qk_copied"], done(g))
                        act.wait_ge(s["added"], freed(g))
                        nc.scalar.activation(square[:, p], qk[:, p], ACT.Square).then_inc(s["square"], 1)
                        if i % 4 == 3:
                            part, first, last = i // 4, i - 3, i + 1
                            act.wait_ge(s["v_copied"], done(g))
                            lo = max(first, 1)
                            act.dma_start(v_off[0:64, lo:last], v[64:128, lo - 1:last - 1]).then_inc(v_moved[part], 16)
                            act.dma_start(v_off[64:128, first:last], v[0:64, first:last]).then_inc(v_moved[part], 16)
                    if 1 <= i <= TILES:
                        g = b * TILES + i - 1
                        p = 1 - i % 2
                        act.wait_ge(s["floor"], done(g))
                        nc.scalar.activation(log[:, p], floor[:, p], ACT.Ln, scale=2.0 ** 30).then_inc(s["log"], 1)
                        act.wait_ge(s["log"], done(g))
                        act.wait_ge(s["scaled"], freed(g))
                        nc.scalar.activation(rnorm[:, p], log[:, p], ACT.Exp, scale=-0.5,
                                             bias=float(15 * np.log(2.0))).then_inc(s["rnorm"], 1)
                    if i >= LAG:
                        g = b * TILES + i - LAG
                        act.wait_ge(s["qkT"], done(g))
                        if i == LAG:
                            act.wait_ge(s["sim"], b * TILES + PRIME)
                        at = (i - LAG) * TILE
                        nc.scalar.activation(qT[:, :, at:at + TILE],
                                             ps[:, 6].rearrange("p (m t) -> p m t", m=4), ACT.Copy)
                        nc.scalar.activation(kT[:, :, WINDOW + at:WINDOW + at + TILE],
                                             ps[:, 7].rearrange("p (m t) -> p m t", m=4), ACT.Copy
                                             ).then_inc(s["qkT_copied"], 1)

                def exponentials(i):
                    g = b * TILES + i
                    act.wait_ge(s["shifted"], done(g))
                    nc.scalar.activation(prob[:, i % 2], prob[:, i % 2], ACT.Exp).then_inc(s["prob"], 1)

                exponentials(0)
                for i in range(TILES + 1):
                    g = b * TILES + i
                    if i < TILES:
                        act.wait_ge(s["pT"], done(g))
                        act.wait_ge(s["av"], freed(g + 1))
                        nc.scalar.activation(pT[:].rearrange("p h q -> p (h q)"),
                                             ps[:, 4:6].rearrange("p a n -> p (a n)"), ACT.Copy
                                             ).then_inc(s["pT_copied"], 1)
                    if i + 1 < TILES:
                        exponentials(i + 1)
                    if i >= 1:
                        act.wait_ge(s["oT"], done(g - 1))
                        act.wait_ge(s["wo"], freed(g - 1))
                        nc.scalar.activation(oT[:, (i - 1) % 2].rearrange("p m t -> p (m t)"), ps[:, 7], ACT.Copy
                                             ).then_inc(s["oT_copied"], 1)

        @block.gpsimd
        def _(pool):
            for name in "added scaled".split():
                pool.sem_inc(s[name], PRIME)
            with pool.Fori(0, SEQS) as b:
                for i in range(TILES):
                    g = b * TILES + i
                    p, d = i % 2, i % 4
                    pool.wait_ge(s["crossed"], done(g))
                    nc.gpsimd.tensor_tensor(direct[:, d], direct[:, d], crossed[:, p], ALU.add
                                            ).then_inc(s["added"], 1)
                    pool.wait_ge(s["added"], done(g))
                    pool.wait_ge(s["rnorm"], done(g))
                    nc.gpsimd.tensor_tensor(direct[:, d].rearrange("p (h e) -> p h e", e=HEAD),
                                            direct[:, d].rearrange("p (h e) -> p h e", e=HEAD),
                                            rnorm[:, p].unsqueeze(2).broadcast_to([P, 2 * HEADS, HEAD]),
                                            ALU.mult).then_inc(s["scaled"], 1)

        @block.vector
        def _(dve):
            for name in "sums floor direct crossed peak shifted total inv out branch".split():
                dve.sem_inc(s[name], PRIME)
            nc.vector.memset(hs[64:128, 0:1], 0.0).then_inc(s["zeroed"], 1)
            nc.vector.memset(kT[:, :, 0:WINDOW], 0.0).then_inc(s["zeroed"], 1)
            nc.vector.memset(v_off[0:64, 0], 0.0).then_inc(s["zeroed"], 1)
            dve.wait_ge(s["tables_loaded"], 16 * 7)
            dve.wait_ge(s["zeroed"], 3)
            for n in range(2):
                nc.vector.tensor_tensor(turn[:, n], turn[:, n],
                                        scales[:, n].unsqueeze(1).broadcast_to([P, TILES, 2, HEAD]), ALU.mult
                                        ).then_inc(s["tables_ready"], 1)
            dve.wait_ge(s["tables_ready"], 2)
            with dve.Fori(0, SEQS) as b:
                for i in range(TILES):
                    g = b * TILES + i
                    p = i % 2
                    dve.wait_ge(s["square"], done(g))
                    nc.vector.tensor_reduce(sums[:, p], square[:, p].rearrange("p (h d) -> p h d", d=HEAD), AX_X,
                                            ALU.add).then_inc(s["sums"], 1)
                    dve.wait_ge(s["sums"], done(g))
                    nc.vector.tensor_scalar(floor[:, p], sums[:, p], 1e-24, None, ALU.max).then_inc(s["floor"], 1)
                    if i >= 4:
                        dve.wait_ge(s["qkT"], done(g - 4))
                    for m in range(2):
                        of = qk[:, p, m * INNER:(m + 1) * INNER].rearrange("p (h d) -> p h d", d=HEAD)
                        to = direct[:, i % 4, m * INNER:(m + 1) * INNER].rearrange("p (h d) -> p h d", d=HEAD)
                        last = nc.vector.tensor_tensor(to, of, turn[:, 0, i, m:m + 1].broadcast_to([P, HEADS, HEAD]),
                                                       ALU.mult)
                    last.then_inc(s["direct"], 1)
                    for half in range(2):
                        h0, h1 = 32 * half, 32 * (1 - half)
                        for m in range(2):
                            of = qk[:, p, m * INNER:(m + 1) * INNER].rearrange("p (h d) -> p h d", d=HEAD)
                            to = crossed[:, p, m * INNER:(m + 1) * INNER].rearrange("p (h d) -> p h d", d=HEAD)
                            last = nc.vector.tensor_tensor(
                                to[:, :, h0:h0 + 32], of[:, :, h1:h1 + 32],
                                turn[:, 1, i, m:m + 1, h0:h0 + 32].broadcast_to([P, HEADS, 32]), ALU.mult)
                    last.then_inc(s["crossed"], 1)
                def shifted_scores(i):
                    g = b * TILES + i
                    p = i % 2
                    dve.wait_ge(s["sim"], done(g))
                    scores = ps[:, 2 * p:2 * p + 2].rearrange("p a (h j) -> p (a h) j", h=4)
                    nc.vector.tensor_reduce(peak[:, p], scores, AX_X, ALU.max).then_inc(s["peak"], 1)
                    dve.wait_ge(s["peak"], done(g))
                    dve.wait_ge(s["pT"], freed(g))
                    dve.wait_ge(s["total"], freed(g))
                    nc.vector.tensor_tensor(prob[:, p], scores,
                                            peak[:, p].unsqueeze(2).broadcast_to([P, HEADS, TILE]),
                                            ALU.subtract).then_inc(s["shifted"], 1)

                shifted_scores(0)
                for i in range(TILES + 2):
                    g = b * TILES + i
                    p = i % 2
                    if i + 1 < TILES:
                        shifted_scores(i + 1)
                    if i >= 2:
                        at = branch[:, cols(g - 2, TILE)]
                        dve.wait_ge(s["wo"], done(g - 2))
                        nc.vector.tensor_tensor(at, at, ps[:, 7, 0:TILE], ALU.add).then_inc(s["branch"], 1)
                    if i < TILES:
                        dve.wait_ge(s["prob"], done(g))
                        nc.vector.tensor_reduce(total[:, p], prob[:, p], AX_X, ALU.add).then_inc(s["total"], 1)
                        dve.wait_ge(s["total"], done(g))
                        nc.vector.reciprocal(inv[:, p], total[:, p]).then_inc(s["inv"], 1)
                        dve.wait_ge(s["inv"], done(g))
                        dve.wait_ge(s["av"], done(g))
                        dve.wait_ge(s["oT"], freed(g))
                        nc.vector.tensor_tensor(
                            out[:, p].rearrange("p (h a d) -> p a h d", a=2, d=HEAD),
                            ps[:, 6].rearrange("p (h a d) -> p a h d", a=2, d=HEAD),
                            inv[:, p].rearrange("p (a h) -> p a h", a=2).unsqueeze(3).broadcast_to([P, 2, 4, HEAD]),
                            ALU.mult).then_inc(s["out"], 1)


GLU = ("w_loaded lb_done biased folded zeroed hs centred square variance log rstd normed up gate act prod down branch")


def gated_mlp(nc, mem, dram, layer):
    branch, x, centre, mean = mem["branch"], mem["x"], mem["centre"], mem["mean"]
    with ExitStack() as ctx:
        def sb(name, shape, dt=F32):
            return ctx.enter_context(nc.sbuf_tensor(f"glu{layer}_{name}", shape, dt))

        w1 = sb("w1", [P, 2 * HID])
        w2 = sb("w2", [P, 3, P])
        ln_g = sb("ln_g", [P, 1])
        ln_b = sb("ln_b", [P, 1])
        b1 = sb("b1", [P, 2, 3])
        b2 = sb("b2", [P, 1])
        hs = sb("hs", [P, 1 + T])
        square = sb("square", [P, 2, CH])
        log = sb("log", [P, 2, CH])
        rstd = sb("rstd", [P, 2, CH])
        normed = sb("normed", [P, ALL])
        gelu = sb("gelu", [P, 2, 3, CH])
        prod = sb("prod", [P, 2, 3, CH])
        bank = [ctx.enter_context(nc.psum_tensor(f"glu{layer}_bank{n}", [P, CH], F32)) for n in range(8)]
        s = dict(zip(GLU.split(), semaphores(ctx, nc, f"glu{layer}", GLU)))
        (x_sem,) = semaphores(ctx, nc, f"glu{layer}", "x")
        block = ctx.enter_context(nc.Block())

        @block.sync
        def _(sp):
            n = 0
            loads = [(w1[:], dram["w1"][layer]), (ln_g[:], dram["ln_g"][layer]),
                     (ln_b[:], dram["ln_b"][layer]), (b2[:], dram["b2"][layer]),
                     (b1[:], dram["b1"][layer])]
            for c, (first, size) in enumerate(HID_PARTS):
                loads.append((w2[0:size, c], dram["w2"][layer, first:first + size]))
            for to, of in loads:
                sp.dma_start(to, of).then_inc(s["w_loaded"], 16)
                n += 16
            sp.wait_ge(s["w_loaded"], n)

        @block.tensor
        def _(pe):
            for name in "centred variance up down".split():
                pe.sem_inc(s[name], PRIME)
            pe.wait_ge(s["w_loaded"], 16 * 8)
            for m in range(2):
                for c, (first, size) in enumerate(HID_PARTS):
                    last = nc.tensor.matmul(bank[6][0:size, 3 * m + c:3 * m + c + 1],
                                            w1[:, m * HID + first:m * HID + first + size], ln_b[:],
                                            start=True, stop=True)
            last.then_inc(s["lb_done"], 1)
            pe.wait_ge(s["folded"], 1)
            with pe.Fori(0, SEQS) as b:
                for k in range(2):
                    t = b * 2 + k
                    pe.wait_ge(s["hs"], done(t))
                    pe.wait_ge(s["normed"], freed(t))
                    nc.tensor.matmul(bank[k][:], centre[:], hs[:, k * CH:(k + 1) * CH], start=True, stop=True
                                     ).then_inc(s["centred"], 1)
                for k in range(2):
                    t = b * 2 + k
                    pe.wait_ge(s["square"], done(t))
                    nc.tensor.matmul(bank[2 + k][:], mean[:], square[:, k], start=True, stop=True
                                     ).then_inc(s["variance"], 1)
            pe.wait_ge(s["normed"], done(2 * SEQS - 1))

            def up(t):
                pe.wait_ge(s["prod"], freed(t + 1))
                for m in range(2):
                    for c, (first, size) in enumerate(HID_PARTS):
                        last = nc.tensor.matmul(bank[3 * m + c][0:size, :],
                                                w1[:, m * HID + first:m * HID + first + size],
                                                normed[:, cols(t)], start=True, stop=True)
                last.then_inc(s["up"], 1)

            def down(t, k):
                pe.wait_ge(s["prod"], done(t))
                pe.wait_ge(s["branch"], freed(t))
                for c, (first, size) in enumerate(HID_PARTS):
                    last = nc.tensor.matmul(bank[6 + k][:], w2[0:size, c], prod[0:size, k, c],
                                            start=c == 0, stop=c == 2)
                last.then_inc(s["down"], 1)

            up(0)
            with pe.Fori(0, SEQS - 1) as b:
                for k in range(2):
                    t = b * 2 + k
                    up(t + 1)
                    down(t, k)
            up(2 * SEQS - 1)
            down(2 * SEQS - 2, 0)
            down(2 * SEQS - 1, 1)

        @block.scalar
        def _(act):
            for name in "hs square log rstd act".split():
                act.sem_inc(s[name], PRIME)
            act.preload_act_table_set("natural_log_exp_and_others")
            act.wait_ge(s["zeroed"], 1)
            with act.Fori(0, SEQS) as b:
                for k in range(2):
                    t = b * 2 + k
                    act.wait_ge(s["centred"], freed(t))
                    nc.scalar.activation(hs[0:64, k * CH:(k + 1) * CH], branch[0:64, cols(t)], ACT.Copy)
                    nc.scalar.activation(hs[64:128, 1 + k * CH:1 + (k + 1) * CH], branch[64:128, cols(t)], ACT.Copy
                                         ).then_inc(s["hs"], 1)
                for k in range(2):
                    t = b * 2 + k
                    act.wait_ge(s["centred"], done(t))
                    nc.scalar.activation(square[:, k], bank[k][:], ACT.Square).then_inc(s["square"], 1)
                for k in range(2):
                    t = b * 2 + k
                    act.wait_ge(s["variance"], done(t))
                    nc.scalar.activation(log[:, k], bank[2 + k][:], ACT.Ln, bias=EPS_LN).then_inc(s["log"], 1)
                for k in range(2):
                    t = b * 2 + k
                    act.wait_ge(s["log"], done(t))
                    act.wait_ge(s["normed"], freed(t))
                    nc.scalar.activation(rstd[:, k], log[:, k], ACT.Exp, scale=-0.5).then_inc(s["rstd"], 1)
            act.preload_act_table_set("gelu_and_others")
            with act.Fori(0, SEQS) as b:
                for k in range(2):
                    t = b * 2 + k
                    act.wait_ge(s["up"], done(t))
                    act.wait_ge(s["prod"], freed(t))
                    for c, (first, size) in enumerate(HID_PARTS):
                        last = nc.scalar.activation(gelu[0:size, k, c], bank[3 + c][0:size, :], ACT.Gelu,
                                                    bias=b1[0:size, 1, c:c + 1])
                    last.then_inc(s["act"], 1)

        @block.vector
        def _(dve):
            for name in "normed prod branch".split():
                dve.sem_inc(s[name], PRIME)
            nc.vector.memset(hs[64:128, 0:1], 0.0).then_inc(s["zeroed"], 1)
            dve.wait_ge(s["w_loaded"], 16 * 8)
            dve.wait_ge(s["lb_done"], 1)
            for c, (first, size) in enumerate(HID_PARTS):
                last = nc.vector.tensor_tensor(
                    b1[0:size, :, c], b1[0:size, :, c],
                    bank[6][0:size, 0:6].rearrange("p (m c) -> p m c", m=2)[:, :, c], ALU.add)
            last.then_inc(s["biased"], 1)
            nc.vector.tensor_scalar(w1[:], w1[:], ln_g[:, 0:1], None, ALU.mult).then_inc(s["folded"], 1)
            dve.wait_ge(s["biased"], 1)
            with dve.Fori(0, SEQS) as b:
                for k in range(2):
                    t = b * 2 + k
                    dve.wait_ge(s["rstd"], done(t))
                    nc.vector.tensor_tensor(normed[:, cols(t)], bank[k][:], rstd[:, k], ALU.mult
                                            ).then_inc(s["normed"], 1)

            def gated(t, k):
                dve.wait_ge(s["act"], done(t))
                dve.wait_ge(s["down"], freed(t))
                for c, (first, size) in enumerate(HID_PARTS):
                    last = nc.vector.scalar_tensor_tensor(prod[0:size, k, c], bank[c][0:size, :],
                                                          b1[0:size, 0, c:c + 1], gelu[0:size, k, c],
                                                          ALU.add, ALU.mult)
                last.then_inc(s["prod"], 1)

            def added(t, k):
                at = branch[:, cols(t)]
                dve.wait_ge(s["down"], done(t))
                nc.vector.scalar_tensor_tensor(at, bank[6 + k][:], b2[:, 0:1], at, ALU.add, ALU.add
                                               ).then_inc(s["branch"], 1)
                if layer == 1:
                    dve.wait_ge(s["branch"], done(t))
                    nc.vector.tensor_tensor(x[:, cols(t)], x[:, cols(t)], at, ALU.add).then_inc(x_sem, 1)

            gated(0, 0)
            with dve.Fori(0, SEQS - 1) as b:
                for k in range(2):
                    t = b * 2 + k
                    gated(t + 1, 1 - k)
                    added(t, k)
            gated(2 * SEQS - 1, 1)
            added(2 * SEQS - 2, 0)
            added(2 * SEQS - 1, 1)


def store_result(nc, mem, out):
    with ExitStack() as ctx:
        (stored,) = semaphores(ctx, nc, "end", "stored")
        block = ctx.enter_context(nc.Block())

        @block.sync
        def _(sp):
            sp.dma_start(out, mem["x"][:]).then_inc(stored, 16)
            sp.wait_ge(stored, 16)


def attend_first(nc, mem, dram):
    attend(nc, mem, dram, 0)


def gated_mlp_first(nc, mem, dram):
    gated_mlp(nc, mem, dram, 0)


def attend_second(nc, mem, dram):
    attend(nc, mem, dram, 1)


def gated_mlp_second(nc, mem, dram):
    gated_mlp(nc, mem, dram, 1)


STAGES = [min_gru, experts, mamba, mlp, normalise, attend_first, gated_mlp_first, attend_second, gated_mlp_second]


def program(nc, dram, out, stages=None):
    with ExitStack() as ctx:
        mem = {name: ctx.enter_context(nc.sbuf_tensor(name, shape, F32)) for name, shape in (
            ("x", [P, ALL]), ("branch", [P, ALL]), ("centre", [P, P]), ("mean", [P, P]), ("ident", [P, P]))}
        load_constants(nc, mem, dram)
        nc.all_engine_barrier()
        for stage in STAGES if stages is None else stages:
            stage(nc, mem, dram)
            nc.all_engine_barrier()
        store_result(nc, mem, out)


def shape_constants():
    eye = np.eye(P, dtype=np.float32)
    mean = np.full((P, P), 1.0 / P, np.float32)
    pick = np.zeros((P, 32, P), np.float32)
    for first in (0, 64, 96):
        pick[first + np.arange(32), np.arange(32)] = 1.0
    query, key = np.arange(TILE)[:, None] % WINDOW, np.arange(TILE)[None, :]
    masked = (key - WINDOW > query) | (query > key)
    first = masked | ((np.arange(TILE)[:, None] < WINDOW) & (key < WINDOW))
    mask = np.where(np.stack([masked, first], 1), np.float32(-1e30), np.float32(0))
    half = np.arange(0, HEAD, 2, dtype=np.float32)
    inv_freq = (np.float32(1.0) / np.float32(10000.0) ** (half / np.float32(HEAD))).astype(np.float32)
    t = np.arange(T, dtype=np.float32)
    freqs = t[:, None] * inv_freq[None, :]
    base = (half + np.float32(0.4 * HEAD)) / np.float32(1.4 * HEAD)
    scale = base[None, :] ** ((t - T // 2) / np.float32(WINDOW // 2))[:, None]
    turn = np.zeros((2, T, 2, HEAD), np.float32)
    for n, size in ((0, 8.0 * scale), (1, 1.0 / scale)):
        turn[0, :, n] = np.tile(np.cos(freqs) * size, 2)
        turn[1, :, n] = np.concatenate([-np.sin(freqs) * size, np.sin(freqs) * size], 1)
    turn = turn.reshape(2, TILES, P, 2, HEAD).transpose(2, 0, 1, 3, 4)
    bf16 = mybir.dt.np(BF16)
    order = np.arange(E, 0, -1, dtype=np.float32)[None, :]
    index = np.arange(BLOCKS, dtype=np.float32)[None, :]
    going = np.ones((E, TOKEN_TILES), np.float32)
    going[:, 0] = 0.0
    return {"before": np.triu(np.ones((P, P), np.float32), 1), "index": index, "going": going.reshape(1, -1), "order": order, "eye16": eye.astype(bf16), "mask": mask.astype(bf16), "turn": turn, "ident": eye, "mean": mean, "centre": eye - mean, "pick": pick.astype(mybir.dt.np(BF16))}


def laid_out(i):
    def halves(v):
        return v.reshape(2, P, *v.shape[1:]).swapaxes(0, 1)

    x_proj = i["L1_attn_x_proj_w"].T
    dbc = np.zeros((2 * P, P), x_proj.dtype)
    dbc[:, 32:40] = x_proj[:, 0:8]
    for first in (0, 64, 96):
        dbc[:, first:first + 32] = x_proj[:, 8:40]
    fc2 = i["L1_attn_fc2_w"].T
    b1 = np.zeros((2, 2, 3 * P), i["L1_ffn_b1"].dtype)
    b1[:, :, 0:HID] = i["L1_ffn_b1"].reshape(2, 2, HID)
    return {
        "router_w": i["L0_ffn_router_w"],
        "router_b": i["L0_ffn_router_b"][None, :],
        "moe_w1": i["L0_ffn_W1"],
        "moe_w2": i["L0_ffn_W2"],
        "moe_b1": i["L0_ffn_b1"].reshape(8, 4, P).transpose(2, 0, 1),
        "moe_b2": i["L0_ffn_b2"][None],
        "wqkv": i["L1_ffn_wqkv"],
        "wo": i["L1_ffn_wo"],
        "q_scale": i["L1_ffn_q_scale"],
        "k_scale": i["L1_ffn_k_scale"],
        "ln_g": i["L1_ffn_ln_g"][:, :, None],
        "ln_b": i["L1_ffn_ln_b"][:, :, None],
        "w1": i["L1_ffn_w1"],
        "b1": b1.reshape(2, 2, 3, P).transpose(0, 3, 1, 2),
        "w2": i["L1_ffn_w2"],
        "b2": i["L1_ffn_b2"][:, :, None],
        "in_w": i["L1_attn_in_proj_w"].T,
        "dbc_w": halves(dbc),
        "dt_w": i["L1_attn_dt_proj_w"].T,
        "out_w": halves(i["L1_attn_out_proj_w"].T),
        "rms1": i["L1_attn_rms1_w"][:, None],
        "conv_w": halves(i["L1_attn_conv_w"]),
        "conv_b": halves(i["L1_attn_conv_b"]),
        "dt_b": halves(i["L1_attn_dt_proj_b"]),
        "skip": halves(i["L1_attn_D_skip"]),
        "a_log": halves(i["L1_attn_A_log"]),
        "rms2": i["L1_attn_rms2_w"][:, None],
        "fc1": i["L1_attn_fc1_w"].T.reshape(P, 2, P),
        "fc2": halves(fc2).reshape(P, 2, 2, P),
        "fc3": halves(i["L1_attn_fc3_w"].T),
        "mlp_b": np.concatenate([i["L1_attn_fc1_b"].reshape(2, P), i["L1_attn_fc2_b"].reshape(2, P),
                                 i["L1_attn_fc3_b"].reshape(1, P)]).T,
        "x": i["L0_attn_h"].reshape(ALL, P).T,
        "gru_w0": i["L0_attn_W0"],
        "gru_w1": i["L0_attn_W1"],
    }


def kernel(**inputs):
    import concourse.bacc as bacc
    from concourse.bass_utils import run_bass_kernel_spmd

    arrays = {k: np.ascontiguousarray(v) for k, v in laid_out({k: np.asarray(v) for k, v in inputs.items()}).items()}
    arrays.update(shape_constants())
    arrays = {f"in_{k}": v for k, v in arrays.items()}
    nc = bacc.Bacc("TRN2", target_bir_lowering=False, num_devices=1)
    dram = {k[3:]: nc.dram_tensor(k, v.shape, mybir.dt.from_np(v.dtype), kind="ExternalInput").ap()
            for k, v in arrays.items()}
    out = nc.dram_tensor("out_x", (P, ALL), F32, kind="ExternalOutput").ap()
    program(nc, dram, out)
    result = run_bass_kernel_spmd(nc, [arrays], core_ids=[0]).results[0]["out_x"]
    return np.ascontiguousarray(np.asarray(result).T).reshape(SEQS, T, P)
```

```python
from contextlib import ExitStack

import numpy as np

import concourse.bass as bass
from concourse import mybir

F32 = mybir.dt.float32
BF16 = mybir.dt.bfloat16
U32 = mybir.dt.uint32
ACT = mybir.ActivationFunctionType
ALU = mybir.AluOpType
AX_X = mybir.AxisListType.X

P = 128
SEQS = 4
T = 1024
CH = 512
CHUNKS = T // CH
ALL = SEQS * T
EPS_LN = 1e-5
EPS_RMS = 1e-6

PRIME = 2


def done(t):
    return t + 1 + PRIME


def freed(t):
    return t - 1 + PRIME


def cols(t, width=CH):
    return bass.ds(t * width, width)


def semaphores(ctx, nc, stage, names):
    made = [nc.alloc_semaphore(f"{stage}_{n}") for n in names.split()]
    ctx.callback(nc.clear_and_free_semaphores, made)
    return made


def load_constants(nc, mem, dram):
    with ExitStack() as ctx:
        (loaded,) = semaphores(ctx, nc, "init", "loaded")
        block = ctx.enter_context(nc.Block())

        @block.sync
        def _(sp):
            n = 0
            for name in ("centre", "mean", "ident"):
                sp.dma_start(mem[name][:], dram[name]).then_inc(loaded, 16)
                n += 16
            sp.dma_start(mem["x"][:], dram["x"]).then_inc(loaded, 16)
            sp.wait_ge(loaded, n + 16)


def min_gru(nc, mem, dram):
    x, centre, mean = mem["x"], mem["centre"], mem["mean"]
    with ExitStack() as ctx:
        def sb(name, shape, dt=F32):
            return ctx.enter_context(nc.sbuf_tensor(f"gru_{name}", shape, dt))

        w = sb("w", [P, 2, 3, P])
        square = sb("square", [P, 2, CH])
        log = sb("log", [P, 2, CH])
        rstd = sb("rstd", [P, 2, CH])
        h = [sb(f"h{n}", [P, 2, CH]) for n in range(3)]
        update = sb("update", [P, 2, CH])
        keep = sb("keep", [P, 2, CH])
        cand = sb("cand", [P, 2, CH])
        gate = sb("gate", [P, 2, CH])
        value = sb("value", [P, 2, CH])
        scan = sb("scan", [P, 2, 2, CH])
        mix = sb("mix", [P, 2, CH])
        bank = [ctx.enter_context(nc.psum_tensor(f"gru_bank{n}", [P, CH], F32)) for n in range(8)]
        centred, variance = bank[0:2], bank[2:4]
        (w_loaded, centred_ready, square_ready, variance_ready, log_ready, rstd_ready,
         h0_ready, x_done) = semaphores(
            ctx, nc, "gru", "w_loaded centred square variance log rstd normed x_done")
        gates_ready = semaphores(ctx, nc, "gru", "z0 z1")
        update_ready = semaphores(ctx, nc, "gru", "update0 update1")
        keep_ready = semaphores(ctx, nc, "gru", "keep0 keep1")
        cand_ready = semaphores(ctx, nc, "gru", "cand0 cand1")
        gate_ready = semaphores(ctx, nc, "gru", "gate0 gate1")
        (low_done, value_done, fed_done, scan_done, off_done, gated_done, h_done) = (
            semaphores(ctx, nc, "gru", f"{n}_0 {n}_1") for n in
            ("low", "value", "fed", "scan", "off", "gated", "h"))
        block = ctx.enter_context(nc.Block())

        @block.sync
        def _(sp):
            sp.dma_start(w[:, 0], dram["gru_w0"].rearrange("d (g n) -> d g n", g=3)).then_inc(w_loaded, 16)
            sp.dma_start(w[:, 1], dram["gru_w1"].rearrange("d (g n) -> d g n", g=3)).then_inc(w_loaded, 16)
            sp.wait_ge(w_loaded, 32)

        @block.tensor
        def _(pe):
            for s in [centred_ready, variance_ready] + gates_ready:
                pe.sem_inc(s, PRIME)
            pe.wait_ge(w_loaded, 32)
            with pe.Fori(0, SEQS) as b:
                for k in range(2):
                    t = b * 2 + k
                    pe.wait_ge(keep_ready[1], freed(t))
                    pe.wait_ge(h0_ready, freed(t))
                    nc.tensor.matmul(centred[k][:], centre[:], x[:, cols(t)], start=True, stop=True
                                     ).then_inc(centred_ready, 1)
                for k in range(2):
                    t = b * 2 + k
                    pe.wait_ge(square_ready, done(t))
                    pe.wait_ge(keep_ready[0], freed(t))
                    nc.tensor.matmul(variance[k][:], mean[:], square[:, k], start=True, stop=True
                                     ).then_inc(variance_ready, 1)
                for layer in range(2):
                    for k in range(2):
                        t = b * 2 + k
                        if layer == 0:
                            pe.wait_ge(h0_ready, done(t))
                            pe.wait_ge(fed_done[1], freed(t))
                            pe.wait_ge(gate_ready[1], freed(t))
                        else:
                            pe.wait_ge(h_done[0], done(t))
                            pe.wait_ge(fed_done[0], done(t))
                            pe.wait_ge(gate_ready[0], done(t))
                        for g, out in ((0, bank[4 + k]), (1, bank[6 + k]),
                                       (2, bank[2 + k] if layer == 0 else bank[k])):
                            last = nc.tensor.matmul(out[:], w[:, layer, g], h[layer][:, k],
                                                    start=True, stop=True)
                        last.then_inc(gates_ready[layer], 1)

        @block.scalar
        def _(act):
            for s in [square_ready, log_ready, rstd_ready] + update_ready + keep_ready + cand_ready + gate_ready:
                act.sem_inc(s, PRIME)
            with act.Fori(0, SEQS) as b:
                for k in range(2):
                    t = b * 2 + k
                    act.wait_ge(centred_ready, done(t))
                    nc.scalar.activation(square[:, k], centred[k][:], ACT.Square).then_inc(square_ready, 1)
                for k in range(2):
                    t = b * 2 + k
                    act.wait_ge(variance_ready, done(t))
                    nc.scalar.activation(log[:, k], variance[k][:], ACT.Ln, bias=EPS_LN).then_inc(log_ready, 1)
                for k in range(2):
                    t = b * 2 + k
                    act.wait_ge(log_ready, done(t))
                    act.wait_ge(h0_ready, freed(t))
                    nc.scalar.activation(rstd[:, k], log[:, k], ACT.Exp, scale=-0.5).then_inc(rstd_ready, 1)
                for layer in range(2):
                    for k in range(2):
                        t = b * 2 + k
                        act.wait_ge(gates_ready[layer], done(t))
                        if layer == 0:
                            act.wait_ge(h_done[1], freed(t))
                        else:
                            act.wait_ge(h_done[0], done(t))
                        nc.scalar.activation(cand[:, k], bank[4 + k][:], ACT.Sigmoid).then_inc(cand_ready[layer], 1)
                        nc.scalar.activation(update[:, k], bank[6 + k][:], ACT.Sigmoid).then_inc(update_ready[layer], 1)
                        nc.scalar.activation(gate[:, k], bank[6 + k][:], ACT.Sigmoid, scale=-1.0
                                             ).then_inc(gate_ready[layer], 1)
                        nc.scalar.activation(keep[:, k], (bank[2 + k] if layer == 0 else bank[k])[:], ACT.Sigmoid
                                             ).then_inc(keep_ready[layer], 1)

        @block.vector
        def _(dve):
            for s in ([h0_ready, x_done] + low_done + value_done + fed_done + scan_done + off_done
                      + gated_done + h_done):
                dve.sem_inc(s, PRIME)
            with dve.Fori(0, SEQS) as b:
                for k in range(2):
                    t = b * 2 + k
                    dve.wait_ge(rstd_ready, done(t))
                    dve.wait_ge(h_done[0], freed(t))
                    nc.vector.tensor_tensor(h[0][:, k], centred[k][:], rstd[:, k], ALU.mult).then_inc(h0_ready, 1)
                for layer in range(2):
                    for k in range(2):
                        t = b * 2 + k
                        hidden = bank[4 + k]
                        dve.wait_ge(cand_ready[layer], done(t))
                        nc.vector.tensor_scalar(cand[:, k], cand[:, k], 0.5, None, ALU.min
                                                ).then_inc(low_done[layer], 1)
                        dve.wait_ge(low_done[layer], done(t))
                        nc.vector.scalar_tensor_tensor(value[:, k], hidden[:], 0.0, cand[:, k],
                                                       ALU.max, ALU.add).then_inc(fed_done[layer], 1)
                        dve.wait_ge(fed_done[layer], done(t))
                        dve.wait_ge(update_ready[layer], done(t))
                        nc.vector.tensor_tensor(value[:, k], value[:, k], update[:, k], ALU.mult
                                                ).then_inc(value_done[layer], 1)
                        dve.wait_ge(value_done[layer], done(t))
                        dve.wait_ge(gate_ready[layer], done(t))
                        start = 0.0 if k == 0 else scan[:, layer, 0, CH - 1:CH]
                        if k == 1:
                            dve.wait_ge(scan_done[layer], done(t - 1))
                        nc.vector.tensor_tensor_scan(scan[:, layer, k], gate[:, k], value[:, k], start,
                                                     ALU.mult, ALU.add).then_inc(scan_done[layer], 1)
                        dve.wait_ge(scan_done[layer], done(t))
                        nc.vector.tensor_tensor(mix[:, k], scan[:, layer, k], h[layer][:, k], ALU.subtract
                                                ).then_inc(off_done[layer], 1)
                        dve.wait_ge(off_done[layer], done(t))
                        dve.wait_ge(keep_ready[layer], done(t))
                        nc.vector.tensor_tensor(mix[:, k], mix[:, k], keep[:, k], ALU.mult
                                                ).then_inc(gated_done[layer], 1)
                        dve.wait_ge(gated_done[layer], done(t))
                        nc.vector.tensor_tensor(h[layer + 1][:, k], mix[:, k], h[layer][:, k], ALU.add
                                                ).then_inc(h_done[layer], 1)
                for k in range(2):
                    t = b * 2 + k
                    dve.wait_ge(h_done[1], done(t))
                    nc.vector.tensor_tensor(x[:, cols(t)], x[:, cols(t)], h[2][:, k], ALU.add
                                            ).then_inc(x_done, 1)


MOE = ("weights_ready experts_ready cleared_tile cleared centred square variance log rstd normed logits biased best "
       "same preferred first chosen turned rows "
       "ranked totals totals_copied running ahead further blocks ends base based slot own_slot slots expert_no clipped "
       "block_expert scattered loaded0 loaded1 columns_turned columns picked up act down out stored0 stored1 "
       "back added")
E = 8
PARTS = 4
TOKEN_TILES = ALL // P
GROUP = 4
PAIRS = -(-(TOKEN_TILES + E - 1) // (2 * GROUP))
BLOCKS = PAIRS * 2 * GROUP


def experts(nc, mem, dram):
    x, centre, mean, ident = mem["x"], mem["centre"], mem["mean"], mem["ident"]
    with ExitStack() as ctx:
        def sb(name, shape, dt=F32):
            return ctx.enter_context(nc.sbuf_tensor(f"moe_{name}", shape, dt))

        router = sb("router", [P, E])
        router_b = sb("router_b", [P, E])
        order = sb("order", [P, E])
        before = sb("before", [P, P])
        index = sb("index", [P, BLOCKS])
        going = sb("going", [P, E * TOKEN_TILES])
        w1 = sb("w1", [P, E, PARTS * P])
        w2 = sb("w2", [P, E, PARTS * P])
        b1 = sb("b1", [P, E, PARTS])
        b2 = sb("b2", [1, E, P])
        zeros = sb("zeros", [P, GROUP * P])
        ones = sb("ones", [1, P])
        square = sb("square", [P, 2, CH])
        log = sb("log", [P, 2, CH])
        rstd = sb("rstd", [P, 2, CH])
        normed = sb("normed", [P, 2, CH])
        logits = sb("logits", [P, 2, 4, E])
        best = sb("best", [P, 2, 4])
        chosen = sb("chosen", [P, TOKEN_TILES, E])
        rows = sb("rows", [P, TOKEN_TILES, P])
        total = sb("total", [P, E, TOKEN_TILES])
        running = sb("running", [P, E, TOKEN_TILES])
        ahead = sb("ahead", [P, E, TOKEN_TILES])
        further = sb("further", [P, E, TOKEN_TILES])
        blocks = sb("blocks", [P, E])
        ends = sb("ends", [P, E])
        base = sb("base", [P, E])
        own_slot = sb("own_slot", [P, TOKEN_TILES])
        slots = sb("slots", [P, TOKEN_TILES], U32)
        passed = sb("passed", [1, BLOCKS, E])
        expert_no = sb("expert_no", [1, BLOCKS])
        block_expert = sb("block_expert", [1, BLOCKS], U32)
        slot_rows = sb("slot_rows", [P, 2, GROUP, P])
        columns = sb("columns", [P, 2, GROUP * P])
        w1_now = sb("w1_now", [P, 4, PARTS * P])
        w2_now = sb("w2_now", [P, 4, PARTS * P])
        b1_now = sb("b1_now", [P, 4, PARTS])
        b2_now = sb("b2_now", [1, 4, P])
        hidden = sb("hidden", [P, 2, PARTS, P])
        out_rows = sb("out_rows", [P, 2, GROUP, P])
        to_experts = nc.dram_tensor("moe_to_experts", (BLOCKS * P, P), F32, kind="Internal").ap()
        from_experts = nc.dram_tensor("moe_from_experts", (BLOCKS * P, P), F32, kind="Internal").ap()
        bank = [ctx.enter_context(nc.psum_tensor(f"moe_bank{n}", [P, CH], F32)) for n in range(8)]
        s = dict(zip(MOE.split(), semaphores(ctx, nc, "moe", MOE)))
        loaded, stored = (s["loaded0"], s["loaded1"]), (s["stored0"], s["stored1"])
        weights, expert_weights = semaphores(ctx, nc, "moe", "weights expert_weights")
        returned = semaphores(ctx, nc, "moe", " ".join(f"returned{n}" for n in range(2 * SEQS)))
        block = ctx.enter_context(nc.Block())

        def group_of(scratch, n):
            return scratch[n * GROUP * P:(n + 1) * GROUP * P].rearrange("(j p) d -> p j d", p=P)

        @block.sync
        def _(sp):
            first = [(router[:], dram["router_w"]), (router_b[:], dram["router_b"].partition_broadcast(P)),
                     (order[:], dram["order"].partition_broadcast(P)), (before[:], dram["before"]),
                     (index[:], dram["index"].partition_broadcast(P)),
                     (going[:], dram["going"].partition_broadcast(P))]
            for to, of in first:
                sp.dma_start(to, of).then_inc(weights, 16)
            sp.wait_ge(weights, 16 * len(first))
            sp.sem_inc(s["weights_ready"], 1)
            sp.wait_ge(s["cleared_tile"], 1)
            for n in range(2 * PAIRS):
                sp.dma_start(group_of(to_experts, n), zeros[:].rearrange("p (j d) -> p j d", j=GROUP)
                             ).then_inc(s["cleared"], 16)
            second = [(b1[:], dram["moe_b1"]), (b2[:], dram["moe_b2"])]
            for e in range(E):
                second += [(w1[:, e], dram["moe_w1"][e]),
                           (w2[:, e].rearrange("p (c n) -> p c n", n=P),
                            dram["moe_w2"][e].rearrange("(c p) n -> p c n", p=P))]
            for to, of in second:
                sp.dma_start(to, of).then_inc(expert_weights, 16)
            sp.wait_ge(expert_weights, 16 * len(second))
            sp.sem_inc(s["experts_ready"], 1)
            sp.wait_ge(s["scattered"], 16 * TOKEN_TILES)
            for n in range(2 * PAIRS + 2):
                if n < 2 * PAIRS:
                    if n >= 2:
                        sp.wait_ge(s["columns_turned"], n - 1 + PRIME)
                    sp.dma_start(slot_rows[:, n % 2], group_of(to_experts, n)).then_inc(loaded[n % 2], 16)
                if n >= 2:
                    sp.wait_ge(s["out"], n - 1 + PRIME)
                    sp.dma_start(group_of(from_experts, n - 2), out_rows[:, n % 2]).then_inc(stored[n % 2], 16)
            for n in range(2):
                sp.wait_ge(stored[n], 16 * (1 + PAIRS))

        @block.tensor
        def _(pe):
            for name in "centred variance logits turned columns_turned up down".split():
                pe.sem_inc(s[name], PRIME)
            pe.wait_ge(s["weights_ready"], 1)
            with pe.Fori(0, SEQS) as b:
                for k in range(2):
                    t = b * 2 + k
                    pe.wait_ge(s["normed"], freed(t))
                    nc.tensor.matmul(bank[k][:], centre[:], x[:, cols(t)], start=True, stop=True
                                     ).then_inc(s["centred"], 1)
                for k in range(2):
                    t = b * 2 + k
                    pe.wait_ge(s["square"], done(t))
                    nc.tensor.matmul(bank[2 + k][:], mean[:], square[:, k], start=True, stop=True
                                     ).then_inc(s["variance"], 1)
                for k in range(2):
                    t = b * 2 + k
                    pe.wait_ge(s["normed"], done(t))
                    pe.wait_ge(s["biased"], freed(t))
                    for j in range(4):
                        last = nc.tensor.matmul(bank[4 + k][:, j * E:(j + 1) * E], normed[:, k, j * P:(j + 1) * P],
                                                router[:], start=True, stop=True)
                    last.then_inc(s["logits"], 1)
                    pe.wait_ge(s["rows"], freed(t))
                    for j in range(4):
                        last = nc.tensor.transpose(bank[6 + k][:, j * P:(j + 1) * P],
                                                   normed[:, k, j * P:(j + 1) * P], ident[:])
                    last.then_inc(s["turned"], 1)
            pe.wait_ge(s["chosen"], done(2 * SEQS - 1))
            everyone = chosen[:].rearrange("p t e -> p (t e)")
            nc.tensor.matmul(bank[0][:, 0:TOKEN_TILES * E], before[:], everyone, start=True, stop=True
                             ).then_inc(s["ranked"], 1)
            nc.tensor.matmul(bank[1][:, 0:TOKEN_TILES * E], mean[:], everyone, start=True, stop=True
                             ).then_inc(s["totals"], 1)
            pe.wait_ge(s["slots"], 1)
            with pe.Fori(0, PAIRS) as b:
                for g in range(2):
                    n = b * 2 + g
                    pe.wait_ge(loaded[g], b * 16 + 16)
                    pe.wait_ge(s["columns"], freed(n))
                    for j in range(GROUP):
                        last = nc.tensor.transpose(bank[g][:, j * P:(j + 1) * P], slot_rows[:, g, j], ident[:])
                    last.then_inc(s["columns_turned"], 1)
                for m in range(2 * GROUP + 1):
                    if m < 2 * GROUP:
                        i = b * 2 * GROUP + m
                        g, j = divmod(m, GROUP)
                        if j == 0:
                            pe.wait_ge(s["columns"], done(b * 2 + g))
                        pe.wait_ge(s["picked"], done(i))
                        pe.wait_ge(s["act"], freed(i))
                        for c in range(PARTS):
                            last = nc.tensor.matmul(bank[2 + m % 2][:, c * P:(c + 1) * P],
                                                    w1_now[:, m % 4, c * P:(c + 1) * P],
                                                    columns[:, g, j * P:(j + 1) * P], start=True, stop=True)
                        last.then_inc(s["up"], 1)
                    if m >= 1:
                        i = b * 2 * GROUP + m - 1
                        g, j = divmod(m - 1, GROUP)
                        if j == 0:
                            pe.wait_ge(s["out"], freed(b * 2 + g))
                        pe.wait_ge(s["act"], done(i))
                        to = bank[4 + g][:, j * P:(j + 1) * P]
                        for c in range(PARTS):
                            nc.tensor.matmul(to, hidden[:, (m - 1) % 2, c], w2_now[:, (m - 1) % 4, c * P:(c + 1) * P],
                                             start=c == 0, stop=False)
                        nc.tensor.matmul(to, ones[:], b2_now[:, (m - 1) % 4], start=False, stop=True
                                         ).then_inc(s["down"], 1)
            for t in range(2 * SEQS):
                pe.wait_ge(returned[t], 16 * 4)
                if t >= 2:
                    pe.wait_ge(s["added"], t - 1)
                for j in range(4):
                    last = nc.tensor.transpose(bank[6 + t % 2][:, j * P:(j + 1) * P], rows[:, 4 * t + j], ident[:])
                last.then_inc(s["back"], 1)

        @block.scalar
        def _(act):
            for name in "square log rstd columns act out".split():
                act.sem_inc(s[name], PRIME)
            for n in range(2):
                act.sem_inc(stored[n], 16)
            act.preload_act_table_set("natural_log_exp_and_others")
            with act.Fori(0, SEQS) as b:
                for k in range(2):
                    t = b * 2 + k
                    act.wait_ge(s["centred"], done(t))
                    nc.scalar.activation(square[:, k], bank[k][:], ACT.Square).then_inc(s["square"], 1)
                for k in range(2):
                    t = b * 2 + k
                    act.wait_ge(s["variance"], done(t))
                    nc.scalar.activation(log[:, k], bank[2 + k][:], ACT.Ln, bias=EPS_LN).then_inc(s["log"], 1)
                for k in range(2):
                    t = b * 2 + k
                    act.wait_ge(s["log"], done(t))
                    act.wait_ge(s["normed"], freed(t))
                    nc.scalar.activation(rstd[:, k], log[:, k], ACT.Exp, scale=-0.5).then_inc(s["rstd"], 1)
            act.preload_act_table_set("gelu_and_others")
            with act.Fori(0, PAIRS) as b:
                def result(g):
                    act.wait_ge(s["down"], done(b * 2 * GROUP + g * GROUP + GROUP - 1))
                    act.wait_ge(stored[g], b * 16 + 16)
                    nc.scalar.activation(out_rows[:, g], bank[4 + g][:].rearrange("p (j d) -> p j d", j=GROUP),
                                         ACT.Copy).then_inc(s["out"], 1)

                for g in range(2):
                    act.wait_ge(s["columns_turned"], done(b * 2 + g))
                    nc.scalar.activation(columns[:, g], bank[g][:], ACT.Copy).then_inc(s["columns"], 1)
                for m in range(2 * GROUP):
                    i = b * 2 * GROUP + m
                    act.wait_ge(s["up"], done(i))
                    act.wait_ge(s["down"], freed(i))
                    for c in range(PARTS):
                        last = nc.scalar.activation(hidden[:, m % 2, c], bank[2 + m % 2][:, c * P:(c + 1) * P],
                                                    ACT.Gelu, bias=b1_now[:, m % 4, c:c + 1])
                    last.then_inc(s["act"], 1)
                    if m == GROUP + 1:
                        result(0)
                result(1)

        @block.gpsimd
        def _(pool):
            pool.wait_ge(s["slots"], 1)
            pool.wait_ge(s["cleared"], 16 * 2 * PAIRS)
            pool.wait_ge(s["rows"], done(2 * SEQS - 1))
            for n in range(TOKEN_TILES):
                nc.gpsimd.indirect_dma_start(to_experts, bass.IndirectOffsetOnAxis(slots[:, n:n + 1], 0),
                                             rows[:, n], None).then_inc(s["scattered"], 16)
            pool.wait_ge(s["scattered"], 16 * TOKEN_TILES)
            for n in range(2):
                pool.wait_ge(stored[n], 16 * (1 + PAIRS))
            for n in range(TOKEN_TILES):
                nc.gpsimd.indirect_dma_start(rows[:, n], None, from_experts,
                                             bass.IndirectOffsetOnAxis(slots[:, n:n + 1], 0)
                                             ).then_inc(returned[n // 4], 16)

        @block.vector
        def _(dve):
            for name in "normed biased best same preferred first chosen rows picked".split():
                dve.sem_inc(s[name], PRIME)
            nc.vector.memset(ones[:], 1.0)
            nc.vector.memset(zeros[:], 0.0).then_inc(s["cleared_tile"], 1)
            dve.wait_ge(s["weights_ready"], 1)
            with dve.Fori(0, SEQS) as b:
                for k in range(2):
                    t = b * 2 + k
                    dve.wait_ge(s["rstd"], done(t))
                    dve.wait_ge(s["turned"], freed(t))
                    nc.vector.tensor_tensor(normed[:, k], bank[k][:], rstd[:, k], ALU.mult).then_inc(s["normed"], 1)
                for k in range(2):
                    t = b * 2 + k
                    dve.wait_ge(s["logits"], done(t))
                    nc.vector.tensor_tensor(logits[:, k], bank[4 + k][:, 0:4 * E].rearrange("p (j e) -> p j e", e=E),
                                            router_b[:].unsqueeze(1).broadcast_to([P, 4, E]), ALU.add
                                            ).then_inc(s["biased"], 1)
                for k in range(2):
                    t = b * 2 + k
                    dve.wait_ge(s["biased"], done(t))
                    nc.vector.tensor_reduce(best[:, k], logits[:, k], AX_X, ALU.max).then_inc(s["best"], 1)
                for k in range(2):
                    t = b * 2 + k
                    dve.wait_ge(s["best"], done(t))
                    nc.vector.tensor_tensor(logits[:, k], logits[:, k], best[:, k].unsqueeze(2).broadcast_to([P, 4, E]),
                                            ALU.is_equal).then_inc(s["same"], 1)
                for k in range(2):
                    t = b * 2 + k
                    dve.wait_ge(s["same"], done(t))
                    nc.vector.tensor_tensor(logits[:, k], logits[:, k],
                                            order[:].unsqueeze(1).broadcast_to([P, 4, E]), ALU.mult
                                            ).then_inc(s["preferred"], 1)
                for k in range(2):
                    t = b * 2 + k
                    dve.wait_ge(s["preferred"], done(t))
                    nc.vector.tensor_reduce(best[:, k], logits[:, k], AX_X, ALU.max).then_inc(s["first"], 1)
                for k in range(2):
                    t = b * 2 + k
                    dve.wait_ge(s["first"], done(t))
                    nc.vector.tensor_tensor(chosen[:, bass.ds(t * 4, 4)], logits[:, k],
                                            best[:, k].unsqueeze(2).broadcast_to([P, 4, E]), ALU.is_equal
                                            ).then_inc(s["chosen"], 1)
                for k in range(2):
                    t = b * 2 + k
                    dve.wait_ge(s["turned"], done(t))
                    nc.vector.tensor_scalar(rows[:, bass.ds(t * 4, 4)],
                                            bank[6 + k][:].rearrange("p (j d) -> p j d", j=4), 1.0, None, ALU.mult
                                            ).then_inc(s["rows"], 1)

            def by_expert(ap):
                return ap.rearrange("p (t e) -> p e t", e=E)

            def flat(ap):
                return ap[:].rearrange("p e t -> p (e t)")

            dve.wait_ge(s["totals"], 1)
            nc.vector.tensor_copy(total[:], by_expert(bank[1][:, 0:TOKEN_TILES * E])).then_inc(s["totals_copied"], 1)
            dve.wait_ge(s["totals_copied"], 1)
            nc.vector.tensor_tensor_scan(flat(running), going[:], flat(total), 0.0, ALU.mult, ALU.add
                                         ).then_inc(s["running"], 1)
            dve.wait_ge(s["running"], 1)
            nc.vector.tensor_tensor(ahead[:], running[:], total[:], ALU.subtract).then_inc(s["ahead"], 1)
            nc.vector.tensor_tensor(further[:], running[:, :, TOKEN_TILES - 1:].broadcast_to([P, E, TOKEN_TILES]),
                                    index[:, 0:TOKEN_TILES].unsqueeze(1).broadcast_to([P, E, TOKEN_TILES]), ALU.is_gt
                                    ).then_inc(s["further"], 1)
            dve.wait_ge(s["further"], 1)
            nc.vector.tensor_reduce(blocks[:], further[:], AX_X, ALU.add).then_inc(s["blocks"], 1)
            dve.wait_ge(s["blocks"], 1)
            nc.vector.tensor_tensor_scan(ends[:], going[:, 1:1 + E], blocks[:], 0.0, ALU.mult, ALU.add
                                         ).then_inc(s["ends"], 1)
            dve.wait_ge(s["ends"], 1)
            nc.vector.tensor_tensor(base[:], ends[:], blocks[:], ALU.subtract).then_inc(s["base"], 1)
            dve.wait_ge(s["base"], 1)
            dve.wait_ge(s["ahead"], 1)
            nc.vector.tensor_tensor(ahead[:], ahead[:], base[:].unsqueeze(2).broadcast_to([P, E, TOKEN_TILES]),
                                    ALU.add).then_inc(s["based"], 1)
            dve.wait_ge(s["based"], 1)
            dve.wait_ge(s["ranked"], 1)
            nc.vector.scalar_tensor_tensor(ahead[:], ahead[:], float(P), by_expert(bank[0][:, 0:TOKEN_TILES * E]),
                                           ALU.mult, ALU.add).then_inc(s["slot"], 1)
            dve.wait_ge(s["slot"], 1)
            nc.vector.tensor_tensor(ahead[:], ahead[:], chosen[:].rearrange("p t e -> p e t"), ALU.mult
                                    ).then_inc(s["slot"], 1)
            dve.wait_ge(s["slot"], 2)
            nc.vector.tensor_reduce(own_slot[:], ahead[:].rearrange("p e t -> p t e"), AX_X, ALU.add
                                    ).then_inc(s["own_slot"], 1)
            dve.wait_ge(s["own_slot"], 1)
            nc.vector.tensor_copy(slots[:], own_slot[:]).then_inc(s["slots"], 1)
            nc.vector.tensor_tensor(passed[:], index[0:1].unsqueeze(2).broadcast_to([1, BLOCKS, E]),
                                    ends[0:1].unsqueeze(1).broadcast_to([1, BLOCKS, E]), ALU.is_ge
                                    ).then_inc(s["expert_no"], 1)
            dve.wait_ge(s["expert_no"], 1)
            nc.vector.tensor_reduce(expert_no[:], passed[:], AX_X, ALU.add).then_inc(s["expert_no"], 1)
            dve.wait_ge(s["expert_no"], 2)
            nc.vector.tensor_scalar(expert_no[:], expert_no[:], float(E - 1), None, ALU.min
                                    ).then_inc(s["clipped"], 1)
            dve.wait_ge(s["clipped"], 1)
            nc.vector.tensor_copy(block_expert[:], expert_no[:]).then_inc(s["block_expert"], 1)
            dve.wait_ge(s["block_expert"], 1)
            dve.wait_ge(s["experts_ready"], 1)
            with dve.Fori(0, PAIRS) as b:
                for m in range(2 * GROUP):
                    i = b * 2 * GROUP + m
                    half = m % 4
                    dve.wait_ge(s["up"], freed(i))
                    e = dve.value_load(block_expert[0:1, bass.ds(i, 1)], min_val=0, max_val=E - 1)
                    nc.vector.tensor_copy(w1_now[:, half], w1[:, bass.ds(e, 1)])
                    nc.vector.tensor_copy(b1_now[:, half], b1[:, bass.ds(e, 1)])
                    nc.vector.tensor_copy(b2_now[:, half], b2[:, bass.ds(e, 1)])
                    nc.vector.tensor_copy(w2_now[:, half], w2[:, bass.ds(e, 1)]).then_inc(s["picked"], 1)
            for t in range(2 * SEQS):
                dve.wait_ge(s["back"], t + 1)
                nc.vector.tensor_tensor(x[:, t * CH:(t + 1) * CH], x[:, t * CH:(t + 1) * CH], bank[6 + t % 2][:],
                                        ALU.add).then_inc(s["added"], 1)


SSM = ("weights_ready folded zeroed decay decay_ready centred square variance log rstd x0 uz raw tap z conv0 conv1 "
       "conv u dbc dt_low hi rest1 mid rest2 parts dtraw size small over dtlog dt dtu b c b_all da dbu "
       "state carried seen y summed gated out branch")


def mamba(nc, mem, dram):
    x, centre, mean, ident = mem["x"], mem["centre"], mem["mean"], mem["ident"]
    branch = mem["branch"]
    STATES = 16
    STEPS = 2 * STATES
    with ExitStack() as ctx:
        def sb(name, shape, dt=F32):
            return ctx.enter_context(nc.sbuf_tensor(f"ssm_{name}", shape, dt))

        in_w = sb("in_w", [P, 4 * P])
        dbc_w = sb("dbc_w", [P, 2, P])
        dt_w = sb("dt_w", [40, 2 * P])
        out_w = sb("out_w", [P, 2, P])
        pick = sb("pick", [P, 2 * STATES, P], BF16)
        rms_w = sb("rms_w", [P, 1])
        conv_w = sb("conv_w", [P, 2, 4])
        conv_b = sb("conv_b", [P, 2])
        dt_b = sb("dt_b", [P, 2])
        skip = sb("skip", [P, 2])
        a_log = sb("a_log", [P, 2, STATES])
        decay = sb("decay", [P, 2, STATES])
        u = sb("u", [P, 2, ALL])
        z = sb("z", [P, 2, ALL])
        dt = sb("dt", [P, 2, ALL])
        parts = sb("parts", [P, ALL], BF16)
        x0 = dt[:, 0]
        dtu = sb("dtu", [P, 2, 2, CH])
        b_all = sb("b_all", [P, 2, CH])
        da = sb("da", [P, 2, 2, CH])
        dbu = sb("dbu", [P, 2, 2, CH])
        state = sb("state", [P, 2, 2, CH])
        carry = sb("carry", [P, STATES, 2])
        shared = sb("shared", [P, 2, 4 * CH])
        seen = shared[:, 0].rearrange("p (a h c) -> p a h c", a=2, h=2)
        y = shared[:, 1].rearrange("p (a h c) -> p a h c", a=2, h=2)
        square = b_all
        log = da
        rstd = dbu
        raw = shared[:, :, 0:3 + T]
        conv = state
        dt_low = b_all[32:64]
        rest = dtu[:, 0]
        size = seen
        bank = [ctx.enter_context(nc.psum_tensor(f"ssm_bank{n}", [P, CH], F32)) for n in range(8)]
        s = dict(zip(SSM.split(), semaphores(ctx, nc, "ssm", SSM)))
        weights = semaphores(ctx, nc, "ssm", "weights")[0]
        block = ctx.enter_context(nc.Block())

        @block.sync
        def _(sp):
            loads = [(in_w[:], "in_w"), (dbc_w[:], "dbc_w"), (dt_w[32:40], "dt_w"), (out_w[:], "out_w"),
                     (pick[:], "pick"), (rms_w[:], "rms1"), (conv_w[:], "conv_w"), (conv_b[:], "conv_b"),
                     (dt_b[:], "dt_b"), (skip[:], "skip"), (a_log[:], "a_log")]
            for to, name in loads:
                sp.dma_start(to, dram[name]).then_inc(weights, 16)
            sp.wait_ge(weights, 16 * len(loads))
            sp.sem_inc(s["weights_ready"], 1)

        @block.tensor
        def _(pe):
            for name in "centred variance uz dbc dtraw b c y out".split():
                pe.sem_inc(s[name], PRIME)
            with pe.Fori(0, SEQS) as b:
                for k in range(2):
                    t = b * 2 + k
                    pe.wait_ge(s["x0"], freed(t))
                    nc.tensor.matmul(bank[k][:], centre[:], x[:, cols(t)], start=True, stop=True
                                     ).then_inc(s["centred"], 1)
                for k in range(2):
                    t = b * 2 + k
                    pe.wait_ge(s["square"], done(t))
                    nc.tensor.matmul(bank[2 + k][:], mean[:], square[:, k], start=True, stop=True
                                     ).then_inc(s["variance"], 1)
            pe.wait_ge(s["folded"], 1)
            pe.wait_ge(s["x0"], done(2 * SEQS - 1))
            with pe.Fori(0, SEQS) as b:
                for k in range(2):
                    t = b * 2 + k
                    pe.wait_ge(s["z"], freed(t))
                    for m in range(4):
                        last = nc.tensor.matmul(bank[4 * k + m][:], in_w[:, m * P:(m + 1) * P], x0[:, cols(t)],
                                                start=True, stop=True)
                    last.then_inc(s["uz"], 1)
            pe.wait_ge(s["z"], done(2 * SEQS - 1))
            pe.wait_ge(s["u"], done(2 * SEQS - 1))
            with pe.Fori(0, SEQS) as b:
                for k in range(2):
                    t = b * 2 + k
                    pe.wait_ge(s["rest1"], freed(t))
                    for half in range(2):
                        last = nc.tensor.matmul(bank[k][:], dbc_w[:, half], u[:, half, cols(t)],
                                                start=half == 0, stop=half == 1)
                    last.then_inc(s["dbc"], 1)
                for k in range(2):
                    t = b * 2 + k
                    pe.wait_ge(s["dt_low"], done(t))
                    pe.wait_ge(s["dt"], freed(t))
                    for half in range(2):
                        last = nc.tensor.matmul(bank[2 + 2 * k + half][:], dt_w[32:40, half * P:(half + 1) * P],
                                                dt_low[:, k][0:8], start=True, stop=True)
                    last.then_inc(s["dtraw"], 1)
            pe.wait_ge(s["parts"], done(2 * SEQS - 1))
            pe.wait_ge(s["dt"], done(2 * SEQS - 1))
            with pe.Fori(0, SEQS) as b:
                for m in range(STEPS + 3):
                    if m < STEPS:
                        i = b * STEPS + m
                        pe.wait_ge(s["b_all"], freed(i))
                        nc.tensor.matmul(bank[m % 2][:], pick[:, m % STATES], parts[:, cols(b * 2 + m // STATES)],
                                         start=True, stop=True).then_inc(s["b"], 1)
                    if 1 <= m <= STEPS:
                        i = b * STEPS + m - 1
                        pe.wait_ge(s["seen"], freed(i))
                        nc.tensor.matmul(bank[2 + (m - 1) % 2][:], pick[:, STATES + (m - 1) % STATES],
                                         parts[:, cols(b * 2 + (m - 1) // STATES)],
                                         start=True, stop=True).then_inc(s["c"], 1)
                    if m >= 3:
                        k, n = divmod(m - 3, STATES)
                        pe.wait_ge(s["seen"], done(b * STEPS + m - 3))
                        if n == 0:
                            pe.wait_ge(s["branch"], freed(b * 2 + k))
                        for half in range(2):
                            last = nc.tensor.matmul(bank[4 + 2 * k + half][:], ident[:], seen[:, n % 2, half],
                                                    start=n == 0, stop=n == STATES - 1)
                        last.then_inc(s["y"], 1)
                    for k in range(2):
                        if m == (STATES + 6 if k == 0 else STEPS + 2):
                            pe.wait_ge(s["gated"], done(b * 2 + k))
                            for half in range(2):
                                last = nc.tensor.matmul(bank[4 + 2 * k][:], out_w[:, half], y[:, k, half],
                                                        start=half == 0, stop=half == 1)
                            last.then_inc(s["out"], 1)

        @block.scalar
        def _(act):
            for name in "square log rstd raw tap z u dt_low hi size small dtlog b_all da".split():
                act.sem_inc(s[name], PRIME)
            act.preload_act_table_set("natural_log_exp_and_others")
            act.wait_ge(s["weights_ready"], 1)
            nc.scalar.activation(decay[:], a_log[:], ACT.Exp).then_inc(s["decay"], 1)
            with act.Fori(0, SEQS) as b:
                for k in range(2):
                    t = b * 2 + k
                    act.wait_ge(s["centred"], done(t))
                    nc.scalar.activation(square[:, k], bank[k][:], ACT.Square).then_inc(s["square"], 1)
                for k in range(2):
                    t = b * 2 + k
                    act.wait_ge(s["variance"], done(t))
                    nc.scalar.activation(log[:, k, 0], bank[2 + k][:], ACT.Ln, bias=EPS_LN)
                    nc.scalar.activation(log[:, k, 1], bank[2 + k][:], ACT.Ln, scale=1.0 + EPS_RMS,
                                         bias=EPS_RMS * EPS_LN).then_inc(s["log"], 1)
                for k in range(2):
                    t = b * 2 + k
                    act.wait_ge(s["log"], done(t))
                    act.wait_ge(s["x0"], freed(t))
                    nc.scalar.activation(rstd[:, k], log[:, k], ACT.Exp, scale=-0.5).then_inc(s["rstd"], 1)
            act.preload_act_table_set("silu_and_others")
            act.wait_ge(s["zeroed"], 1)
            with act.Fori(0, SEQS) as b:
                for k in range(2):
                    t = b * 2 + k
                    act.wait_ge(s["uz"], done(t))
                    act.wait_ge(s["conv"], freed(t + 1 - k))
                    for half in range(2):
                        last = nc.scalar.activation(raw[:, half, 3 + k * CH:3 + (k + 1) * CH],
                                                    bank[4 * k + half][:], ACT.Copy)
                    last.then_inc(s["raw"], 1)
                    act.wait_ge(s["u"], freed(t))
                    for half in range(2):
                        last = nc.scalar.activation(conv[:, k, half], bank[4 * k + half][:], ACT.Identity,
                                                    scale=conv_w[:, half, 3:4], bias=conv_b[:, half:half + 1])
                    last.then_inc(s["tap"], 1)
                    for half in range(2):
                        last = nc.scalar.activation(z[:, half, cols(t)], bank[4 * k + 2 + half][:], ACT.Silu)
                    last.then_inc(s["z"], 1)
                for k in range(2):
                    t = b * 2 + k
                    act.wait_ge(s["conv"], done(t))
                    act.wait_ge(s["zeroed"], 1)
                    for half in range(2):
                        last = nc.scalar.activation(u[:, half, cols(t)], conv[:, k, half], ACT.Silu)
                    last.then_inc(s["u"], 1)
            act.preload_act_table_set("natural_log_exp_and_others")
            with act.Fori(0, SEQS) as b:
                for k in range(2):
                    t = b * 2 + k
                    act.wait_ge(s["dbc"], done(t))
                    act.wait_ge(s["dtraw"], freed(t))
                    nc.scalar.activation(dt_low[:, k], bank[k][32:64, :], ACT.Copy).then_inc(s["dt_low"], 1)
                    nc.scalar.activation(parts[:, cols(t)], bank[k][:], ACT.Copy).then_inc(s["hi"], 1)
                for k in range(2):
                    t = b * 2 + k
                    act.wait_ge(s["dtraw"], done(t))
                    act.wait_ge(s["dt"], freed(t))
                    for half in range(2):
                        last = nc.scalar.activation(size[:, k, half], bank[2 + 2 * k + half][:], ACT.Abs,
                                                    bias=dt_b[:, half:half + 1])
                    last.then_inc(s["size"], 1)
                    act.wait_ge(s["size"], done(t))
                    nc.scalar.activation(size[:, k], size[:, k], ACT.Exp, scale=-1.0).then_inc(s["small"], 1)
                    act.wait_ge(s["small"], done(t))
                    nc.scalar.activation(size[:, k], size[:, k], ACT.Ln, bias=1.0).then_inc(s["dtlog"], 1)
            act.wait_ge(s["decay_ready"], 1)
            act.wait_ge(s["dtraw"], done(2 * SEQS - 1))
            with act.Fori(0, SEQS) as b:
                for m in range(STEPS):
                    i = b * STEPS + m
                    k, n = divmod(m, STATES)
                    act.wait_ge(s["b"], done(i))
                    act.wait_ge(s["dbu"], freed(i))
                    act.wait_ge(s["state"], freed(i))
                    nc.scalar.activation(b_all[:, m % 2], bank[m % 2][:], ACT.Copy).then_inc(s["b_all"], 1)
                    for half in range(2):
                        last = nc.scalar.activation(da[:, n % 2, half], dt[:, half, cols(b * 2 + k)],
                                                    ACT.Exp, scale=decay[:, half, n:n + 1])
                    last.then_inc(s["da"], 1)

        @block.gpsimd
        def _(pool):
            for name in "dtu dbu".split():
                pool.sem_inc(s[name], PRIME)
            pool.wait_ge(s["parts"], done(2 * SEQS - 1))
            pool.wait_ge(s["dt"], done(2 * SEQS - 1))
            with pool.Fori(0, SEQS) as b:
                def increments(k):
                    t = b * 2 + k
                    nc.gpsimd.tensor_tensor(dtu[:, k], dt[:, :, cols(t)], u[:, :, cols(t)], ALU.mult
                                            ).then_inc(s["dtu"], 1)

                pool.wait_ge(s["dbu"], freed(b * STEPS + 1))
                increments(0)
                for m in range(STEPS):
                    i = b * STEPS + m
                    k, n = divmod(m, STATES)
                    if n == 0:
                        pool.wait_ge(s["dtu"], done(b * 2 + k))
                    if m == STATES // 2:
                        increments(1)
                    pool.wait_ge(s["b_all"], done(i))
                    pool.wait_ge(s["state"], freed(i))
                    nc.gpsimd.tensor_tensor(dbu[:, n % 2], dtu[:, k],
                                            b_all[:, n % 2:n % 2 + 1, :].broadcast_to([P, 2, CH]), ALU.mult
                                            ).then_inc(s["dbu"], 1)

        @block.vector
        def _(dve):
            for name in ("x0 conv0 conv1 conv rest1 mid rest2 parts over dt state carried seen "
                         "summed gated branch").split():
                dve.sem_inc(s[name], PRIME)
            nc.vector.memset(raw[:, :, 0:3], 0.0).then_inc(s["zeroed"], 1)
            dve.wait_ge(s["weights_ready"], 1)
            nc.vector.tensor_scalar(in_w[:], in_w[:], rms_w[:, 0:1], None, ALU.mult).then_inc(s["folded"], 1)
            dve.wait_ge(s["decay"], 1)
            nc.vector.tensor_scalar(decay[:], decay[:], -1.0, None, ALU.mult).then_inc(s["decay_ready"], 1)
            with dve.Fori(0, SEQS) as b:
                for k in range(2):
                    t = b * 2 + k
                    dve.wait_ge(s["rstd"], done(t))
                    nc.vector.tensor_tensor(branch[:, cols(t)], bank[k][:], rstd[:, k, 0], ALU.mult)
                    nc.vector.tensor_tensor(x0[:, cols(t)], bank[k][:], rstd[:, k, 1], ALU.mult
                                            ).then_inc(s["x0"], 1)
            with dve.Fori(0, SEQS) as b:
                for k in range(2):
                    t = b * 2 + k
                    dve.wait_ge(s["tap"], done(t))
                    for tap, finished in ((2, "conv0"), (1, "conv1"), (0, "conv")):
                        for half in range(2):
                            at = raw[:, half, k * CH + tap:k * CH + tap + CH]
                            last = nc.vector.scalar_tensor_tensor(conv[:, k, half], at,
                                                                  conv_w[:, half, tap:tap + 1],
                                                                  conv[:, k, half], ALU.mult, ALU.add)
                        last.then_inc(s[finished], 1)
                        if tap:
                            dve.wait_ge(s[finished], done(t))
            with dve.Fori(0, SEQS) as b:
                for k in range(2):
                    t = b * 2 + k
                    dve.wait_ge(s["hi"], done(t))
                    nc.vector.tensor_tensor(rest[64:128, k], bank[k][64:128, :], parts[64:128, cols(t)], ALU.subtract
                                            ).then_inc(s["rest1"], 1)
                    dve.wait_ge(s["rest1"], done(t))
                    nc.vector.tensor_scalar(parts[64:128, cols(t)], rest[64:128, k], 1.0, None, ALU.mult).then_inc(s["mid"], 1)
                    dve.wait_ge(s["mid"], done(t))
                    nc.vector.tensor_tensor(rest[96:128, k], rest[96:128, k], parts[96:128, cols(t)], ALU.subtract
                                            ).then_inc(s["rest2"], 1)
                    dve.wait_ge(s["rest2"], done(t))
                    nc.vector.tensor_scalar(parts[96:128, cols(t)], rest[96:128, k], 1.0, None, ALU.mult).then_inc(s["parts"], 1)
                for k in range(2):
                    t = b * 2 + k
                    dve.wait_ge(s["size"], done(t))
                    for half in range(2):
                        last = nc.vector.tensor_scalar(dt[:, half, cols(t)], bank[2 + 2 * k + half][:],
                                                       dt_b[:, half:half + 1], 0.0, ALU.add, ALU.max)
                    last.then_inc(s["over"], 1)
                    dve.wait_ge(s["over"], done(t))
                    dve.wait_ge(s["dtlog"], done(t))
                    nc.vector.tensor_tensor(dt[:, :, cols(t)], dt[:, :, cols(t)], size[:, k], ALU.add
                                            ).then_inc(s["dt"], 1)
            with dve.Fori(0, SEQS) as b:
                def chunk_end(k):
                    t = b * 2 + k
                    dve.wait_ge(s["y"], done(b * STEPS + k * STATES + STATES - 1))
                    for half in range(2):
                        nc.vector.scalar_tensor_tensor(y[:, k, half], u[:, half, cols(t)], skip[:, half:half + 1],
                                                       bank[4 + 2 * k + half][:], ALU.mult, ALU.add
                                                       ).then_inc(s["summed"], 1)
                        dve.wait_ge(s["summed"], done(t * 2 + half))
                        last = nc.vector.tensor_tensor(y[:, k, half], y[:, k, half], z[:, half, cols(t)], ALU.mult)
                    last.then_inc(s["gated"], 1)

                def projected(k):
                    t = b * 2 + k
                    dve.wait_ge(s["out"], done(t))
                    nc.vector.tensor_tensor(branch[:, cols(t)], branch[:, cols(t)], bank[4 + 2 * k][:], ALU.add
                                            ).then_inc(s["branch"], 1)

                for m in range(STEPS):
                    k, n = divmod(m, STATES)
                    i = b * STEPS + m
                    if m == STATES + 4:
                        chunk_end(0)
                    if m == STATES + 8:
                        projected(0)
                    dve.wait_ge(s["da"], done(i))
                    dve.wait_ge(s["dbu"], done(i))
                    if k == 1:
                        dve.wait_ge(s["carried"], b * STATES + n + 1 + PRIME)
                    for half in range(2):
                        start = 0.0 if k == 0 else carry[:, n, half:half + 1]
                        last = nc.vector.tensor_tensor_scan(state[:, n % 2, half], da[:, n % 2, half],
                                                            dbu[:, n % 2, half], start, ALU.mult, ALU.add)
                    last.then_inc(s["state"], 1)
                    dve.wait_ge(s["state"], done(i))
                    dve.wait_ge(s["c"], done(i))
                    dve.wait_ge(s["y"], freed(i))
                    nc.vector.tensor_tensor(seen[:, n % 2], state[:, n % 2],
                                            bank[2 + n % 2][:].unsqueeze(1).broadcast_to([P, 2, CH]),
                                            ALU.mult).then_inc(s["seen"], 1)
                    if k == 0:
                        nc.vector.tensor_copy(carry[:, n], state[:, n % 2, :, CH - 1]).then_inc(s["carried"], 1)
                chunk_end(1)
                projected(1)


def mlp(nc, mem, dram):
    x, mean, branch = mem["x"], mem["mean"], mem["branch"]
    with ExitStack() as ctx:
        def sb(name, shape, dt=F32):
            return ctx.enter_context(nc.sbuf_tensor(f"mlp_{name}", shape, dt))

        fc1 = sb("fc1", [P, 2, P])
        fc2 = sb("fc2", [P, 2, 2, P])
        fc3 = sb("fc3", [P, 2, P])
        rms_w = sb("rms_w", [P, 1])
        bias = sb("bias", [P, 5])
        square = sb("square", [P, 2, CH])
        log = sb("log", [P, 2, CH])
        rstd = sb("rstd", [P, 2, CH])
        normed = sb("normed", [P, 2, CH])
        hidden = [sb(f"hidden{n}", [P, 2, 2, CH]) for n in range(2)]
        bank = [ctx.enter_context(nc.psum_tensor(f"mlp_bank{n}", [P, CH], F32)) for n in range(8)]
        (weights, folded, sq, power, lg, rs, nm, up, act1, mid, act2, down, first, xd) = semaphores(
            ctx, nc, "mlp", "weights folded square power log rstd normed up hidden0 mid hidden1 down first x")
        block = ctx.enter_context(nc.Block())

        @block.sync
        def _(sp):
            for to, name in ((fc1[:], "fc1"), (fc2[:], "fc2"), (fc3[:], "fc3"), (rms_w[:], "rms2"), (bias[:], "mlp_b")):
                sp.dma_start(to, dram[name]).then_inc(weights, 16)
            sp.wait_ge(weights, 80)

        @block.tensor
        def _(pe):
            for n in (power, up, mid, down):
                pe.sem_inc(n, PRIME)
            pe.wait_ge(folded, 1)
            with pe.Fori(0, SEQS) as b:
                for k in range(2):
                    t = b * 2 + k
                    pe.wait_ge(sq, done(t))
                    pe.wait_ge(xd, freed(t))
                    nc.tensor.matmul(bank[k][:], mean[:], square[:, k], start=True, stop=True).then_inc(power, 1)
                for k in range(2):
                    t = b * 2 + k
                    pe.wait_ge(nm, done(t))
                    pe.wait_ge(act2, freed(t))
                    for m in range(2):
                        last = nc.tensor.matmul(bank[2 + 2 * k + m][:], fc1[:, m], normed[:, k], start=True, stop=True)
                    last.then_inc(up, 1)
                for k in range(2):
                    t = b * 2 + k
                    pe.wait_ge(act1, done(t))
                    for m in range(2):
                        for c in range(2):
                            last = nc.tensor.matmul(bank[2 + 2 * k + m][:], fc2[:, c, m], hidden[0][:, k, c],
                                                    start=c == 0, stop=c == 1)
                    last.then_inc(mid, 1)
                for k in range(2):
                    t = b * 2 + k
                    pe.wait_ge(act2, done(t))
                    for c in range(2):
                        last = nc.tensor.matmul(bank[k][:], fc3[:, c], hidden[1][:, k, c], start=c == 0, stop=c == 1)
                    last.then_inc(down, 1)

        @block.scalar
        def _(act):
            for n in (sq, lg, rs, act1, act2):
                act.sem_inc(n, PRIME)
            act.wait_ge(weights, 80)
            with act.Fori(0, SEQS) as b:
                for k in range(2):
                    t = b * 2 + k
                    nc.scalar.activation(square[:, k], branch[:, cols(t)], ACT.Square).then_inc(sq, 1)
                for k in range(2):
                    t = b * 2 + k
                    act.wait_ge(power, done(t))
                    nc.scalar.activation(log[:, k], bank[k][:], ACT.Ln, bias=EPS_RMS).then_inc(lg, 1)
                for k in range(2):
                    t = b * 2 + k
                    act.wait_ge(lg, done(t))
                    act.wait_ge(nm, freed(t))
                    nc.scalar.activation(rstd[:, k], log[:, k], ACT.Exp, scale=-0.5).then_inc(rs, 1)
                for k in range(2):
                    t = b * 2 + k
                    act.wait_ge(up, done(t))
                    for m in range(2):
                        last = nc.scalar.activation(hidden[0][:, k, m], bank[2 + 2 * k + m][:], ACT.Relu,
                                                    bias=bias[:, m:m + 1])
                    last.then_inc(act1, 1)
                for k in range(2):
                    t = b * 2 + k
                    act.wait_ge(mid, done(t))
                    act.wait_ge(down, freed(t))
                    for m in range(2):
                        last = nc.scalar.activation(hidden[1][:, k, m], bank[2 + 2 * k + m][:], ACT.Relu,
                                                    bias=bias[:, 2 + m:3 + m])
                    last.then_inc(act2, 1)

        @block.vector
        def _(dve):
            for n in (nm, first, xd):
                dve.sem_inc(n, PRIME)
            dve.wait_ge(weights, 80)
            nc.vector.tensor_scalar(fc1[:], fc1[:], rms_w[:, 0:1], None, ALU.mult).then_inc(folded, 1)
            with dve.Fori(0, SEQS) as b:
                for k in range(2):
                    t = b * 2 + k
                    dve.wait_ge(rs, done(t))
                    dve.wait_ge(up, freed(t))
                    nc.vector.tensor_tensor(normed[:, k], branch[:, cols(t)], rstd[:, k], ALU.mult).then_inc(nm, 1)
                for k in range(2):
                    t = b * 2 + k
                    nc.vector.tensor_tensor(x[:, cols(t)], x[:, cols(t)], branch[:, cols(t)], ALU.add
                                            ).then_inc(first, 1)
                for k in range(2):
                    t = b * 2 + k
                    dve.wait_ge(down, done(t))
                    dve.wait_ge(first, done(t))
                    nc.vector.scalar_tensor_tensor(x[:, cols(t)], bank[k][:], bias[:, 4:5], x[:, cols(t)],
                                                   ALU.add, ALU.add).then_inc(xd, 1)


HEADS = 8
HEAD = 64
WINDOW = 64
INNER = HEADS * HEAD
TILE = 128
TILES = T // TILE
HID = 341
HID_PARTS = [(0, 128), (128, 128), (256, 85)]


def normalise(nc, mem, dram):
    x, centre, mean, branch = mem["x"], mem["centre"], mem["mean"], mem["branch"]
    with ExitStack() as ctx:
        def sb(name, shape, dt=F32):
            return ctx.enter_context(nc.sbuf_tensor(f"norm_{name}", shape, dt))

        square = sb("square", [P, 2, CH])
        log = sb("log", [P, 2, CH])
        rstd = sb("rstd", [P, 2, CH])
        bank = [ctx.enter_context(nc.psum_tensor(f"norm_bank{n}", [P, CH], F32)) for n in range(4)]
        centred, sq, variance, lg, rs, out = semaphores(ctx, nc, "norm", "centred square variance log rstd out")
        block = ctx.enter_context(nc.Block())

        @block.tensor
        def _(pe):
            for n in (centred, variance):
                pe.sem_inc(n, PRIME)
            with pe.Fori(0, SEQS) as b:
                for k in range(2):
                    t = b * 2 + k
                    pe.wait_ge(out, freed(t))
                    nc.tensor.matmul(bank[k][:], centre[:], x[:, cols(t)], start=True, stop=True).then_inc(centred, 1)
                for k in range(2):
                    t = b * 2 + k
                    pe.wait_ge(sq, done(t))
                    nc.tensor.matmul(bank[2 + k][:], mean[:], square[:, k], start=True, stop=True).then_inc(variance, 1)

        @block.scalar
        def _(act):
            for n in (sq, lg, rs):
                act.sem_inc(n, PRIME)
            act.preload_act_table_set("natural_log_exp_and_others")
            with act.Fori(0, SEQS) as b:
                for k in range(2):
                    t = b * 2 + k
                    act.wait_ge(centred, done(t))
                    nc.scalar.activation(square[:, k], bank[k][:], ACT.Square).then_inc(sq, 1)
                for k in range(2):
                    t = b * 2 + k
                    act.wait_ge(variance, done(t))
                    nc.scalar.activation(log[:, k], bank[2 + k][:], ACT.Ln, bias=EPS_LN).then_inc(lg, 1)
                for k in range(2):
                    t = b * 2 + k
                    act.wait_ge(lg, done(t))
                    act.wait_ge(out, freed(t))
                    nc.scalar.activation(rstd[:, k], log[:, k], ACT.Exp, scale=-0.5).then_inc(rs, 1)

        @block.vector
        def _(dve):
            dve.sem_inc(out, PRIME)
            with dve.Fori(0, SEQS) as b:
                for k in range(2):
                    t = b * 2 + k
                    dve.wait_ge(rs, done(t))
                    nc.vector.tensor_tensor(branch[:, cols(t)], bank[k][:], rstd[:, k], ALU.mult).then_inc(out, 1)


ATTEND = ("qkv_loaded tables_loaded zeroed hs tables_ready proj qk_copied v_copied v_mixed "
          "square sums floor log rnorm direct crossed added scaled qkT qkT_copied "
          "sim peak shifted prob total inv weighted pT pT_copied av oT_copied wo branch")
NORM, SCORE, EXP, VALUE, OUT = 1, 3, 4, 5, 6


def steps(engine, step):
    for i in range(TILES):
        step(0, i, lambda lag: lag <= i)
    with engine.Fori(1, SEQS) as b:
        for i in range(TILES):
            step(b, i, lambda lag: True)
    for i in range(OUT):
        step(SEQS, i, lambda lag: lag > i)


def attend(nc, mem, dram, layer):
    branch, ident = mem["branch"], mem["ident"]
    with ExitStack() as ctx:
        def sb(name, shape, dt=F32):
            return ctx.enter_context(nc.sbuf_tensor(f"at{layer}_{name}", shape, dt))

        w = sb("w", [P, 3 * INNER])
        wo = sb("wo", [P, 4, P])
        eye16 = sb("eye16", [P, P], BF16)
        mask = sb("mask", [P, 2, TILE], BF16)
        turn = sb("turn", [P, 2, TILES, 2, HEAD])
        scales = sb("scales", [P, 2, 2, HEAD])
        hs = sb("hs", [P, 1 + T])
        qk = sb("qk", [P, 2, 2 * INNER])
        square = sb("square", [P, 2, 2 * INNER])
        direct = sb("direct", [P, 4, 2 * INNER])
        crossed = square
        sums = sb("sums", [P, 2, 2 * HEADS])
        floor = sb("floor", [P, 2, 2 * HEADS])
        log = sb("log", [P, 2, 2 * HEADS])
        rnorm = sb("rnorm", [P, 2, 2 * HEADS])
        qT = sb("qT", [P, 2, 4, TILE])
        kT = sb("kT", [P, 4, WINDOW + T])
        v = sb("v", [P, TILES, INNER])
        v_mix = sb("v_mix", [P, TILES, INNER])
        peak = sb("peak", [P, 2, HEADS])
        prob = sb("prob", [P, 2, HEADS, TILE])
        pT = sb("pT", [P, HEADS, TILE])
        total = sb("total", [P, 2, HEADS])
        inv = sb("inv", [P, 2, HEADS])
        oT = sb("oT", [P, 2, 4, TILE])
        ps = ctx.enter_context(nc.psum_tensor(f"at{layer}_ps", [P, 8, CH], F32))
        Q, K, V, TURN, SIM, AV = 0, 1, 2, 3, 5, 7
        s = dict(zip(ATTEND.split(), semaphores(ctx, nc, f"at{layer}", ATTEND)))
        block = ctx.enter_context(nc.Block())

        @block.sync
        def _(sp):
            sp.dma_start(w[:], dram["wqkv"][layer]).then_inc(s["qkv_loaded"], 16)
            sp.dma_start(wo[:], dram["wo"][layer].rearrange("(c p) n -> p c n", p=P)).then_inc(s["qkv_loaded"], 16)
            sp.dma_start(eye16[:], dram["eye16"]).then_inc(s["qkv_loaded"], 16)
            sp.dma_start(mask[:], dram["mask"]).then_inc(s["qkv_loaded"], 16)
            sp.dma_start(turn[:], dram["turn"]).then_inc(s["tables_loaded"], 16)
            for n, name in enumerate(("q_scale", "k_scale")):
                row = dram[name][layer:layer + 1]
                for half in range(2):
                    h0, h1 = half * 32, (1 - half) * 32
                    if half == 0:
                        sp.dma_start(scales[:, 0, n], row.partition_broadcast(P)).then_inc(s["tables_loaded"], 16)
                    sp.dma_start(scales[:, 1, n, h0:h0 + 32], row[:, h1:h1 + 32].partition_broadcast(P)
                                 ).then_inc(s["tables_loaded"], 16)
            sp.wait_ge(s["tables_loaded"], 16 * 7)

        @block.tensor
        def _(pe):
            for name in "proj qkT sim pT av wo".split():
                pe.sem_inc(s[name], PRIME)
            pe.wait_ge(s["qkv_loaded"], 64)

            def step(b, i, live):
                g = b * TILES + i
                if live(SCORE):
                    n, at_tile = g - SCORE, (i - SCORE) % TILES
                    pe.wait_ge(s["scaled"], done(n))
                    if live(OUT):
                        pe.wait_ge(s["pT_copied"], done(g - OUT))
                    for m in range(8):
                        last = nc.tensor.transpose(ps[:, TURN + m // 4, (m % 4) * TILE:(m % 4 + 1) * TILE],
                                                   direct[:, at_tile % 4, m * TILE:(m + 1) * TILE], ident[:])
                    last.then_inc(s["qkT"], 1)
                if live(0):
                    if i % 4 == 0:
                        pe.wait_ge(s["hs"], 2 * b + i // 4 + 1)
                    pe.wait_ge(s["qk_copied"], freed(g + 1))
                    pe.wait_ge(s["v_copied"], freed(g + 1))
                    if live(OUT + 1):
                        pe.wait_ge(s["branch"], done(g - OUT - 1))
                    for m, to in enumerate((Q, K, V)):
                        last = nc.tensor.matmul(ps[:, to], hs[:, i * TILE:(i + 1) * TILE],
                                                w[:, m * INNER:(m + 1) * INNER], start=True, stop=True)
                    last.then_inc(s["proj"], 1)
                if live(SCORE):
                    n, at_tile = g - SCORE, (i - SCORE) % TILES
                    pe.wait_ge(s["qkT_copied"], done(n))
                    pe.wait_ge(s["shifted"], freed(n + 1))
                    first = int(at_tile == 0)
                    for parity in range(2):
                        nc.tensor.matmul(ps[:, SIM + parity].rearrange("p (h j) -> p h j", h=4), eye16[:],
                                         mask[:, first:first + 1].broadcast_to([P, 4, TILE]),
                                         start=True, stop=False, skip_group_check=True)
                    for h in range(HEADS):
                        at = slice(HEAD * (h % 2), HEAD * (h % 2) + HEAD)
                        c = (h // 2) * TILE
                        windows = at_tile * TILE
                        def score(queries, keys, to):
                            return nc.tensor.matmul(ps[queries, SIM + h % 2, to], qT[at, at_tile % 2, h // 2, queries],
                                                    keys, start=False, stop=True, skip_group_check=True)

                        pair = kT[at, h // 2, windows:windows + TILE].rearrange("p (w c) -> p w c", w=2)
                        nc.tensor.matmul(ps[0:64, SIM + h % 2, c:c + TILE].rearrange("p (w c) -> p w c", w=2), qT[at, at_tile % 2, h // 2, 0:64],
                                                    pair[:, ::-1], start=False, stop=True, skip_group_check=True)
                        last = score(slice(64, 128), kT[at, h // 2, windows + WINDOW:windows + WINDOW + TILE],
                                     slice(c, c + TILE))
                    last.then_inc(s["sim"], 1)
                if live(VALUE):
                    n, half = g - VALUE, (i - VALUE) % 2
                    pe.wait_ge(s["weighted"], done(n))
                    for h in range(HEADS):
                        last = nc.tensor.transpose(ps[:, TURN + h // 4, (h % 4) * TILE:(h % 4 + 1) * TILE],
                                                   prob[:, half, h], ident[:])
                    last.then_inc(s["pT"], 1)
                if live(OUT):
                    n, half = g - OUT, (i - OUT) % 2
                    pe.wait_ge(s["oT_copied"], done(n))
                    if live(0):
                        pe.wait_ge(s["v_copied"], done(g))
                    else:
                        pe.wait_ge(s["branch"], freed(n + 1))
                    for m in range(4):
                        last = nc.tensor.matmul(ps[:, V, 0:TILE], wo[:, m], oT[:, half, m],
                                                start=m == 0, stop=m == 3)
                    last.then_inc(s["wo"], 1)
                if live(VALUE):
                    n, at_tile = g - VALUE, (i - VALUE) % TILES
                    sequence = b if i >= VALUE else b - 1
                    pe.wait_ge(s["pT_copied"], done(n))
                    pe.wait_ge(s["v_copied"], done(n))
                    pe.wait_ge(s["v_mixed"], sequence * (TILES - 1) + at_tile + PRIME)
                    pe.wait_ge(s["oT_copied"], freed(n + 1))
                    for j in range(HEADS):
                        h = 2 * (j % 4) + j // 4
                        to = slice(HEAD * (h % 2), HEAD * (h % 2) + HEAD)
                        for q, values in ((0, v_mix), (1, v)):
                            c = (h // 2) * TILE + q * WINDOW
                            last = nc.tensor.matmul(ps[to, AV, c:c + WINDOW],
                                                    values[:, at_tile, h * HEAD:(h + 1) * HEAD],
                                                    pT[:, j, q * WINDOW:(q + 1) * WINDOW], start=True, stop=True)
                    last.then_inc(s["av"], 1)

            steps(pe, step)

        @block.scalar
        def _(act):
            for name in "qk_copied v_copied square log rnorm qkT_copied prob pT_copied oT_copied".split():
                act.sem_inc(s[name], PRIME)
            act.preload_act_table_set("natural_log_exp_and_others")
            act.wait_ge(s["zeroed"], 3)

            def step(b, i, live):
                g = b * TILES + i
                if live(0) and i < 2:
                    if live(TILES):
                        act.wait_ge(s["proj"], freed(g + 1 - i))
                    nc.scalar.activation(hs[0:64, i * CH:(i + 1) * CH], branch[0:64, cols(b * 2 + i)], ACT.Copy)
                    nc.scalar.activation(hs[64:128, 1 + i * CH:1 + (i + 1) * CH], branch[64:128, cols(b * 2 + i)],
                                         ACT.Copy).then_inc(s["hs"], 1)
                if live(SCORE):
                    n, at_tile = g - SCORE, (i - SCORE) % TILES
                    act.wait_ge(s["qkT"], done(n))
                    act.wait_ge(s["sim"], freed(n))
                    nc.scalar.activation(qT[:, at_tile % 2], ps[:, TURN].rearrange("p (m t) -> p m t", m=4), ACT.Copy)
                    at = WINDOW + at_tile * TILE
                    nc.scalar.activation(kT[:, :, at:at + TILE], ps[:, TURN + 1].rearrange("p (m t) -> p m t", m=4),
                                         ACT.Copy).then_inc(s["qkT_copied"], 1)
                if live(EXP):
                    n, half = g - EXP, (i - EXP) % 2
                    act.wait_ge(s["shifted"], done(n))
                    nc.scalar.activation(prob[:, half], prob[:, half], ACT.Exp).then_inc(s["prob"], 1)
                if live(NORM):
                    n, half = g - NORM, (i - NORM) % 2
                    act.wait_ge(s["floor"], done(n))
                    nc.scalar.activation(log[:, half], floor[:, half], ACT.Ln, scale=2.0 ** 30).then_inc(s["log"], 1)
                    act.wait_ge(s["log"], done(n))
                    act.wait_ge(s["scaled"], freed(n))
                    nc.scalar.activation(rnorm[:, half], log[:, half], ACT.Exp, scale=-0.5,
                                         bias=float(15 * np.log(2.0))).then_inc(s["rnorm"], 1)
                if live(0):
                    act.wait_ge(s["proj"], done(g))
                    act.wait_ge(s["crossed"], freed(g))
                    nc.scalar.activation(qk[:, i % 2], ps[:, Q:Q + 2].rearrange("p a n -> p (a n)"), ACT.Copy
                                         ).then_inc(s["qk_copied"], 1)
                    nc.scalar.activation(v[:, i], ps[:, V], ACT.Copy)
                    nc.scalar.activation(v_mix[0:64, i], ps[0:64, V], ACT.Copy).then_inc(s["v_copied"], 1)
                if live(VALUE):
                    n = g - VALUE
                    act.wait_ge(s["pT"], done(n))
                    act.wait_ge(s["av"], freed(n + 1))
                    nc.scalar.activation(pT[:].rearrange("p h j -> p (h j)"),
                                         ps[:, TURN:TURN + 2].rearrange("p a n -> p (a n)"), ACT.Copy
                                         ).then_inc(s["pT_copied"], 1)
                if live(0):
                    act.wait_ge(s["qk_copied"], done(g))
                    act.wait_ge(s["added"], freed(g))
                    nc.scalar.activation(square[:, i % 2], qk[:, i % 2], ACT.Square).then_inc(s["square"], 1)
                if live(VALUE):
                    n, half = g - VALUE, (i - VALUE) % 2
                    act.wait_ge(s["av"], done(n))
                    act.wait_ge(s["wo"], freed(n))
                    nc.scalar.activation(oT[:, half], ps[:, AV].rearrange("p (m t) -> p m t", m=4), ACT.Copy
                                         ).then_inc(s["oT_copied"], 1)

            steps(act, step)

        @block.gpsimd
        def _(pool):
            for name in "added scaled weighted".split():
                pool.sem_inc(s[name], PRIME)

            def step(b, i, live):
                g = b * TILES + i
                if live(NORM):
                    n = g - NORM
                    half, quarter = (i - NORM) % 2, (i - NORM) % 4
                    pool.wait_ge(s["crossed"], done(n))
                    nc.gpsimd.tensor_tensor(direct[:, quarter], direct[:, quarter], crossed[:, half], ALU.add
                                            ).then_inc(s["added"], 1)
                if live(EXP):
                    n, half = g - EXP, (i - EXP) % 2
                    pool.wait_ge(s["inv"], done(n))
                    nc.gpsimd.tensor_tensor(prob[:, half], prob[:, half],
                                            inv[:, half].unsqueeze(2).broadcast_to([P, HEADS, TILE]), ALU.mult
                                            ).then_inc(s["weighted"], 1)
                if live(NORM):
                    n = g - NORM
                    half, quarter = (i - NORM) % 2, (i - NORM) % 4
                    heads = direct[:, quarter].rearrange("p (h e) -> p h e", e=HEAD)
                    pool.wait_ge(s["added"], done(n))
                    pool.wait_ge(s["rnorm"], done(n))
                    nc.gpsimd.tensor_tensor(heads, heads,
                                            rnorm[:, half].unsqueeze(2).broadcast_to([P, 2 * HEADS, HEAD]),
                                            ALU.mult).then_inc(s["scaled"], 1)

            steps(pool, step)

        @block.vector
        def _(dve):
            for name in "v_mixed sums floor direct crossed peak shifted total inv branch".split():
                dve.sem_inc(s[name], PRIME)
            nc.vector.memset(hs[64:128, 0:1], 0.0).then_inc(s["zeroed"], 1)
            nc.vector.memset(kT[:, :, 0:WINDOW], 0.0).then_inc(s["zeroed"], 1)
            nc.vector.memset(v_mix[64:128, 0], 0.0).then_inc(s["zeroed"], 1)
            dve.wait_ge(s["tables_loaded"], 16 * 7)
            dve.wait_ge(s["zeroed"], 3)
            for n in range(2):
                nc.vector.tensor_tensor(turn[:, n], turn[:, n],
                                        scales[:, n].unsqueeze(1).broadcast_to([P, TILES, 2, HEAD]), ALU.mult
                                        ).then_inc(s["tables_ready"], 1)
            dve.wait_ge(s["tables_ready"], 2)

            def step(b, i, live):
                g = b * TILES + i
                if live(NORM):
                    n, at_tile = g - NORM, (i - NORM) % TILES
                    p = at_tile % 2
                    dve.wait_ge(s["square"], done(n))
                    nc.vector.tensor_reduce(sums[:, p], square[:, p].rearrange("p (h d) -> p h d", d=HEAD), AX_X,
                                            ALU.add).then_inc(s["sums"], 1)
                    dve.wait_ge(s["sums"], done(n))
                    nc.vector.tensor_scalar(floor[:, p], sums[:, p], 1e-24, None, ALU.max).then_inc(s["floor"], 1)
                    if live(NORM + 4):
                        dve.wait_ge(s["qkT"], done(n - 4))
                    for m in range(2):
                        of = qk[:, p, m * INNER:(m + 1) * INNER].rearrange("p (h d) -> p h d", d=HEAD)
                        to = direct[:, at_tile % 4, m * INNER:(m + 1) * INNER].rearrange("p (h d) -> p h d", d=HEAD)
                        last = nc.vector.tensor_tensor(
                            to, of, turn[:, 0, at_tile, m:m + 1].broadcast_to([P, HEADS, HEAD]), ALU.mult)
                    last.then_inc(s["direct"], 1)
                    for half in range(2):
                        h0, h1 = 32 * half, 32 * (1 - half)
                        for m in range(2):
                            of = qk[:, p, m * INNER:(m + 1) * INNER].rearrange("p (h d) -> p h d", d=HEAD)
                            to = crossed[:, p, m * INNER:(m + 1) * INNER].rearrange("p (h d) -> p h d", d=HEAD)
                            last = nc.vector.tensor_tensor(
                                to[:, :, h0:h0 + 32], of[:, :, h1:h1 + 32],
                                turn[:, 1, at_tile, m:m + 1, h0:h0 + 32].broadcast_to([P, HEADS, 32]), ALU.mult)
                    last.then_inc(s["crossed"], 1)
                if live(EXP):
                    n, half = g - EXP, (i - EXP) % 2
                    dve.wait_ge(s["prob"], done(n))
                    nc.vector.tensor_reduce(total[:, half], prob[:, half], AX_X, ALU.add).then_inc(s["total"], 1)
                    dve.wait_ge(s["total"], done(n))
                    dve.wait_ge(s["weighted"], freed(n))
                    nc.vector.reciprocal(inv[:, half], total[:, half]).then_inc(s["inv"], 1)
                if live(SCORE):
                    n, half = g - SCORE, (i - SCORE) % 2
                    dve.wait_ge(s["sim"], done(n))
                    scores = ps[:, SIM:SIM + 2].rearrange("p a (h j) -> p (a h) j", h=4)
                    nc.vector.tensor_reduce(peak[:, half], scores, AX_X, ALU.max).then_inc(s["peak"], 1)
                    dve.wait_ge(s["peak"], done(n))
                    dve.wait_ge(s["pT"], freed(n))
                    nc.vector.tensor_tensor(prob[:, half], scores,
                                            peak[:, half].unsqueeze(2).broadcast_to([P, HEADS, TILE]),
                                            ALU.subtract).then_inc(s["shifted"], 1)
                if live(0) and i > 0:
                    dve.wait_ge(s["v_copied"], done(g - 1))
                    nc.vector.tensor_copy(v_mix[64:128, i], v[64:128, i - 1]).then_inc(s["v_mixed"], 1)
                if live(OUT):
                    n = g - OUT
                    at = branch[:, cols(n, TILE)]
                    dve.wait_ge(s["wo"], done(n))
                    nc.vector.tensor_tensor(at, at, ps[:, V, 0:TILE], ALU.add).then_inc(s["branch"], 1)

            steps(dve, step)


GLU = ("w_loaded lb_done biased folded zeroed hs centred square variance log rstd normed up gate act prod down branch")


def gated_mlp(nc, mem, dram, layer):
    branch, x, centre, mean = mem["branch"], mem["x"], mem["centre"], mem["mean"]
    with ExitStack() as ctx:
        def sb(name, shape, dt=F32):
            return ctx.enter_context(nc.sbuf_tensor(f"glu{layer}_{name}", shape, dt))

        w1 = sb("w1", [P, 2 * HID])
        w2 = sb("w2", [P, 3, P])
        ln_g = sb("ln_g", [P, 1])
        ln_b = sb("ln_b", [P, 1])
        b1 = sb("b1", [P, 2, 3])
        b2 = sb("b2", [P, 1])
        hs = sb("hs", [P, 1 + T])
        square = sb("square", [P, 2, CH])
        log = sb("log", [P, 2, CH])
        rstd = sb("rstd", [P, 2, CH])
        normed = sb("normed", [P, ALL])
        gelu = sb("gelu", [P, 2, 3, CH])
        prod = sb("prod", [P, 2, 3, CH])
        bank = [ctx.enter_context(nc.psum_tensor(f"glu{layer}_bank{n}", [P, CH], F32)) for n in range(8)]
        s = dict(zip(GLU.split(), semaphores(ctx, nc, f"glu{layer}", GLU)))
        (x_sem,) = semaphores(ctx, nc, f"glu{layer}", "x")
        block = ctx.enter_context(nc.Block())

        @block.sync
        def _(sp):
            n = 0
            loads = [(w1[:], dram["w1"][layer]), (ln_g[:], dram["ln_g"][layer]),
                     (ln_b[:], dram["ln_b"][layer]), (b2[:], dram["b2"][layer]),
                     (b1[:], dram["b1"][layer])]
            for c, (first, size) in enumerate(HID_PARTS):
                loads.append((w2[0:size, c], dram["w2"][layer, first:first + size]))
            for to, of in loads:
                sp.dma_start(to, of).then_inc(s["w_loaded"], 16)
                n += 16
            sp.wait_ge(s["w_loaded"], n)

        @block.tensor
        def _(pe):
            for name in "centred variance up down".split():
                pe.sem_inc(s[name], PRIME)
            pe.wait_ge(s["w_loaded"], 16 * 8)
            for m in range(2):
                for c, (first, size) in enumerate(HID_PARTS):
                    last = nc.tensor.matmul(bank[6][0:size, 3 * m + c:3 * m + c + 1],
                                            w1[:, m * HID + first:m * HID + first + size], ln_b[:],
                                            start=True, stop=True)
            last.then_inc(s["lb_done"], 1)
            pe.wait_ge(s["folded"], 1)
            with pe.Fori(0, SEQS) as b:
                for k in range(2):
                    t = b * 2 + k
                    pe.wait_ge(s["hs"], done(t))
                    pe.wait_ge(s["normed"], freed(t))
                    nc.tensor.matmul(bank[k][:], centre[:], hs[:, k * CH:(k + 1) * CH], start=True, stop=True
                                     ).then_inc(s["centred"], 1)
                for k in range(2):
                    t = b * 2 + k
                    pe.wait_ge(s["square"], done(t))
                    nc.tensor.matmul(bank[2 + k][:], mean[:], square[:, k], start=True, stop=True
                                     ).then_inc(s["variance"], 1)
            pe.wait_ge(s["normed"], done(2 * SEQS - 1))

            def up(t):
                pe.wait_ge(s["prod"], freed(t + 1))
                for m in range(2):
                    for c, (first, size) in enumerate(HID_PARTS):
                        last = nc.tensor.matmul(bank[3 * m + c][0:size, :],
                                                w1[:, m * HID + first:m * HID + first + size],
                                                normed[:, cols(t)], start=True, stop=True)
                last.then_inc(s["up"], 1)

            def down(t, k):
                pe.wait_ge(s["prod"], done(t))
                pe.wait_ge(s["branch"], freed(t))
                for c, (first, size) in enumerate(HID_PARTS):
                    last = nc.tensor.matmul(bank[6 + k][:], w2[0:size, c], prod[0:size, k, c],
                                            start=c == 0, stop=c == 2)
                last.then_inc(s["down"], 1)

            up(0)
            with pe.Fori(0, SEQS - 1) as b:
                for k in range(2):
                    t = b * 2 + k
                    up(t + 1)
                    down(t, k)
            up(2 * SEQS - 1)
            down(2 * SEQS - 2, 0)
            down(2 * SEQS - 1, 1)

        @block.scalar
        def _(act):
            for name in "hs square log rstd act".split():
                act.sem_inc(s[name], PRIME)
            act.preload_act_table_set("natural_log_exp_and_others")
            act.wait_ge(s["zeroed"], 1)
            with act.Fori(0, SEQS) as b:
                for k in range(2):
                    t = b * 2 + k
                    act.wait_ge(s["centred"], freed(t))
                    nc.scalar.activation(hs[0:64, k * CH:(k + 1) * CH], branch[0:64, cols(t)], ACT.Copy)
                    nc.scalar.activation(hs[64:128, 1 + k * CH:1 + (k + 1) * CH], branch[64:128, cols(t)], ACT.Copy
                                         ).then_inc(s["hs"], 1)
                for k in range(2):
                    t = b * 2 + k
                    act.wait_ge(s["centred"], done(t))
                    nc.scalar.activation(square[:, k], bank[k][:], ACT.Square).then_inc(s["square"], 1)
                for k in range(2):
                    t = b * 2 + k
                    act.wait_ge(s["variance"], done(t))
                    nc.scalar.activation(log[:, k], bank[2 + k][:], ACT.Ln, bias=EPS_LN).then_inc(s["log"], 1)
                for k in range(2):
                    t = b * 2 + k
                    act.wait_ge(s["log"], done(t))
                    act.wait_ge(s["normed"], freed(t))
                    nc.scalar.activation(rstd[:, k], log[:, k], ACT.Exp, scale=-0.5).then_inc(s["rstd"], 1)
            act.preload_act_table_set("gelu_and_others")
            with act.Fori(0, SEQS) as b:
                for k in range(2):
                    t = b * 2 + k
                    act.wait_ge(s["up"], done(t))
                    act.wait_ge(s["prod"], freed(t))
                    for c, (first, size) in enumerate(HID_PARTS):
                        last = nc.scalar.activation(gelu[0:size, k, c], bank[3 + c][0:size, :], ACT.Gelu,
                                                    bias=b1[0:size, 1, c:c + 1])
                    last.then_inc(s["act"], 1)

        @block.vector
        def _(dve):
            for name in "normed prod branch".split():
                dve.sem_inc(s[name], PRIME)
            nc.vector.memset(hs[64:128, 0:1], 0.0).then_inc(s["zeroed"], 1)
            dve.wait_ge(s["w_loaded"], 16 * 8)
            dve.wait_ge(s["lb_done"], 1)
            for c, (first, size) in enumerate(HID_PARTS):
                last = nc.vector.tensor_tensor(
                    b1[0:size, :, c], b1[0:size, :, c],
                    bank[6][0:size, 0:6].rearrange("p (m c) -> p m c", m=2)[:, :, c], ALU.add)
            last.then_inc(s["biased"], 1)
            nc.vector.tensor_scalar(w1[:], w1[:], ln_g[:, 0:1], None, ALU.mult).then_inc(s["folded"], 1)
            dve.wait_ge(s["biased"], 1)
            with dve.Fori(0, SEQS) as b:
                for k in range(2):
                    t = b * 2 + k
                    dve.wait_ge(s["rstd"], done(t))
                    nc.vector.tensor_tensor(normed[:, cols(t)], bank[k][:], rstd[:, k], ALU.mult
                                            ).then_inc(s["normed"], 1)

            def gated(t, k):
                dve.wait_ge(s["act"], done(t))
                dve.wait_ge(s["down"], freed(t))
                for c, (first, size) in enumerate(HID_PARTS):
                    last = nc.vector.scalar_tensor_tensor(prod[0:size, k, c], bank[c][0:size, :],
                                                          b1[0:size, 0, c:c + 1], gelu[0:size, k, c],
                                                          ALU.add, ALU.mult)
                last.then_inc(s["prod"], 1)

            def added(t, k):
                at = branch[:, cols(t)]
                dve.wait_ge(s["down"], done(t))
                nc.vector.scalar_tensor_tensor(at, bank[6 + k][:], b2[:, 0:1], at, ALU.add, ALU.add
                                               ).then_inc(s["branch"], 1)
                if layer == 1:
                    dve.wait_ge(s["branch"], done(t))
                    nc.vector.tensor_tensor(x[:, cols(t)], x[:, cols(t)], at, ALU.add).then_inc(x_sem, 1)

            gated(0, 0)
            with dve.Fori(0, SEQS - 1) as b:
                for k in range(2):
                    t = b * 2 + k
                    gated(t + 1, 1 - k)
                    added(t, k)
            gated(2 * SEQS - 1, 1)
            added(2 * SEQS - 2, 0)
            added(2 * SEQS - 1, 1)


def store_result(nc, mem, out):
    with ExitStack() as ctx:
        (stored,) = semaphores(ctx, nc, "end", "stored")
        block = ctx.enter_context(nc.Block())

        @block.sync
        def _(sp):
            sp.dma_start(out, mem["x"][:]).then_inc(stored, 16)
            sp.wait_ge(stored, 16)


def attend_first(nc, mem, dram):
    attend(nc, mem, dram, 0)


def gated_mlp_first(nc, mem, dram):
    gated_mlp(nc, mem, dram, 0)


def attend_second(nc, mem, dram):
    attend(nc, mem, dram, 1)


def gated_mlp_second(nc, mem, dram):
    gated_mlp(nc, mem, dram, 1)


STAGES = [min_gru, experts, mamba, mlp, normalise, attend_first, gated_mlp_first, attend_second, gated_mlp_second]


def program(nc, dram, out, stages=None):
    with ExitStack() as ctx:
        mem = {name: ctx.enter_context(nc.sbuf_tensor(name, shape, F32)) for name, shape in (
            ("x", [P, ALL]), ("branch", [P, ALL]), ("centre", [P, P]), ("mean", [P, P]), ("ident", [P, P]))}
        load_constants(nc, mem, dram)
        nc.all_engine_barrier()
        for stage in STAGES if stages is None else stages:
            stage(nc, mem, dram)
            nc.all_engine_barrier()
        store_result(nc, mem, out)


def shape_constants():
    eye = np.eye(P, dtype=np.float32)
    mean = np.full((P, P), 1.0 / P, np.float32)
    pick = np.zeros((P, 32, P), np.float32)
    for first in (0, 64, 96):
        pick[first + np.arange(32), np.arange(32)] = 1.0
    query, key = np.arange(TILE)[:, None] % WINDOW, np.arange(TILE)[None, :] % WINDOW
    own = (np.arange(TILE)[:, None] < WINDOW) == (np.arange(TILE)[None, :] < WINDOW)
    masked = np.where(own, key > query, query > key)
    first = masked | ((np.arange(TILE)[:, None] < WINDOW) & (np.arange(TILE)[None, :] >= WINDOW))
    mask = np.where(np.stack([masked, first], 1), np.float32(-1e30), np.float32(0))
    half = np.arange(0, HEAD, 2, dtype=np.float32)
    inv_freq = (np.float32(1.0) / np.float32(10000.0) ** (half / np.float32(HEAD))).astype(np.float32)
    t = np.arange(T, dtype=np.float32)
    freqs = t[:, None] * inv_freq[None, :]
    base = (half + np.float32(0.4 * HEAD)) / np.float32(1.4 * HEAD)
    scale = base[None, :] ** ((t - T // 2) / np.float32(WINDOW // 2))[:, None]
    turn = np.zeros((2, T, 2, HEAD), np.float32)
    for n, size in ((0, 8.0 * scale), (1, 1.0 / scale)):
        turn[0, :, n] = np.tile(np.cos(freqs) * size, 2)
        turn[1, :, n] = np.concatenate([-np.sin(freqs) * size, np.sin(freqs) * size], 1)
    turn = turn.reshape(2, TILES, P, 2, HEAD).transpose(2, 0, 1, 3, 4)
    bf16 = mybir.dt.np(BF16)
    order = np.arange(E, 0, -1, dtype=np.float32)[None, :]
    index = np.arange(BLOCKS, dtype=np.float32)[None, :]
    going = np.ones((E, TOKEN_TILES), np.float32)
    going[:, 0] = 0.0
    return {"before": np.triu(np.ones((P, P), np.float32), 1), "index": index, "going": going.reshape(1, -1), "order": order, "eye16": eye.astype(bf16), "mask": mask.astype(bf16), "turn": turn, "ident": eye, "mean": mean, "centre": eye - mean, "pick": pick.astype(mybir.dt.np(BF16))}


def laid_out(i):
    def halves(v):
        return v.reshape(2, P, *v.shape[1:]).swapaxes(0, 1)

    x_proj = i["L1_attn_x_proj_w"].T
    dbc = np.zeros((2 * P, P), x_proj.dtype)
    dbc[:, 32:40] = x_proj[:, 0:8]
    for first in (0, 64, 96):
        dbc[:, first:first + 32] = x_proj[:, 8:40]
    fc2 = i["L1_attn_fc2_w"].T
    b1 = np.zeros((2, 2, 3 * P), i["L1_ffn_b1"].dtype)
    b1[:, :, 0:HID] = i["L1_ffn_b1"].reshape(2, 2, HID)
    return {
        "router_w": i["L0_ffn_router_w"],
        "router_b": i["L0_ffn_router_b"][None, :],
        "moe_w1": i["L0_ffn_W1"],
        "moe_w2": i["L0_ffn_W2"],
        "moe_b1": i["L0_ffn_b1"].reshape(8, 4, P).transpose(2, 0, 1),
        "moe_b2": i["L0_ffn_b2"][None],
        "wqkv": i["L1_ffn_wqkv"],
        "wo": i["L1_ffn_wo"],
        "q_scale": i["L1_ffn_q_scale"],
        "k_scale": i["L1_ffn_k_scale"],
        "ln_g": i["L1_ffn_ln_g"][:, :, None],
        "ln_b": i["L1_ffn_ln_b"][:, :, None],
        "w1": i["L1_ffn_w1"],
        "b1": b1.reshape(2, 2, 3, P).transpose(0, 3, 1, 2),
        "w2": i["L1_ffn_w2"],
        "b2": i["L1_ffn_b2"][:, :, None],
        "in_w": i["L1_attn_in_proj_w"].T,
        "dbc_w": halves(dbc),
        "dt_w": i["L1_attn_dt_proj_w"].T,
        "out_w": halves(i["L1_attn_out_proj_w"].T),
        "rms1": i["L1_attn_rms1_w"][:, None],
        "conv_w": halves(i["L1_attn_conv_w"]),
        "conv_b": halves(i["L1_attn_conv_b"]),
        "dt_b": halves(i["L1_attn_dt_proj_b"]),
        "skip": halves(i["L1_attn_D_skip"]),
        "a_log": halves(i["L1_attn_A_log"]),
        "rms2": i["L1_attn_rms2_w"][:, None],
        "fc1": i["L1_attn_fc1_w"].T.reshape(P, 2, P),
        "fc2": halves(fc2).reshape(P, 2, 2, P),
        "fc3": halves(i["L1_attn_fc3_w"].T),
        "mlp_b": np.concatenate([i["L1_attn_fc1_b"].reshape(2, P), i["L1_attn_fc2_b"].reshape(2, P),
                                 i["L1_attn_fc3_b"].reshape(1, P)]).T,
        "x": i["L0_attn_h"].reshape(ALL, P).T,
        "gru_w0": i["L0_attn_W0"],
        "gru_w1": i["L0_attn_W1"],
    }


def kernel(**inputs):
    import concourse.bacc as bacc
    from concourse.bass_utils import run_bass_kernel_spmd

    arrays = {k: np.ascontiguousarray(v) for k, v in laid_out({k: np.asarray(v) for k, v in inputs.items()}).items()}
    arrays.update(shape_constants())
    arrays = {f"in_{k}": v for k, v in arrays.items()}
    nc = bacc.Bacc("TRN2", target_bir_lowering=False, num_devices=1)
    dram = {k[3:]: nc.dram_tensor(k, v.shape, mybir.dt.from_np(v.dtype), kind="ExternalInput").ap()
            for k, v in arrays.items()}
    out = nc.dram_tensor("out_x", (P, ALL), F32, kind="ExternalOutput").ap()
    program(nc, dram, out)
    result = run_bass_kernel_spmd(nc, [arrays], core_ids=[0]).results[0]["out_x"]
    return np.ascontiguousarray(np.asarray(result).T).reshape(SEQS, T, P)
```

```python
from contextlib import ExitStack

import numpy as np

import concourse.bass as bass
from concourse import mybir

F32 = mybir.dt.float32
BF16 = mybir.dt.bfloat16
U32 = mybir.dt.uint32
ACT = mybir.ActivationFunctionType
ALU = mybir.AluOpType
AX_X = mybir.AxisListType.X

P = 128
SEQS = 4
T = 1024
CH = 512
CHUNKS = T // CH
ALL = SEQS * T
EPS_LN = 1e-5
EPS_RMS = 1e-6

PRIME = 2


def done(t):
    return t + 1 + PRIME


def freed(t):
    return t - 1 + PRIME


def cols(t, width=CH):
    return bass.ds(t * width, width)


def steps(engine, step, count, tail):
    peeled = -(-tail // count)
    for b in range(peeled):
        for i in range(count):
            step(b, i, lambda lag: lag <= b * count + i)
    with engine.Fori(peeled, SEQS) as b:
        for i in range(count):
            step(b, i, lambda lag: True)
    for i in range(tail):
        step(SEQS + i // count, i % count, lambda lag: lag > i)


def semaphores(ctx, nc, stage, names):
    made = [nc.alloc_semaphore(f"{stage}_{n}") for n in names.split()]
    ctx.callback(nc.clear_and_free_semaphores, made)
    return made


def load_constants(nc, mem, dram):
    with ExitStack() as ctx:
        (loaded,) = semaphores(ctx, nc, "init", "loaded")
        block = ctx.enter_context(nc.Block())

        @block.sync
        def _(sp):
            n = 0
            for name in ("centre", "mean", "ident"):
                sp.dma_start(mem[name][:], dram[name]).then_inc(loaded, 16)
                n += 16
            sp.dma_start(mem["x"][:], dram["x"]).then_inc(loaded, 16)
            sp.wait_ge(loaded, n + 16)


def layer_norm(nc, mem, name, source, into, shifted=False, rms_into=None, loads=()):
    centre, mean = mem["centre"], mem["mean"]
    AHEAD = 4

    def raised(t):
        return t + 1 + AHEAD

    def free(t):
        return t + 1

    with ExitStack() as ctx:
        def sb(what, shape):
            return ctx.enter_context(nc.sbuf_tensor(f"{name}_{what}", shape, F32))

        kinds = 1 if rms_into is None else 2
        square = sb("square", [P, AHEAD, CH])
        log = sb("log", [P, AHEAD, kinds, CH])
        rstd = sb("rstd", [P, AHEAD, kinds, CH])
        hs = sb("shifted", [P, SEQS, 1 + T]) if shifted else None
        bank = [ctx.enter_context(nc.psum_tensor(f"{name}_bank{n}", [P, CH], F32)) for n in range(8)]
        loaded, moved, centred, squared, variance, logged, rooted, through = semaphores(
            ctx, nc, name, "loaded moved centred squared variance logged rooted through")
        block = ctx.enter_context(nc.Block())

        if loads:
            @block.sync
            def _(sp):
                for to, of in loads:
                    sp.dma_start(to, of).then_inc(loaded, 16)
                sp.wait_ge(loaded, 16 * len(loads))

        @block.tensor
        def _(pe):
            for n in (centred, variance):
                pe.sem_inc(n, AHEAD)
            with pe.Fori(0, ALL // (AHEAD * CH)) as b:
                for m in range(AHEAD + 1):
                    if m < AHEAD:
                        t = b * AHEAD + m
                        pe.wait_ge(through, free(t))
                        if shifted:
                            pe.wait_ge(moved, raised(t))
                            of = hs[:, bass.ds(b * (AHEAD // CHUNKS) + m // CHUNKS, 1),
                                    m % CHUNKS * CH:(m % CHUNKS + 1) * CH]
                        else:
                            of = source[:, cols(t)]
                        nc.tensor.matmul(bank[m][:], centre[:], of, start=True, stop=True).then_inc(centred, 1)
                    if m >= 1:
                        t = b * AHEAD + m - 1
                        pe.wait_ge(squared, raised(t))
                        nc.tensor.matmul(bank[AHEAD + m - 1][:], mean[:], square[:, m - 1], start=True, stop=True
                                         ).then_inc(variance, 1)

        @block.scalar
        def _(act):
            for n in (squared, logged, rooted):
                act.sem_inc(n, AHEAD)
            act.preload_act_table_set("natural_log_exp_and_others")
            with act.Fori(0, ALL // (AHEAD * CH)) as b:
                for m in range(AHEAD + 1):
                    if m < AHEAD:
                        t = b * AHEAD + m
                        act.wait_ge(centred, raised(t))
                        nc.scalar.activation(square[:, m], bank[m][:], ACT.Square).then_inc(squared, 1)
                    if m >= 1:
                        t = b * AHEAD + m - 1
                        act.wait_ge(variance, raised(t))
                        last = nc.scalar.activation(log[:, m - 1, 0], bank[AHEAD + m - 1][:], ACT.Ln, bias=EPS_LN)
                        if kinds == 2:
                            last = nc.scalar.activation(log[:, m - 1, 1], bank[AHEAD + m - 1][:], ACT.Ln,
                                                        scale=1.0 + EPS_RMS, bias=EPS_RMS * EPS_LN)
                        last.then_inc(logged, 1)
                        act.wait_ge(logged, raised(t))
                        act.wait_ge(through, free(t))
                        nc.scalar.activation(rstd[:, m - 1], log[:, m - 1], ACT.Exp, scale=-0.5).then_inc(rooted, 1)

        @block.vector
        def _(dve):
            for n in (through, moved):
                dve.sem_inc(n, AHEAD)
            if shifted:
                nc.vector.memset(hs[64:128, :, 0:1], 0.0)
            with dve.Fori(0, ALL // (AHEAD * CH)) as b:
                if shifted:
                    for m in range(AHEAD):
                        t, k = b * AHEAD + m, m % CHUNKS
                        of_sequence = bass.ds(b * (AHEAD // CHUNKS) + m // CHUNKS, 1)
                        for rows, on in ((slice(0, 64), 0), (slice(64, 128), 1)):
                            last = nc.vector.tensor_copy(hs[rows, of_sequence, on + k * CH:on + (k + 1) * CH],
                                                         source[rows, cols(t)])
                        last.then_inc(moved, 1)
                for m in range(AHEAD):
                    t = b * AHEAD + m
                    dve.wait_ge(rooted, raised(t))
                    if kinds == 2:
                        nc.vector.tensor_tensor(rms_into[:, cols(t)], bank[m][:], rstd[:, m, 1], ALU.mult)
                    nc.vector.tensor_tensor(into[:, cols(t)], bank[m][:], rstd[:, m, 0], ALU.mult
                                            ).then_inc(through, 1)
    nc.all_engine_barrier()


def min_gru(nc, mem, dram):
    x = mem["x"]
    LAYERS = ((0, 0), (1, 2))
    with ExitStack() as ctx:
        def sb(name, shape, dt=F32):
            return ctx.enter_context(nc.sbuf_tensor(f"gru_{name}", shape, dt))

        w = sb("w", [P, 2, 3, P])
        h = [sb("h0", [P, ALL]), mem["branch"]]
        layer_norm(nc, mem, "gru_norm", x, h[0], loads=[
            (w[:, n], dram[f"gru_w{n}"].rearrange("d (g n) -> d g n", g=3)) for n in range(2)])
        cand, update, keep, gate, value, scan, mix = (
            sb(name, [P, 2, 2, CH]) for name in "cand update keep gate value scan mix".split())
        bank = [[ctx.enter_context(nc.psum_tensor(f"gru_bank{layer}{g}", [P, CH], F32)) for g in range(3)]
                for layer in range(2)]
        names = "gates cand update gate keep low fed value scan off gated h".split()
        s = {name: semaphores(ctx, nc, "gru", f"{name}_0 {name}_1") for name in names}
        (x_done,) = semaphores(ctx, nc, "gru", "x_done")
        block = ctx.enter_context(nc.Block())

        def prime(engine, names):
            for name in names.split():
                for layer in range(2):
                    engine.sem_inc(s[name][layer], PRIME)

        @block.tensor
        def _(pe):
            prime(pe, "gates")

            def step(b, k, live):
                for layer, lag in LAYERS:
                    if live(lag):
                        t = b * 2 + k - lag
                        if layer == 1:
                            pe.wait_ge(s["h"][0], done(t))
                        pe.wait_ge(s["fed"][layer], freed(t + 1))
                        pe.wait_ge(s["keep"][layer], freed(t + 1))
                        for g in range(3):
                            last = nc.tensor.matmul(bank[layer][g][:], w[:, layer, g], h[layer][:, cols(t)],
                                                    start=True, stop=True)
                        last.then_inc(s["gates"][layer], 1)

            steps(pe, step, CHUNKS, 3)

        @block.scalar
        def _(act):
            prime(act, "cand update gate keep")

            def step(b, k, live):
                for layer, lag in LAYERS:
                    if live(lag):
                        t = b * 2 + k - lag
                        act.wait_ge(s["gates"][layer], done(t))
                        act.wait_ge(s["h"][layer], freed(t))
                        for to, name, g, scale in ((cand, "cand", 0, 1.0), (update, "update", 1, 1.0),
                                                   (gate, "gate", 1, -1.0), (keep, "keep", 2, 1.0)):
                            nc.scalar.activation(to[:, layer, k], bank[layer][g][:], ACT.Sigmoid, scale=scale
                                                 ).then_inc(s[name][layer], 1)

            steps(act, step, CHUNKS, 3)

        @block.gpsimd
        def _(pool):
            prime(pool, "off")
            pool.sem_inc(x_done, PRIME)

            def step(b, k, live):
                if live(3):
                    t = b * 2 + k - 3
                    pool.wait_ge(s["h"][1], done(t))
                    nc.gpsimd.tensor_tensor(x[:, cols(t)], x[:, cols(t)], mix[:, 1, 1 - k], ALU.add
                                            ).then_inc(x_done, 1)
                for layer, lag in LAYERS:
                    if live(lag):
                        t = b * 2 + k - lag
                        pool.wait_ge(s["scan"][layer], done(t))
                        if layer == 0:
                            pool.wait_ge(s["h"][0], freed(t))
                        else:
                            pool.wait_ge(x_done, freed(t))
                        nc.gpsimd.tensor_tensor(mix[:, layer, k], scan[:, layer, k], h[layer][:, cols(t)],
                                                ALU.subtract).then_inc(s["off"][layer], 1)

            steps(pool, step, CHUNKS, 3)

        @block.vector
        def _(dve):
            prime(dve, "low fed value scan gated h")

            def step(b, k, live):
                scanned = [(layer, b * 2 + k - lag) for layer, lag in LAYERS if live(lag)]
                def feed(layer, t):
                    dve.wait_ge(s["cand"][layer], done(t))
                    nc.vector.tensor_scalar(cand[:, layer, k], cand[:, layer, k], 0.5, None, ALU.min
                                            ).then_inc(s["low"][layer], 1)
                    dve.wait_ge(s["low"][layer], done(t))
                    nc.vector.scalar_tensor_tensor(value[:, layer, k], bank[layer][0][:], 0.0, cand[:, layer, k],
                                                   ALU.max, ALU.add).then_inc(s["fed"][layer], 1)

                if live(0):
                    feed(*scanned[0])
                mixed = [(layer, b * 2 + k - lag - 1) for layer, lag in LAYERS if live(lag + 1)]
                for layer, t in mixed:
                    dve.wait_ge(s["off"][layer], done(t))
                    dve.wait_ge(s["keep"][layer], done(t))
                    nc.vector.tensor_tensor(mix[:, layer, 1 - k], mix[:, layer, 1 - k], keep[:, layer, 1 - k],
                                            ALU.mult).then_inc(s["gated"][layer], 1)
                for layer, t in mixed:
                    dve.wait_ge(s["gated"][layer], done(t))
                    to = h[1][:, cols(t)] if layer == 0 else mix[:, 1, 1 - k]
                    nc.vector.tensor_tensor(to, mix[:, layer, 1 - k], h[layer][:, cols(t)], ALU.add
                                            ).then_inc(s["h"][layer], 1)
                if live(LAYERS[1][1]):
                    feed(*scanned[-1])
                for layer, t in scanned:
                    dve.wait_ge(s["fed"][layer], done(t))
                    dve.wait_ge(s["update"][layer], done(t))
                    nc.vector.tensor_tensor(value[:, layer, k], value[:, layer, k], update[:, layer, k], ALU.mult
                                            ).then_inc(s["value"][layer], 1)
                for layer, t in scanned:
                    dve.wait_ge(s["value"][layer], done(t))
                    dve.wait_ge(s["gate"][layer], done(t))
                    dve.wait_ge(s["off"][layer], freed(t))
                    start = 0.0 if k == 0 else scan[:, layer, 0, CH - 1:CH]
                    if k == 1:
                        dve.wait_ge(s["scan"][layer], freed(t + 1))
                    nc.vector.tensor_tensor_scan(scan[:, layer, k], gate[:, layer, k], value[:, layer, k], start,
                                                 ALU.mult, ALU.add).then_inc(s["scan"][layer], 1)

            steps(dve, step, CHUNKS, 3)


MOE = ("experts_ready cleared_tile cleared logits biased best "
       "same preferred first chosen turned rows "
       "ranked totals totals_copied running ahead further blocks ends base based slot own_slot slots expert_no clipped "
       "block_expert scattered loaded0 loaded1 columns_turned columns picked up act down out stored0 stored1 "
       "back added")
E = 8
PARTS = 4
TOKEN_TILES = ALL // P
GROUP = 4
PAIRS = -(-(TOKEN_TILES + E - 1) // (2 * GROUP))
BLOCKS = PAIRS * 2 * GROUP


def experts(nc, mem, dram):
    x, mean, ident = mem["x"], mem["mean"], mem["ident"]
    with ExitStack() as ctx:
        def sb(name, shape, dt=F32):
            return ctx.enter_context(nc.sbuf_tensor(f"moe_{name}", shape, dt))

        normed = sb("normed", [P, ALL])
        router = sb("router", [P, E])
        router_b = sb("router_b", [P, E])
        order = sb("order", [P, E])
        before = sb("before", [P, P])
        index = sb("index", [P, BLOCKS])
        going = sb("going", [P, E * TOKEN_TILES])
        w1 = sb("w1", [P, E, PARTS * P])
        w2 = sb("w2", [P, E, PARTS * P])
        b1 = sb("b1", [P, E, PARTS])
        b2 = sb("b2", [1, E, P])
        layer_norm(nc, mem, "moe_norm", x, normed, loads=[
            (router[:], dram["router_w"]), (router_b[:], dram["router_b"].partition_broadcast(P)),
            (order[:], dram["order"].partition_broadcast(P)), (before[:], dram["before"]),
            (index[:], dram["index"].partition_broadcast(P)), (going[:], dram["going"].partition_broadcast(P))])
        zeros = sb("zeros", [P, GROUP * P])
        ones = sb("ones", [1, P])
        logits = sb("logits", [P, 2, 4, E])
        best = sb("best", [P, 2, 4])
        chosen = sb("chosen", [P, TOKEN_TILES, E])
        rows = sb("rows", [P, TOKEN_TILES, P])
        total = sb("total", [P, E, TOKEN_TILES])
        running = sb("running", [P, E, TOKEN_TILES])
        ahead = sb("ahead", [P, E, TOKEN_TILES])
        further = sb("further", [P, E, TOKEN_TILES])
        blocks = sb("blocks", [P, E])
        ends = sb("ends", [P, E])
        base = sb("base", [P, E])
        own_slot = sb("own_slot", [P, TOKEN_TILES])
        slots = sb("slots", [P, TOKEN_TILES], U32)
        passed = sb("passed", [1, BLOCKS, E])
        expert_no = sb("expert_no", [1, BLOCKS])
        block_expert = sb("block_expert", [1, BLOCKS], U32)
        slot_rows = sb("slot_rows", [P, 2, GROUP, P])
        columns = sb("columns", [P, 2, GROUP * P])
        w1_now = sb("w1_now", [P, 4, PARTS * P])
        w2_now = sb("w2_now", [P, 4, PARTS * P])
        b1_now = sb("b1_now", [P, 4, PARTS])
        b2_now = sb("b2_now", [1, 4, P])
        hidden = sb("hidden", [P, 2, PARTS, P])
        out_rows = sb("out_rows", [P, 2, GROUP, P])
        to_experts = nc.dram_tensor("moe_to_experts", (BLOCKS * P, P), F32, kind="Internal").ap()
        from_experts = nc.dram_tensor("moe_from_experts", (BLOCKS * P, P), F32, kind="Internal").ap()
        bank = [ctx.enter_context(nc.psum_tensor(f"moe_bank{n}", [P, CH], F32)) for n in range(8)]
        s = dict(zip(MOE.split(), semaphores(ctx, nc, "moe", MOE)))
        loaded, stored = (s["loaded0"], s["loaded1"]), (s["stored0"], s["stored1"])
        (expert_weights,) = semaphores(ctx, nc, "moe", "expert_weights")
        returned = semaphores(ctx, nc, "moe", " ".join(f"returned{n}" for n in range(2 * SEQS)))
        block = ctx.enter_context(nc.Block())

        def group_of(scratch, n):
            return scratch[n * GROUP * P:(n + 1) * GROUP * P].rearrange("(j p) d -> p j d", p=P)

        @block.sync
        def _(sp):
            sp.wait_ge(s["cleared_tile"], 1)
            for n in range(2 * PAIRS):
                sp.dma_start(group_of(to_experts, n), zeros[:].rearrange("p (j d) -> p j d", j=GROUP)
                             ).then_inc(s["cleared"], 16)
            loads = [(b1[:], dram["moe_b1"]), (b2[:], dram["moe_b2"])]
            for e in range(E):
                loads += [(w1[:, e], dram["moe_w1"][e]),
                           (w2[:, e].rearrange("p (c n) -> p c n", n=P),
                            dram["moe_w2"][e].rearrange("(c p) n -> p c n", p=P))]
            for to, of in loads:
                sp.dma_start(to, of).then_inc(expert_weights, 16)
            sp.wait_ge(expert_weights, 16 * len(loads))
            sp.sem_inc(s["experts_ready"], 1)
            sp.wait_ge(s["scattered"], 16 * TOKEN_TILES)
            for n in range(2 * PAIRS + 2):
                if n < 2 * PAIRS:
                    if n >= 2:
                        sp.wait_ge(s["columns_turned"], n - 1 + PRIME)
                    sp.dma_start(slot_rows[:, n % 2], group_of(to_experts, n)).then_inc(loaded[n % 2], 16)
                if n >= 2:
                    sp.wait_ge(s["out"], n - 1 + PRIME)
                    sp.dma_start(group_of(from_experts, n - 2), out_rows[:, n % 2]).then_inc(stored[n % 2], 16)
            for n in range(2):
                sp.wait_ge(stored[n], 16 * (1 + PAIRS))

        @block.tensor
        def _(pe):
            for name in "logits turned columns_turned up down".split():
                pe.sem_inc(s[name], PRIME)
            for t in range(2 * SEQS):
                k = t % 2
                if t >= 2:
                    pe.wait_ge(s["biased"], freed(t))
                for j in range(4):
                    last = nc.tensor.matmul(bank[4 + k][:, j * E:(j + 1) * E], normed[:, cols(4 * t + j, P)],
                                            router[:], start=True, stop=True)
                last.then_inc(s["logits"], 1)
                if t >= 2:
                    pe.wait_ge(s["rows"], freed(t))
                for j in range(4):
                    last = nc.tensor.transpose(bank[6 + k][:, j * P:(j + 1) * P], normed[:, cols(4 * t + j, P)],
                                               ident[:])
                last.then_inc(s["turned"], 1)
            pe.wait_ge(s["chosen"], done(2 * SEQS - 1))
            everyone = chosen[:].rearrange("p t e -> p (t e)")
            nc.tensor.matmul(bank[0][:, 0:TOKEN_TILES * E], before[:], everyone, start=True, stop=True
                             ).then_inc(s["ranked"], 1)
            nc.tensor.matmul(bank[1][:, 0:TOKEN_TILES * E], mean[:], everyone, start=True, stop=True
                             ).then_inc(s["totals"], 1)
            pe.wait_ge(s["slots"], 1)
            with pe.Fori(0, PAIRS) as b:
                for g in range(2):
                    n = b * 2 + g
                    pe.wait_ge(loaded[g], b * 16 + 16)
                    pe.wait_ge(s["columns"], freed(n))
                    for j in range(GROUP):
                        last = nc.tensor.transpose(bank[g][:, j * P:(j + 1) * P], slot_rows[:, g, j], ident[:])
                    last.then_inc(s["columns_turned"], 1)
                for m in range(2 * GROUP + 1):
                    if m < 2 * GROUP:
                        i = b * 2 * GROUP + m
                        g, j = divmod(m, GROUP)
                        if j == 0:
                            pe.wait_ge(s["columns"], done(b * 2 + g))
                        pe.wait_ge(s["picked"], done(i))
                        pe.wait_ge(s["act"], freed(i))
                        for c in range(PARTS):
                            last = nc.tensor.matmul(bank[2 + m % 2][:, c * P:(c + 1) * P],
                                                    w1_now[:, m % 4, c * P:(c + 1) * P],
                                                    columns[:, g, j * P:(j + 1) * P], start=True, stop=True)
                        last.then_inc(s["up"], 1)
                    if m >= 1:
                        i = b * 2 * GROUP + m - 1
                        g, j = divmod(m - 1, GROUP)
                        if j == 0:
                            pe.wait_ge(s["out"], freed(b * 2 + g))
                        pe.wait_ge(s["act"], done(i))
                        to = bank[4 + g][:, j * P:(j + 1) * P]
                        for c in range(PARTS):
                            nc.tensor.matmul(to, hidden[:, (m - 1) % 2, c], w2_now[:, (m - 1) % 4, c * P:(c + 1) * P],
                                             start=c == 0, stop=False)
                        nc.tensor.matmul(to, ones[:], b2_now[:, (m - 1) % 4], start=False, stop=True
                                         ).then_inc(s["down"], 1)
            for t in range(2 * SEQS):
                pe.wait_ge(returned[t], 16 * 4)
                if t >= 2:
                    pe.wait_ge(s["added"], t - 1)
                for j in range(4):
                    last = nc.tensor.transpose(bank[6 + t % 2][:, j * P:(j + 1) * P], rows[:, 4 * t + j], ident[:])
                last.then_inc(s["back"], 1)

        @block.scalar
        def _(act):
            for name in "columns act out".split():
                act.sem_inc(s[name], PRIME)
            for n in range(2):
                act.sem_inc(stored[n], 16)
            act.preload_act_table_set("gelu_and_others")
            with act.Fori(0, PAIRS) as b:
                def result(g):
                    act.wait_ge(s["down"], done(b * 2 * GROUP + g * GROUP + GROUP - 1))
                    act.wait_ge(stored[g], b * 16 + 16)
                    nc.scalar.activation(out_rows[:, g], bank[4 + g][:].rearrange("p (j d) -> p j d", j=GROUP),
                                         ACT.Copy).then_inc(s["out"], 1)

                for g in range(2):
                    act.wait_ge(s["columns_turned"], done(b * 2 + g))
                    nc.scalar.activation(columns[:, g], bank[g][:], ACT.Copy).then_inc(s["columns"], 1)
                for m in range(2 * GROUP):
                    i = b * 2 * GROUP + m
                    act.wait_ge(s["up"], done(i))
                    act.wait_ge(s["down"], freed(i))
                    for c in range(PARTS):
                        last = nc.scalar.activation(hidden[:, m % 2, c], bank[2 + m % 2][:, c * P:(c + 1) * P],
                                                    ACT.Gelu, bias=b1_now[:, m % 4, c:c + 1])
                    last.then_inc(s["act"], 1)
                    if m == GROUP + 1:
                        result(0)
                result(1)

        @block.gpsimd
        def _(pool):
            pool.wait_ge(s["slots"], 1)
            pool.wait_ge(s["cleared"], 16 * 2 * PAIRS)
            pool.wait_ge(s["rows"], done(2 * SEQS - 1))
            for n in range(TOKEN_TILES):
                nc.gpsimd.indirect_dma_start(to_experts, bass.IndirectOffsetOnAxis(slots[:, n:n + 1], 0),
                                             rows[:, n], None).then_inc(s["scattered"], 16)
            pool.wait_ge(s["scattered"], 16 * TOKEN_TILES)
            for n in range(2):
                pool.wait_ge(stored[n], 16 * (1 + PAIRS))
            for n in range(TOKEN_TILES):
                nc.gpsimd.indirect_dma_start(rows[:, n], None, from_experts,
                                             bass.IndirectOffsetOnAxis(slots[:, n:n + 1], 0)
                                             ).then_inc(returned[n // 4], 16)

        @block.vector
        def _(dve):
            for name in "biased best same preferred first chosen rows picked".split():
                dve.sem_inc(s[name], PRIME)
            nc.vector.memset(ones[:], 1.0)
            nc.vector.memset(zeros[:], 0.0).then_inc(s["cleared_tile"], 1)
            with dve.Fori(0, SEQS) as b:
                for k in range(2):
                    t = b * 2 + k
                    dve.wait_ge(s["logits"], done(t))
                    dve.wait_ge(s["chosen"], freed(t))
                    nc.vector.tensor_tensor(logits[:, k], bank[4 + k][:, 0:4 * E].rearrange("p (j e) -> p j e", e=E),
                                            router_b[:].unsqueeze(1).broadcast_to([P, 4, E]), ALU.add
                                            ).then_inc(s["biased"], 1)
                for k in range(2):
                    t = b * 2 + k
                    dve.wait_ge(s["biased"], done(t))
                    nc.vector.tensor_reduce(best[:, k], logits[:, k], AX_X, ALU.max).then_inc(s["best"], 1)
                for k in range(2):
                    t = b * 2 + k
                    dve.wait_ge(s["best"], done(t))
                    nc.vector.tensor_tensor(logits[:, k], logits[:, k], best[:, k].unsqueeze(2).broadcast_to([P, 4, E]),
                                            ALU.is_equal).then_inc(s["same"], 1)
                for k in range(2):
                    t = b * 2 + k
                    dve.wait_ge(s["same"], done(t))
                    nc.vector.tensor_tensor(logits[:, k], logits[:, k],
                                            order[:].unsqueeze(1).broadcast_to([P, 4, E]), ALU.mult
                                            ).then_inc(s["preferred"], 1)
                for k in range(2):
                    t = b * 2 + k
                    dve.wait_ge(s["preferred"], done(t))
                    nc.vector.tensor_reduce(best[:, k], logits[:, k], AX_X, ALU.max).then_inc(s["first"], 1)
                for k in range(2):
                    t = b * 2 + k
                    dve.wait_ge(s["first"], done(t))
                    nc.vector.tensor_tensor(chosen[:, bass.ds(t * 4, 4)], logits[:, k],
                                            best[:, k].unsqueeze(2).broadcast_to([P, 4, E]), ALU.is_equal
                                            ).then_inc(s["chosen"], 1)
                for k in range(2):
                    t = b * 2 + k
                    dve.wait_ge(s["turned"], done(t))
                    nc.vector.tensor_scalar(rows[:, bass.ds(t * 4, 4)],
                                            bank[6 + k][:].rearrange("p (j d) -> p j d", j=4), 1.0, None, ALU.mult
                                            ).then_inc(s["rows"], 1)

            def by_expert(ap):
                return ap.rearrange("p (t e) -> p e t", e=E)

            def flat(ap):
                return ap[:].rearrange("p e t -> p (e t)")

            dve.wait_ge(s["totals"], 1)
            nc.vector.tensor_copy(total[:], by_expert(bank[1][:, 0:TOKEN_TILES * E])).then_inc(s["totals_copied"], 1)
            dve.wait_ge(s["totals_copied"], 1)
            nc.vector.tensor_tensor_scan(flat(running), going[:], flat(total), 0.0, ALU.mult, ALU.add
                                         ).then_inc(s["running"], 1)
            dve.wait_ge(s["running"], 1)
            nc.vector.tensor_tensor(ahead[:], running[:], total[:], ALU.subtract).then_inc(s["ahead"], 1)
            nc.vector.tensor_tensor(further[:], running[:, :, TOKEN_TILES - 1:].broadcast_to([P, E, TOKEN_TILES]),
                                    index[:, 0:TOKEN_TILES].unsqueeze(1).broadcast_to([P, E, TOKEN_TILES]), ALU.is_gt
                                    ).then_inc(s["further"], 1)
            dve.wait_ge(s["further"], 1)
            nc.vector.tensor_reduce(blocks[:], further[:], AX_X, ALU.add).then_inc(s["blocks"], 1)
            dve.wait_ge(s["blocks"], 1)
            nc.vector.tensor_tensor_scan(ends[:], going[:, 1:1 + E], blocks[:], 0.0, ALU.mult, ALU.add
                                         ).then_inc(s["ends"], 1)
            dve.wait_ge(s["ends"], 1)
            nc.vector.tensor_tensor(base[:], ends[:], blocks[:], ALU.subtract).then_inc(s["base"], 1)
            dve.wait_ge(s["base"], 1)
            dve.wait_ge(s["ahead"], 1)
            nc.vector.tensor_tensor(ahead[:], ahead[:], base[:].unsqueeze(2).broadcast_to([P, E, TOKEN_TILES]),
                                    ALU.add).then_inc(s["based"], 1)
            dve.wait_ge(s["based"], 1)
            dve.wait_ge(s["ranked"], 1)
            nc.vector.scalar_tensor_tensor(ahead[:], ahead[:], float(P), by_expert(bank[0][:, 0:TOKEN_TILES * E]),
                                           ALU.mult, ALU.add).then_inc(s["slot"], 1)
            dve.wait_ge(s["slot"], 1)
            nc.vector.tensor_tensor(ahead[:], ahead[:], chosen[:].rearrange("p t e -> p e t"), ALU.mult
                                    ).then_inc(s["slot"], 1)
            dve.wait_ge(s["slot"], 2)
            nc.vector.tensor_reduce(own_slot[:], ahead[:].rearrange("p e t -> p t e"), AX_X, ALU.add
                                    ).then_inc(s["own_slot"], 1)
            dve.wait_ge(s["own_slot"], 1)
            nc.vector.tensor_copy(slots[:], own_slot[:]).then_inc(s["slots"], 1)
            nc.vector.tensor_tensor(passed[:], index[0:1].unsqueeze(2).broadcast_to([1, BLOCKS, E]),
                                    ends[0:1].unsqueeze(1).broadcast_to([1, BLOCKS, E]), ALU.is_ge
                                    ).then_inc(s["expert_no"], 1)
            dve.wait_ge(s["expert_no"], 1)
            nc.vector.tensor_reduce(expert_no[:], passed[:], AX_X, ALU.add).then_inc(s["expert_no"], 1)
            dve.wait_ge(s["expert_no"], 2)
            nc.vector.tensor_scalar(expert_no[:], expert_no[:], float(E - 1), None, ALU.min
                                    ).then_inc(s["clipped"], 1)
            dve.wait_ge(s["clipped"], 1)
            nc.vector.tensor_copy(block_expert[:], expert_no[:]).then_inc(s["block_expert"], 1)
            dve.wait_ge(s["block_expert"], 1)
            dve.wait_ge(s["experts_ready"], 1)
            with dve.Fori(0, PAIRS) as b:
                for m in range(2 * GROUP):
                    i = b * 2 * GROUP + m
                    half = m % 4
                    dve.wait_ge(s["up"], freed(i))
                    e = dve.value_load(block_expert[0:1, bass.ds(i, 1)], min_val=0, max_val=E - 1)
                    nc.vector.tensor_copy(w1_now[:, half], w1[:, bass.ds(e, 1)])
                    nc.vector.tensor_copy(b1_now[:, half], b1[:, bass.ds(e, 1)])
                    nc.vector.tensor_copy(b2_now[:, half], b2[:, bass.ds(e, 1)])
                    nc.vector.tensor_copy(w2_now[:, half], w2[:, bass.ds(e, 1)]).then_inc(s["picked"], 1)
            for t in range(2 * SEQS):
                dve.wait_ge(s["back"], t + 1)
                nc.vector.tensor_tensor(x[:, t * CH:(t + 1) * CH], x[:, t * CH:(t + 1) * CH], bank[6 + t % 2][:],
                                        ALU.add).then_inc(s["added"], 1)


SSM = ("folded zeroed decay decay_ready uz raw tap z conv0 conv1 "
       "conv u dbc dt_low hi rest1 mid rest2 parts dtraw size small over dtlog dt dtu b c b_all da dbu "
       "state carried seen y summed gated out branch")


def mamba(nc, mem, dram):
    ident, branch = mem["ident"], mem["branch"]
    STATES = 16
    STEPS = 2 * STATES
    SUM, GATE, PROJECT, ADD = 3, 5, 7, 9
    with ExitStack() as ctx:
        def sb(name, shape, dt=F32):
            return ctx.enter_context(nc.sbuf_tensor(f"ssm_{name}", shape, dt))

        dt = sb("dt", [P, 2, ALL])
        x0 = dt[:, 0]
        in_w = sb("in_w", [P, 4 * P])
        dbc_w = sb("dbc_w", [P, 2, P])
        dt_w = sb("dt_w", [40, 2 * P])
        out_w = sb("out_w", [P, 2, P])
        pick = sb("pick", [P, 2 * STATES, P], BF16)
        rms_w = sb("rms_w", [P, 1])
        conv_w = sb("conv_w", [P, 2, 4])
        conv_b = sb("conv_b", [P, 2])
        dt_b = sb("dt_b", [P, 2])
        skip = sb("skip", [P, 2])
        a_log = sb("a_log", [P, 2, STATES])
        decay = sb("decay", [P, 2, STATES])
        layer_norm(nc, mem, "ssm_norm", mem["x"], branch, rms_into=x0, loads=[(to[:], dram[name]) for to, name in (
            (in_w, "in_w"), (dbc_w, "dbc_w"), (out_w, "out_w"), (pick, "pick"), (rms_w, "rms1"),
            (conv_w, "conv_w"), (conv_b, "conv_b"), (dt_b, "dt_b"), (skip, "skip"), (a_log, "a_log"))]
            + [(dt_w[32:40], dram["dt_w"])])
        u = sb("u", [P, 2, ALL])
        z = sb("z", [P, 2, ALL])
        parts = sb("parts", [P, ALL], BF16)
        dtu = sb("dtu", [P, 2, 2, CH])
        b_all = sb("b_all", [P, 2, CH])
        da = sb("da", [P, 2, 2, CH])
        dbu = sb("dbu", [P, 2, 2, CH])
        state = sb("state", [P, 2, 2, CH])
        carry = sb("carry", [P, STATES, 2])
        shared = sb("shared", [P, 2, 4 * CH])
        seen = shared[:, 0].rearrange("p (a h c) -> p a h c", a=2, h=2)
        y = shared[:, 1].rearrange("p (a h c) -> p a h c", a=2, h=2)
        raw = shared[:, :, 0:3 + T]
        conv = state
        dt_low = b_all[32:64]
        rest = dtu[:, 0]
        size = seen
        bank = [ctx.enter_context(nc.psum_tensor(f"ssm_bank{n}", [P, CH], F32)) for n in range(8)]
        s = dict(zip(SSM.split(), semaphores(ctx, nc, "ssm", SSM)))
        block = ctx.enter_context(nc.Block())

        @block.tensor
        def _(pe):
            for name in "uz dbc dtraw b c y out".split():
                pe.sem_inc(s[name], PRIME)
            pe.wait_ge(s["folded"], 1)
            with pe.Fori(0, SEQS) as b:
                for k in range(2):
                    t = b * 2 + k
                    pe.wait_ge(s["z"], freed(t))
                    for m in range(4):
                        last = nc.tensor.matmul(bank[4 * k + m][:], in_w[:, m * P:(m + 1) * P], x0[:, cols(t)],
                                                start=True, stop=True)
                    last.then_inc(s["uz"], 1)
            pe.wait_ge(s["z"], done(2 * SEQS - 1))
            pe.wait_ge(s["u"], done(2 * SEQS - 1))
            with pe.Fori(0, SEQS) as b:
                for k in range(2):
                    t = b * 2 + k
                    pe.wait_ge(s["rest1"], freed(t))
                    for half in range(2):
                        last = nc.tensor.matmul(bank[k][:], dbc_w[:, half], u[:, half, cols(t)],
                                                start=half == 0, stop=half == 1)
                    last.then_inc(s["dbc"], 1)
                for k in range(2):
                    t = b * 2 + k
                    pe.wait_ge(s["dt_low"], done(t))
                    pe.wait_ge(s["dt"], freed(t))
                    for half in range(2):
                        last = nc.tensor.matmul(bank[2 + 2 * k + half][:], dt_w[32:40, half * P:(half + 1) * P],
                                                dt_low[:, k][0:8], start=True, stop=True)
                    last.then_inc(s["dtraw"], 1)
            pe.wait_ge(s["parts"], done(2 * SEQS - 1))
            pe.wait_ge(s["dt"], done(2 * SEQS - 1))

            def step(b, m, live):
                i = b * STEPS + m
                if live(0):
                    pe.wait_ge(s["b_all"], freed(i))
                    nc.tensor.matmul(bank[m % 2][:], pick[:, m % STATES], parts[:, cols(b * 2 + m // STATES)],
                                     start=True, stop=True).then_inc(s["b"], 1)
                if live(1):
                    pe.wait_ge(s["seen"], freed(i - 1))
                    nc.tensor.matmul(bank[2 + (m - 1) % 2][:], pick[:, STATES + (m - 1) % STATES],
                                     parts[:, cols(b * 2 + (m - 1) // STATES)],
                                     start=True, stop=True).then_inc(s["c"], 1)
                if live(SUM):
                    t, n = b * 2 + (m - SUM) // STATES, (m - SUM) % STATES
                    k = (m - SUM) // STATES % 2
                    pe.wait_ge(s["seen"], done(i - SUM))
                    if n == 0:
                        pe.wait_ge(s["branch"], freed(t))
                    for half in range(2):
                        last = nc.tensor.matmul(bank[4 + 2 * k + half][:], ident[:], seen[:, n % 2, half],
                                                start=n == 0, stop=n == STATES - 1)
                    last.then_inc(s["y"], 1)
                if live(PROJECT) and (m - PROJECT) % STATES == STATES - 1:
                    t, k = b * 2 + (m - PROJECT) // STATES, (m - PROJECT) // STATES % 2
                    pe.wait_ge(s["gated"], done(t))
                    for half in range(2):
                        last = nc.tensor.matmul(bank[4 + 2 * k][:], out_w[:, half], y[:, k, half],
                                                start=half == 0, stop=half == 1)
                    last.then_inc(s["out"], 1)

            steps(pe, step, STEPS, ADD)

        @block.scalar
        def _(act):
            for name in "raw tap z u dt_low hi size small dtlog b_all da".split():
                act.sem_inc(s[name], PRIME)
            act.preload_act_table_set("natural_log_exp_and_others")
            nc.scalar.activation(decay[:], a_log[:], ACT.Exp).then_inc(s["decay"], 1)
            act.preload_act_table_set("silu_and_others")
            act.wait_ge(s["zeroed"], 1)

            def step(b, k, live):
                t = b * 2 + k
                if live(0):
                    act.wait_ge(s["uz"], done(t))
                    act.wait_ge(s["conv"], freed(t + 1 - k))
                    for half in range(2):
                        last = nc.scalar.activation(raw[:, half, 3 + k * CH:3 + (k + 1) * CH],
                                                    bank[4 * k + half][:], ACT.Copy)
                    last.then_inc(s["raw"], 1)
                    act.wait_ge(s["u"], freed(t))
                    for half in range(2):
                        last = nc.scalar.activation(conv[:, k, half], bank[4 * k + half][:], ACT.Identity,
                                                    scale=conv_w[:, half, 3:4], bias=conv_b[:, half:half + 1])
                    last.then_inc(s["tap"], 1)
                    for half in range(2):
                        last = nc.scalar.activation(z[:, half, cols(t)], bank[4 * k + 2 + half][:], ACT.Silu)
                    last.then_inc(s["z"], 1)
                if live(1):
                    act.wait_ge(s["conv"], done(t - 1))
                    act.wait_ge(s["zeroed"], 1)
                    for half in range(2):
                        last = nc.scalar.activation(u[:, half, cols(t - 1)], conv[:, 1 - k, half], ACT.Silu)
                    last.then_inc(s["u"], 1)

            steps(act, step, 2, 1)
            act.preload_act_table_set("natural_log_exp_and_others")
            with act.Fori(0, SEQS) as b:
                for k in range(2):
                    t = b * 2 + k
                    act.wait_ge(s["dbc"], done(t))
                    act.wait_ge(s["dtraw"], freed(t))
                    nc.scalar.activation(dt_low[:, k], bank[k][32:64, :], ACT.Copy).then_inc(s["dt_low"], 1)
                    nc.scalar.activation(parts[:, cols(t)], bank[k][:], ACT.Copy).then_inc(s["hi"], 1)
                for k in range(2):
                    t = b * 2 + k
                    act.wait_ge(s["dtraw"], done(t))
                    act.wait_ge(s["dt"], freed(t))
                    for half in range(2):
                        last = nc.scalar.activation(size[:, k, half], bank[2 + 2 * k + half][:], ACT.Abs,
                                                    bias=dt_b[:, half:half + 1])
                    last.then_inc(s["size"], 1)
                    act.wait_ge(s["size"], done(t))
                    nc.scalar.activation(size[:, k], size[:, k], ACT.Exp, scale=-1.0).then_inc(s["small"], 1)
                    act.wait_ge(s["small"], done(t))
                    nc.scalar.activation(size[:, k], size[:, k], ACT.Ln, bias=1.0).then_inc(s["dtlog"], 1)
            act.wait_ge(s["decay_ready"], 1)
            act.wait_ge(s["dtraw"], done(2 * SEQS - 1))
            with act.Fori(0, SEQS) as b:
                for m in range(STEPS):
                    i = b * STEPS + m
                    k, n = divmod(m, STATES)
                    act.wait_ge(s["b"], done(i))
                    act.wait_ge(s["dbu"], freed(i))
                    act.wait_ge(s["state"], freed(i))
                    nc.scalar.activation(b_all[:, m % 2], bank[m % 2][:], ACT.Copy).then_inc(s["b_all"], 1)
                    for half in range(2):
                        last = nc.scalar.activation(da[:, n % 2, half], dt[:, half, cols(b * 2 + k)],
                                                    ACT.Exp, scale=decay[:, half, n:n + 1])
                    last.then_inc(s["da"], 1)

        @block.gpsimd
        def _(pool):
            for name in "dtu dbu".split():
                pool.sem_inc(s[name], PRIME)
            pool.wait_ge(s["parts"], done(2 * SEQS - 1))
            pool.wait_ge(s["dt"], done(2 * SEQS - 1))

            def increments(t, k):
                nc.gpsimd.tensor_tensor(dtu[:, k], dt[:, :, cols(t)], u[:, :, cols(t)], ALU.mult
                                        ).then_inc(s["dtu"], 1)

            def sequence(b, more):
                for m in range(STEPS):
                    i = b * STEPS + m
                    k, n = divmod(m, STATES)
                    if n == 0:
                        pool.wait_ge(s["dtu"], done(b * 2 + k))
                    if n == STATES // 2 and (k == 0 or more):
                        increments(b * 2 + k + 1, 1 - k)
                    pool.wait_ge(s["b_all"], done(i))
                    pool.wait_ge(s["state"], freed(i))
                    nc.gpsimd.tensor_tensor(dbu[:, n % 2], dtu[:, k],
                                            b_all[:, n % 2:n % 2 + 1, :].broadcast_to([P, 2, CH]), ALU.mult
                                            ).then_inc(s["dbu"], 1)

            increments(0, 0)
            with pool.Fori(0, SEQS - 1) as b:
                sequence(b, True)
            sequence(SEQS - 1, False)

        @block.vector
        def _(dve):
            for name in ("conv0 conv1 conv rest1 mid rest2 parts over dt state carried seen "
                         "summed gated branch").split():
                dve.sem_inc(s[name], PRIME)
            nc.vector.memset(raw[:, :, 0:3], 0.0).then_inc(s["zeroed"], 1)
            nc.vector.tensor_scalar(in_w[:], in_w[:], rms_w[:, 0:1], None, ALU.mult).then_inc(s["folded"], 1)
            dve.wait_ge(s["decay"], 1)
            nc.vector.tensor_scalar(decay[:], decay[:], -1.0, None, ALU.mult).then_inc(s["decay_ready"], 1)
            with dve.Fori(0, SEQS) as b:
                for k in range(2):
                    t = b * 2 + k
                    dve.wait_ge(s["tap"], done(t))
                    for tap, finished in ((2, "conv0"), (1, "conv1"), (0, "conv")):
                        for half in range(2):
                            at = raw[:, half, k * CH + tap:k * CH + tap + CH]
                            last = nc.vector.scalar_tensor_tensor(conv[:, k, half], at,
                                                                  conv_w[:, half, tap:tap + 1],
                                                                  conv[:, k, half], ALU.mult, ALU.add)
                        last.then_inc(s[finished], 1)
                        if tap:
                            dve.wait_ge(s[finished], done(t))
            with dve.Fori(0, SEQS) as b:
                for k in range(2):
                    t = b * 2 + k
                    dve.wait_ge(s["hi"], done(t))
                    nc.vector.tensor_tensor(rest[64:128, k], bank[k][64:128, :], parts[64:128, cols(t)], ALU.subtract
                                            ).then_inc(s["rest1"], 1)
                    dve.wait_ge(s["rest1"], done(t))
                    nc.vector.tensor_scalar(parts[64:128, cols(t)], rest[64:128, k], 1.0, None, ALU.mult).then_inc(s["mid"], 1)
                    dve.wait_ge(s["mid"], done(t))
                    nc.vector.tensor_tensor(rest[96:128, k], rest[96:128, k], parts[96:128, cols(t)], ALU.subtract
                                            ).then_inc(s["rest2"], 1)
                    dve.wait_ge(s["rest2"], done(t))
                    nc.vector.tensor_scalar(parts[96:128, cols(t)], rest[96:128, k], 1.0, None, ALU.mult).then_inc(s["parts"], 1)
                for k in range(2):
                    t = b * 2 + k
                    dve.wait_ge(s["size"], done(t))
                    for half in range(2):
                        last = nc.vector.tensor_scalar(dt[:, half, cols(t)], bank[2 + 2 * k + half][:],
                                                       dt_b[:, half:half + 1], 0.0, ALU.add, ALU.max)
                    last.then_inc(s["over"], 1)
                    dve.wait_ge(s["over"], done(t))
                    dve.wait_ge(s["dtlog"], done(t))
                    nc.vector.tensor_tensor(dt[:, :, cols(t)], dt[:, :, cols(t)], size[:, k], ALU.add
                                            ).then_inc(s["dt"], 1)

            def chunk_end(t, k):
                dve.wait_ge(s["y"], done(t * STATES + STATES - 1))
                for half in range(2):
                    nc.vector.scalar_tensor_tensor(y[:, k, half], u[:, half, cols(t)], skip[:, half:half + 1],
                                                   bank[4 + 2 * k + half][:], ALU.mult, ALU.add
                                                   ).then_inc(s["summed"], 1)
                    dve.wait_ge(s["summed"], done(t * 2 + half))
                    last = nc.vector.tensor_tensor(y[:, k, half], y[:, k, half], z[:, half, cols(t)], ALU.mult)
                last.then_inc(s["gated"], 1)

            def projected(t, k):
                dve.wait_ge(s["out"], done(t))
                nc.vector.tensor_tensor(branch[:, cols(t)], branch[:, cols(t)], bank[4 + 2 * k][:], ALU.add
                                        ).then_inc(s["branch"], 1)

            def step(b, m, live):
                for lag, then in ((GATE, chunk_end), (ADD, projected)):
                    if live(lag) and (m - lag) % STATES == STATES - 1:
                        then(b * 2 + (m - lag) // STATES, (m - lag) // STATES % 2)
                if not live(0):
                    return
                k, n = divmod(m, STATES)
                i = b * STEPS + m
                dve.wait_ge(s["da"], done(i))
                dve.wait_ge(s["dbu"], done(i))
                if k == 1:
                    dve.wait_ge(s["carried"], b * STATES + n + 1 + PRIME)
                for half in range(2):
                    start = 0.0 if k == 0 else carry[:, n, half:half + 1]
                    last = nc.vector.tensor_tensor_scan(state[:, n % 2, half], da[:, n % 2, half],
                                                        dbu[:, n % 2, half], start, ALU.mult, ALU.add)
                last.then_inc(s["state"], 1)
                dve.wait_ge(s["state"], done(i))
                dve.wait_ge(s["c"], done(i))
                dve.wait_ge(s["y"], freed(i))
                nc.vector.tensor_tensor(seen[:, n % 2], state[:, n % 2],
                                        bank[2 + n % 2][:].unsqueeze(1).broadcast_to([P, 2, CH]),
                                        ALU.mult).then_inc(s["seen"], 1)
                if k == 0:
                    nc.vector.tensor_copy(carry[:, n], state[:, n % 2, :, CH - 1]).then_inc(s["carried"], 1)

            steps(dve, step, STEPS, ADD)


def mlp(nc, mem, dram):
    x, mean, branch = mem["x"], mem["mean"], mem["branch"]
    with ExitStack() as ctx:
        def sb(name, shape, dt=F32):
            return ctx.enter_context(nc.sbuf_tensor(f"mlp_{name}", shape, dt))

        fc1 = sb("fc1", [P, 2, P])
        fc2 = sb("fc2", [P, 2, 2, P])
        fc3 = sb("fc3", [P, 2, P])
        rms_w = sb("rms_w", [P, 1])
        bias = sb("bias", [P, 5])
        square = sb("square", [P, 2, CH])
        log = sb("log", [P, 2, CH])
        rstd = sb("rstd", [P, 2, CH])
        normed = sb("normed", [P, 2, CH])
        hidden = [sb(f"hidden{n}", [P, 2, 2, CH]) for n in range(2)]
        bank = [ctx.enter_context(nc.psum_tensor(f"mlp_bank{n}", [P, CH], F32)) for n in range(8)]
        (weights, folded, sq, power, lg, rs, nm, up, act1, mid, act2, down, first, xd) = semaphores(
            ctx, nc, "mlp", "weights folded square power log rstd normed up hidden0 mid hidden1 down first x")
        block = ctx.enter_context(nc.Block())

        @block.sync
        def _(sp):
            for to, name in ((fc1[:], "fc1"), (fc2[:], "fc2"), (fc3[:], "fc3"), (rms_w[:], "rms2"), (bias[:], "mlp_b")):
                sp.dma_start(to, dram[name]).then_inc(weights, 16)
            sp.wait_ge(weights, 80)

        @block.tensor
        def _(pe):
            for n in (power, up, mid, down):
                pe.sem_inc(n, PRIME)
            pe.wait_ge(folded, 1)
            with pe.Fori(0, SEQS) as b:
                for k in range(2):
                    t = b * 2 + k
                    pe.wait_ge(sq, done(t))
                    pe.wait_ge(xd, freed(t))
                    nc.tensor.matmul(bank[k][:], mean[:], square[:, k], start=True, stop=True).then_inc(power, 1)
                for k in range(2):
                    t = b * 2 + k
                    pe.wait_ge(nm, done(t))
                    pe.wait_ge(act2, freed(t))
                    for m in range(2):
                        last = nc.tensor.matmul(bank[2 + 2 * k + m][:], fc1[:, m], normed[:, k], start=True, stop=True)
                    last.then_inc(up, 1)
                for k in range(2):
                    t = b * 2 + k
                    pe.wait_ge(act1, done(t))
                    for m in range(2):
                        for c in range(2):
                            last = nc.tensor.matmul(bank[2 + 2 * k + m][:], fc2[:, c, m], hidden[0][:, k, c],
                                                    start=c == 0, stop=c == 1)
                    last.then_inc(mid, 1)
                for k in range(2):
                    t = b * 2 + k
                    pe.wait_ge(act2, done(t))
                    for c in range(2):
                        last = nc.tensor.matmul(bank[k][:], fc3[:, c], hidden[1][:, k, c], start=c == 0, stop=c == 1)
                    last.then_inc(down, 1)

        @block.scalar
        def _(act):
            for n in (sq, lg, rs, act1, act2):
                act.sem_inc(n, PRIME)
            act.wait_ge(weights, 80)
            with act.Fori(0, SEQS) as b:
                for k in range(2):
                    t = b * 2 + k
                    nc.scalar.activation(square[:, k], branch[:, cols(t)], ACT.Square).then_inc(sq, 1)
                for k in range(2):
                    t = b * 2 + k
                    act.wait_ge(power, done(t))
                    nc.scalar.activation(log[:, k], bank[k][:], ACT.Ln, bias=EPS_RMS).then_inc(lg, 1)
                for k in range(2):
                    t = b * 2 + k
                    act.wait_ge(lg, done(t))
                    act.wait_ge(nm, freed(t))
                    nc.scalar.activation(rstd[:, k], log[:, k], ACT.Exp, scale=-0.5).then_inc(rs, 1)
                for k in range(2):
                    t = b * 2 + k
                    act.wait_ge(up, done(t))
                    for m in range(2):
                        last = nc.scalar.activation(hidden[0][:, k, m], bank[2 + 2 * k + m][:], ACT.Relu,
                                                    bias=bias[:, m:m + 1])
                    last.then_inc(act1, 1)
                for k in range(2):
                    t = b * 2 + k
                    act.wait_ge(mid, done(t))
                    act.wait_ge(down, freed(t))
                    for m in range(2):
                        last = nc.scalar.activation(hidden[1][:, k, m], bank[2 + 2 * k + m][:], ACT.Relu,
                                                    bias=bias[:, 2 + m:3 + m])
                    last.then_inc(act2, 1)

        @block.vector
        def _(dve):
            for n in (nm, first, xd):
                dve.sem_inc(n, PRIME)
            dve.wait_ge(weights, 80)
            nc.vector.tensor_scalar(fc1[:], fc1[:], rms_w[:, 0:1], None, ALU.mult).then_inc(folded, 1)
            with dve.Fori(0, SEQS) as b:
                for k in range(2):
                    t = b * 2 + k
                    dve.wait_ge(rs, done(t))
                    dve.wait_ge(up, freed(t))
                    nc.vector.tensor_tensor(normed[:, k], branch[:, cols(t)], rstd[:, k], ALU.mult).then_inc(nm, 1)
                for k in range(2):
                    t = b * 2 + k
                    nc.vector.tensor_tensor(x[:, cols(t)], x[:, cols(t)], branch[:, cols(t)], ALU.add
                                            ).then_inc(first, 1)
                for k in range(2):
                    t = b * 2 + k
                    dve.wait_ge(down, done(t))
                    dve.wait_ge(first, done(t))
                    nc.vector.scalar_tensor_tensor(x[:, cols(t)], bank[k][:], bias[:, 4:5], x[:, cols(t)],
                                                   ALU.add, ALU.add).then_inc(xd, 1)


HEADS = 8
HEAD = 64
WINDOW = 64
INNER = HEADS * HEAD
TILE = 128
TILES = T // TILE
HID = 341
HID_PARTS = [(0, 128), (128, 128), (256, 85)]


def attend_operands(ctx, nc):
    def sb(name, shape, dt=F32):
        return ctx.enter_context(nc.sbuf_tensor(f"at_{name}", shape, dt))

    return {
        "wqkv": sb("wqkv", [P, 3 * INNER]),
        "wo": sb("wo", [P, 4, P]),
        "eye16": sb("eye16", [P, P], BF16),
        "mask": sb("mask", [P, 2, TILE], BF16),
        "turn": sb("turn", [P, 2, TILES, 2, HEAD]),
        "scales": sb("scales", [P, 2, 2, HEAD]),
    }


def attend_loads(mem, dram, layer):
    loads = [(mem["wqkv"][:], dram["wqkv"][layer]),
             (mem["wo"][:], dram["wo"][layer].rearrange("(c p) n -> p c n", p=P)),
             (mem["eye16"][:], dram["eye16"]), (mem["mask"][:], dram["mask"]), (mem["turn"][:], dram["turn"])]
    for n, name in enumerate(("q_scale", "k_scale")):
        row = dram[name][layer:layer + 1]
        loads.append((mem["scales"][:, 0, n], row.partition_broadcast(P)))
        for to, of in ((0, 32), (32, 0)):
            loads.append((mem["scales"][:, 1, n, to:to + 32], row[:, of:of + 32].partition_broadcast(P)))
    return loads


def normalise(nc, mem, dram):
    layer_norm(nc, mem, "norm", mem["x"], mem["branch"], loads=attend_loads(mem, dram, 0))


ATTEND = ("zeroed hs tables_ready proj qk_copied v_copied v_mixed "
          "square sums floor log rnorm direct crossed added scaled qkT qkT_copied "
          "sim peak shifted prob total inv weighted pT pT_copied av oT_copied wo branch")
NORM, SCORE, EXP, VALUE, OUT = 1, 3, 4, 5, 6


def attend(nc, mem, dram, layer):
    branch, ident = mem["branch"], mem["ident"]
    with ExitStack() as ctx:
        def sb(name, shape, dt=F32):
            return ctx.enter_context(nc.sbuf_tensor(f"at{layer}_{name}", shape, dt))

        w, wo, eye16, mask, turn, scales = (
            mem[name] for name in ("wqkv", "wo", "eye16", "mask", "turn", "scales"))
        hs = sb("hs", [P, 1 + T])
        qk = sb("qk", [P, 2, 2 * INNER])
        square = sb("square", [P, 2, 2 * INNER])
        direct = sb("direct", [P, 4, 2 * INNER])
        crossed = square
        sums = sb("sums", [P, 2, 2 * HEADS])
        floor = sb("floor", [P, 2, 2 * HEADS])
        log = sb("log", [P, 2, 2 * HEADS])
        rnorm = sb("rnorm", [P, 2, 2 * HEADS])
        qT = sb("qT", [P, 2, 4, TILE])
        kT = sb("kT", [P, 4, WINDOW + T])
        v = sb("v", [P, TILES, INNER])
        v_mix = sb("v_mix", [P, TILES, INNER])
        peak = sb("peak", [P, 2, HEADS])
        prob = sb("prob", [P, 2, HEADS, TILE])
        pT = sb("pT", [P, HEADS, TILE])
        total = sb("total", [P, 2, HEADS])
        inv = sb("inv", [P, 2, HEADS])
        oT = sb("oT", [P, 2, 4, TILE])
        ps = ctx.enter_context(nc.psum_tensor(f"at{layer}_ps", [P, 8, CH], F32))
        Q, K, V, TURN, SIM, AV = 0, 1, 2, 3, 5, 7
        s = dict(zip(ATTEND.split(), semaphores(ctx, nc, f"at{layer}", ATTEND)))
        block = ctx.enter_context(nc.Block())

        @block.tensor
        def _(pe):
            for name in "proj qkT sim pT av wo".split():
                pe.sem_inc(s[name], PRIME)

            def step(b, i, live):
                g = b * TILES + i
                if live(SCORE):
                    n, at_tile = g - SCORE, (i - SCORE) % TILES
                    pe.wait_ge(s["scaled"], done(n))
                    if live(OUT):
                        pe.wait_ge(s["pT_copied"], done(g - OUT))
                    for m in range(8):
                        last = nc.tensor.transpose(ps[:, TURN + m // 4, (m % 4) * TILE:(m % 4 + 1) * TILE],
                                                   direct[:, at_tile % 4, m * TILE:(m + 1) * TILE], ident[:])
                    last.then_inc(s["qkT"], 1)
                if live(0):
                    if i % 4 == 0:
                        pe.wait_ge(s["hs"], 2 * b + i // 4 + 1)
                    pe.wait_ge(s["qk_copied"], freed(g + 1))
                    pe.wait_ge(s["v_copied"], freed(g + 1))
                    if live(OUT + 1):
                        pe.wait_ge(s["branch"], done(g - OUT - 1))
                    for m, to in enumerate((Q, K, V)):
                        last = nc.tensor.matmul(ps[:, to], hs[:, i * TILE:(i + 1) * TILE],
                                                w[:, m * INNER:(m + 1) * INNER], start=True, stop=True)
                    last.then_inc(s["proj"], 1)
                if live(VALUE):
                    n, half = g - VALUE, (i - VALUE) % 2
                    pe.wait_ge(s["weighted"], done(n))
                    if live(SCORE):
                        pe.wait_ge(s["qkT_copied"], done(g - SCORE))
                    for h in range(HEADS):
                        last = nc.tensor.transpose(ps[:, TURN + h // 4, (h % 4) * TILE:(h % 4 + 1) * TILE],
                                                   prob[:, half, h], ident[:])
                    last.then_inc(s["pT"], 1)
                if live(SCORE):
                    n, at_tile = g - SCORE, (i - SCORE) % TILES
                    pe.wait_ge(s["qkT_copied"], done(n))
                    pe.wait_ge(s["shifted"], freed(n + 1))
                    first = int(at_tile == 0)
                    for parity in range(2):
                        nc.tensor.matmul(ps[:, SIM + parity].rearrange("p (h j) -> p h j", h=4), eye16[:],
                                         mask[:, first:first + 1].broadcast_to([P, 4, TILE]),
                                         start=True, stop=False, skip_group_check=True)
                    windows = at_tile * TILE
                    for pair in range(4):
                        c = pair * TILE
                        for first_window in range(2):
                            for odd in range(2):
                                at = slice(HEAD * odd, HEAD * odd + HEAD)
                                to = slice(c, c + TILE)
                                if (first_window + odd) % 2 == 0:
                                    keys = kT[at, pair, windows:windows + TILE].rearrange("p (w c) -> p w c", w=2)
                                    last = nc.tensor.matmul(
                                        ps[0:64, SIM + odd, to].rearrange("p (w c) -> p w c", w=2),
                                        qT[at, at_tile % 2, pair, 0:64], keys[:, ::-1],
                                        start=False, stop=True, skip_group_check=True)
                                else:
                                    last = nc.tensor.matmul(
                                        ps[64:128, SIM + odd, to], qT[at, at_tile % 2, pair, 64:128],
                                        kT[at, pair, windows + WINDOW:windows + WINDOW + TILE],
                                        start=False, stop=True, skip_group_check=True)
                    last.then_inc(s["sim"], 1)
                if live(OUT):
                    n, half = g - OUT, (i - OUT) % 2
                    pe.wait_ge(s["oT_copied"], done(n))
                    if live(0):
                        pe.wait_ge(s["v_copied"], done(g))
                    else:
                        pe.wait_ge(s["branch"], freed(n + 1))
                    for m in range(4):
                        last = nc.tensor.matmul(ps[:, V, 0:TILE], wo[:, m], oT[:, half, m],
                                                start=m == 0, stop=m == 3)
                    last.then_inc(s["wo"], 1)
                if live(VALUE):
                    n, at_tile = g - VALUE, (i - VALUE) % TILES
                    sequence = b if i >= VALUE else b - 1
                    pe.wait_ge(s["pT_copied"], done(n))
                    pe.wait_ge(s["v_copied"], done(n))
                    pe.wait_ge(s["v_mixed"], sequence * (TILES - 1) + at_tile + PRIME)
                    pe.wait_ge(s["oT_copied"], freed(n + 1))
                    for pair in range(4):
                        for q, values in ((0, v_mix), (1, v)):
                            for odd in range(2):
                                h = 2 * pair + odd
                                to = slice(HEAD * odd, HEAD * odd + HEAD)
                                c = pair * TILE + q * WINDOW
                                last = nc.tensor.matmul(ps[to, AV, c:c + WINDOW],
                                                        values[:, at_tile, h * HEAD:(h + 1) * HEAD],
                                                        pT[:, pair + 4 * odd, q * WINDOW:(q + 1) * WINDOW],
                                                        start=True, stop=True)
                    last.then_inc(s["av"], 1)

            steps(pe, step, TILES, OUT)

        @block.scalar
        def _(act):
            for name in "qk_copied v_copied square log rnorm qkT_copied prob pT_copied oT_copied".split():
                act.sem_inc(s[name], PRIME)
            act.preload_act_table_set("natural_log_exp_and_others")
            act.wait_ge(s["zeroed"], 3)

            def step(b, i, live):
                g = b * TILES + i
                if live(0) and i < 2:
                    if live(TILES):
                        act.wait_ge(s["proj"], freed(g + 1 - i))
                    nc.scalar.activation(hs[0:64, i * CH:(i + 1) * CH], branch[0:64, cols(b * 2 + i)], ACT.Copy)
                    nc.scalar.activation(hs[64:128, 1 + i * CH:1 + (i + 1) * CH], branch[64:128, cols(b * 2 + i)],
                                         ACT.Copy).then_inc(s["hs"], 1)
                if live(SCORE):
                    n, at_tile = g - SCORE, (i - SCORE) % TILES
                    act.wait_ge(s["qkT"], done(n))
                    act.wait_ge(s["sim"], freed(n))
                    nc.scalar.activation(qT[:, at_tile % 2], ps[:, TURN].rearrange("p (m t) -> p m t", m=4), ACT.Copy)
                    at = WINDOW + at_tile * TILE
                    nc.scalar.activation(kT[:, :, at:at + TILE], ps[:, TURN + 1].rearrange("p (m t) -> p m t", m=4),
                                         ACT.Copy).then_inc(s["qkT_copied"], 1)
                if live(EXP):
                    n, half = g - EXP, (i - EXP) % 2
                    act.wait_ge(s["shifted"], done(n))
                    nc.scalar.activation(prob[:, half], prob[:, half], ACT.Exp).then_inc(s["prob"], 1)
                if live(NORM):
                    n, half = g - NORM, (i - NORM) % 2
                    act.wait_ge(s["floor"], done(n))
                    nc.scalar.activation(log[:, half], floor[:, half], ACT.Ln, scale=2.0 ** 30).then_inc(s["log"], 1)
                    act.wait_ge(s["log"], done(n))
                    act.wait_ge(s["scaled"], freed(n))
                    nc.scalar.activation(rnorm[:, half], log[:, half], ACT.Exp, scale=-0.5,
                                         bias=float(15 * np.log(2.0))).then_inc(s["rnorm"], 1)
                if live(0):
                    act.wait_ge(s["proj"], done(g))
                    act.wait_ge(s["crossed"], freed(g))
                    nc.scalar.activation(qk[:, i % 2], ps[:, Q:Q + 2].rearrange("p a n -> p (a n)"), ACT.Copy
                                         ).then_inc(s["qk_copied"], 1)
                    nc.scalar.activation(v[:, i], ps[:, V], ACT.Copy)
                    nc.scalar.activation(v_mix[0:64, i], ps[0:64, V], ACT.Copy).then_inc(s["v_copied"], 1)
                if live(VALUE):
                    n = g - VALUE
                    act.wait_ge(s["pT"], done(n))
                    act.wait_ge(s["av"], freed(n + 1))
                    nc.scalar.activation(pT[:].rearrange("p h j -> p (h j)"),
                                         ps[:, TURN:TURN + 2].rearrange("p a n -> p (a n)"), ACT.Copy
                                         ).then_inc(s["pT_copied"], 1)
                if live(0):
                    act.wait_ge(s["qk_copied"], done(g))
                    act.wait_ge(s["added"], freed(g))
                    nc.scalar.activation(square[:, i % 2], qk[:, i % 2], ACT.Square).then_inc(s["square"], 1)
                if live(VALUE):
                    n, half = g - VALUE, (i - VALUE) % 2
                    act.wait_ge(s["av"], done(n))
                    act.wait_ge(s["wo"], freed(n))
                    nc.scalar.activation(oT[:, half], ps[:, AV].rearrange("p (m t) -> p m t", m=4), ACT.Copy
                                         ).then_inc(s["oT_copied"], 1)

            steps(act, step, TILES, OUT)

        @block.gpsimd
        def _(pool):
            for name in "added scaled weighted".split():
                pool.sem_inc(s[name], PRIME)

            def step(b, i, live):
                g = b * TILES + i
                if live(NORM):
                    n = g - NORM
                    half, quarter = (i - NORM) % 2, (i - NORM) % 4
                    pool.wait_ge(s["crossed"], done(n))
                    nc.gpsimd.tensor_tensor(direct[:, quarter], direct[:, quarter], crossed[:, half], ALU.add
                                            ).then_inc(s["added"], 1)
                if live(EXP):
                    n, half = g - EXP, (i - EXP) % 2
                    pool.wait_ge(s["inv"], done(n))
                    nc.gpsimd.tensor_tensor(prob[:, half], prob[:, half],
                                            inv[:, half].unsqueeze(2).broadcast_to([P, HEADS, TILE]), ALU.mult
                                            ).then_inc(s["weighted"], 1)
                if live(NORM):
                    n = g - NORM
                    half, quarter = (i - NORM) % 2, (i - NORM) % 4
                    heads = direct[:, quarter].rearrange("p (h e) -> p h e", e=HEAD)
                    pool.wait_ge(s["added"], done(n))
                    pool.wait_ge(s["rnorm"], done(n))
                    nc.gpsimd.tensor_tensor(heads, heads,
                                            rnorm[:, half].unsqueeze(2).broadcast_to([P, 2 * HEADS, HEAD]),
                                            ALU.mult).then_inc(s["scaled"], 1)

            steps(pool, step, TILES, OUT)

        @block.vector
        def _(dve):
            for name in "v_mixed sums floor direct crossed peak shifted total inv branch".split():
                dve.sem_inc(s[name], PRIME)
            nc.vector.memset(hs[64:128, 0:1], 0.0).then_inc(s["zeroed"], 1)
            nc.vector.memset(kT[:, :, 0:WINDOW], 0.0).then_inc(s["zeroed"], 1)
            nc.vector.memset(v_mix[64:128, 0], 0.0).then_inc(s["zeroed"], 1)
            dve.wait_ge(s["zeroed"], 3)
            for n in range(2):
                nc.vector.tensor_tensor(turn[:, n], turn[:, n],
                                        scales[:, n].unsqueeze(1).broadcast_to([P, TILES, 2, HEAD]), ALU.mult
                                        ).then_inc(s["tables_ready"], 1)
            dve.wait_ge(s["tables_ready"], 2)

            def step(b, i, live):
                g = b * TILES + i
                if live(NORM):
                    n, at_tile = g - NORM, (i - NORM) % TILES
                    p = at_tile % 2
                    dve.wait_ge(s["square"], done(n))
                    nc.vector.tensor_reduce(sums[:, p], square[:, p].rearrange("p (h d) -> p h d", d=HEAD), AX_X,
                                            ALU.add).then_inc(s["sums"], 1)
                    dve.wait_ge(s["sums"], done(n))
                    nc.vector.tensor_scalar(floor[:, p], sums[:, p], 1e-24, None, ALU.max).then_inc(s["floor"], 1)
                    if live(NORM + 4):
                        dve.wait_ge(s["qkT"], done(n - 4))
                    for m in range(2):
                        of = qk[:, p, m * INNER:(m + 1) * INNER].rearrange("p (h d) -> p h d", d=HEAD)
                        to = direct[:, at_tile % 4, m * INNER:(m + 1) * INNER].rearrange("p (h d) -> p h d", d=HEAD)
                        last = nc.vector.tensor_tensor(
                            to, of, turn[:, 0, at_tile, m:m + 1].broadcast_to([P, HEADS, HEAD]), ALU.mult)
                    last.then_inc(s["direct"], 1)
                    for half in range(2):
                        h0, h1 = 32 * half, 32 * (1 - half)
                        for m in range(2):
                            of = qk[:, p, m * INNER:(m + 1) * INNER].rearrange("p (h d) -> p h d", d=HEAD)
                            to = crossed[:, p, m * INNER:(m + 1) * INNER].rearrange("p (h d) -> p h d", d=HEAD)
                            last = nc.vector.tensor_tensor(
                                to[:, :, h0:h0 + 32], of[:, :, h1:h1 + 32],
                                turn[:, 1, at_tile, m:m + 1, h0:h0 + 32].broadcast_to([P, HEADS, 32]), ALU.mult)
                    last.then_inc(s["crossed"], 1)
                if live(EXP):
                    n, half = g - EXP, (i - EXP) % 2
                    dve.wait_ge(s["prob"], done(n))
                    nc.vector.tensor_reduce(total[:, half], prob[:, half], AX_X, ALU.add).then_inc(s["total"], 1)
                    dve.wait_ge(s["total"], done(n))
                    dve.wait_ge(s["weighted"], freed(n))
                    nc.vector.reciprocal(inv[:, half], total[:, half]).then_inc(s["inv"], 1)
                if live(SCORE):
                    n, half = g - SCORE, (i - SCORE) % 2
                    dve.wait_ge(s["sim"], done(n))
                    scores = ps[:, SIM:SIM + 2].rearrange("p a (h j) -> p (a h) j", h=4)
                    nc.vector.tensor_reduce(peak[:, half], scores, AX_X, ALU.max).then_inc(s["peak"], 1)
                    dve.wait_ge(s["peak"], done(n))
                    dve.wait_ge(s["pT"], freed(n))
                    nc.vector.tensor_tensor(prob[:, half], scores,
                                            peak[:, half].unsqueeze(2).broadcast_to([P, HEADS, TILE]),
                                            ALU.subtract).then_inc(s["shifted"], 1)
                if live(0) and i > 0:
                    dve.wait_ge(s["v_copied"], done(g - 1))
                    nc.vector.tensor_copy(v_mix[64:128, i], v[64:128, i - 1]).then_inc(s["v_mixed"], 1)
                if live(OUT):
                    n = g - OUT
                    at = branch[:, cols(n, TILE)]
                    dve.wait_ge(s["wo"], done(n))
                    nc.vector.tensor_tensor(at, at, ps[:, V, 0:TILE], ALU.add).then_inc(s["branch"], 1)

            steps(dve, step, TILES, OUT)


GLU = "lb_done biased folded up act prod down branch"


PARTS_OF_HID = len(HID_PARTS)


def through(t, c):
    return (t + 1) * PARTS_OF_HID + c + 1


def gated_mlp(nc, mem, dram, layer):
    branch, x = mem["branch"], mem["x"]
    with ExitStack() as ctx:
        def sb(name, shape, dt=F32):
            return ctx.enter_context(nc.sbuf_tensor(f"glu{layer}_{name}", shape, dt))

        w1 = sb("w1", [P, 2 * HID])
        w2 = sb("w2", [P, 3, P])
        ln_g = sb("ln_g", [P, 1])
        ln_b = sb("ln_b", [P, 1])
        b1 = sb("b1", [P, 2, 3])
        b2 = sb("b2", [P, 1])
        normed = sb("normed", [P, ALL])
        loads = [(w1[:], dram["w1"][layer]), (ln_g[:], dram["ln_g"][layer]),
                 (ln_b[:], dram["ln_b"][layer]), (b2[:], dram["b2"][layer]),
                 (b1[:], dram["b1"][layer])]
        for c, (first, size) in enumerate(HID_PARTS):
            loads.append((w2[0:size, c], dram["w2"][layer, first:first + size]))
        if layer == 0:
            loads += attend_loads(mem, dram, 1)
        layer_norm(nc, mem, f"glu{layer}_norm", branch, normed, shifted=True, loads=loads)
        gelu = sb("gelu", [P, 2, 3, CH])
        prod = sb("prod", [P, 2, 3, CH])
        bank = [ctx.enter_context(nc.psum_tensor(f"glu{layer}_bank{n}", [P, CH], F32)) for n in range(8)]
        s = dict(zip(GLU.split(), semaphores(ctx, nc, f"glu{layer}", GLU)))
        (x_sem,) = semaphores(ctx, nc, f"glu{layer}", "x")
        block = ctx.enter_context(nc.Block())

        @block.tensor
        def _(pe):
            pe.sem_inc(s["up"], PARTS_OF_HID)
            pe.sem_inc(s["down"], PRIME)
            for m in range(2):
                for c, (first, size) in enumerate(HID_PARTS):
                    last = nc.tensor.matmul(bank[6][0:size, 3 * m + c:3 * m + c + 1],
                                            w1[:, m * HID + first:m * HID + first + size], ln_b[:],
                                            start=True, stop=True)
            last.then_inc(s["lb_done"], 1)
            pe.wait_ge(s["folded"], 1)

            def up(t):
                for c, (first, size) in enumerate(HID_PARTS):
                    pe.wait_ge(s["prod"], through(t - 1, c))
                    for m in (1, 0):
                        last = nc.tensor.matmul(bank[3 * m + c][0:size, :],
                                                w1[:, m * HID + first:m * HID + first + size],
                                                normed[:, cols(t)], start=True, stop=True)
                    last.then_inc(s["up"], 1)

            def down(t, k):
                pe.wait_ge(s["prod"], through(t, PARTS_OF_HID - 1))
                pe.wait_ge(s["branch"], freed(t))
                for c, (first, size) in enumerate(HID_PARTS):
                    last = nc.tensor.matmul(bank[6 + k][:], w2[0:size, c], prod[0:size, k, c],
                                            start=c == 0, stop=c == 2)
                last.then_inc(s["down"], 1)

            up(0)
            with pe.Fori(0, SEQS - 1) as b:
                for k in range(2):
                    t = b * 2 + k
                    up(t + 1)
                    down(t, k)
            up(2 * SEQS - 1)
            down(2 * SEQS - 2, 0)
            down(2 * SEQS - 1, 1)

        @block.scalar
        def _(act):
            act.sem_inc(s["act"], PARTS_OF_HID)
            act.preload_act_table_set("gelu_and_others")
            with act.Fori(0, SEQS) as b:
                for k in range(2):
                    t = b * 2 + k
                    for c, (first, size) in enumerate(HID_PARTS):
                        act.wait_ge(s["up"], through(t, c))
                        nc.scalar.activation(gelu[0:size, k, c], bank[3 + c][0:size, :], ACT.Gelu,
                                             bias=b1[0:size, 1, c:c + 1]).then_inc(s["act"], 1)

        @block.vector
        def _(dve):
            dve.sem_inc(s["prod"], PARTS_OF_HID)
            dve.sem_inc(s["branch"], PRIME)
            dve.wait_ge(s["lb_done"], 1)
            for c, (first, size) in enumerate(HID_PARTS):
                last = nc.vector.tensor_tensor(
                    b1[0:size, :, c], b1[0:size, :, c],
                    bank[6][0:size, 0:6].rearrange("p (m c) -> p m c", m=2)[:, :, c], ALU.add)
            last.then_inc(s["biased"], 1)
            nc.vector.tensor_scalar(w1[:], w1[:], ln_g[:, 0:1], None, ALU.mult).then_inc(s["folded"], 1)
            dve.wait_ge(s["biased"], 1)

            def gated(t, k):
                dve.wait_ge(s["down"], freed(t))
                for c, (first, size) in enumerate(HID_PARTS):
                    dve.wait_ge(s["act"], through(t, c))
                    nc.vector.scalar_tensor_tensor(prod[0:size, k, c], bank[c][0:size, :], b1[0:size, 0, c:c + 1],
                                                   gelu[0:size, k, c], ALU.add, ALU.mult).then_inc(s["prod"], 1)

            def added(t, k):
                at = branch[:, cols(t)]
                dve.wait_ge(s["down"], done(t))
                nc.vector.scalar_tensor_tensor(at, bank[6 + k][:], b2[:, 0:1], at, ALU.add, ALU.add
                                               ).then_inc(s["branch"], 1)
                if layer == 1:
                    dve.wait_ge(s["branch"], done(t))
                    nc.vector.tensor_tensor(x[:, cols(t)], x[:, cols(t)], at, ALU.add).then_inc(x_sem, 1)

            gated(0, 0)
            with dve.Fori(0, SEQS - 1) as b:
                for k in range(2):
                    t = b * 2 + k
                    gated(t + 1, 1 - k)
                    added(t, k)
            gated(2 * SEQS - 1, 1)
            added(2 * SEQS - 2, 0)
            added(2 * SEQS - 1, 1)


def store_result(nc, mem, out):
    with ExitStack() as ctx:
        (stored,) = semaphores(ctx, nc, "end", "stored")
        block = ctx.enter_context(nc.Block())

        @block.sync
        def _(sp):
            sp.dma_start(out, mem["x"][:]).then_inc(stored, 16)
            sp.wait_ge(stored, 16)


def attend_first(nc, mem, dram):
    attend(nc, mem, dram, 0)


def gated_mlp_first(nc, mem, dram):
    gated_mlp(nc, mem, dram, 0)


def attend_second(nc, mem, dram):
    attend(nc, mem, dram, 1)


def gated_mlp_second(nc, mem, dram):
    gated_mlp(nc, mem, dram, 1)


STAGES = [min_gru, experts, mamba, mlp, normalise, attend_first, gated_mlp_first, attend_second, gated_mlp_second]


def program(nc, dram, out, stages=None):
    with ExitStack() as ctx:
        mem = {name: ctx.enter_context(nc.sbuf_tensor(name, shape, F32)) for name, shape in (
            ("x", [P, ALL]), ("branch", [P, ALL]), ("centre", [P, P]), ("mean", [P, P]), ("ident", [P, P]))}
        load_constants(nc, mem, dram)
        nc.all_engine_barrier()
        for stage in STAGES if stages is None else stages:
            if stage is normalise:
                mem.update(attend_operands(ctx, nc))
            stage(nc, mem, dram)
            nc.all_engine_barrier()
        store_result(nc, mem, out)


def shape_constants():
    eye = np.eye(P, dtype=np.float32)
    mean = np.full((P, P), 1.0 / P, np.float32)
    pick = np.zeros((P, 32, P), np.float32)
    for first in (0, 64, 96):
        pick[first + np.arange(32), np.arange(32)] = 1.0
    query, key = np.arange(TILE)[:, None] % WINDOW, np.arange(TILE)[None, :] % WINDOW
    own = (np.arange(TILE)[:, None] < WINDOW) == (np.arange(TILE)[None, :] < WINDOW)
    masked = np.where(own, key > query, query > key)
    first = masked | ((np.arange(TILE)[:, None] < WINDOW) & (np.arange(TILE)[None, :] >= WINDOW))
    mask = np.where(np.stack([masked, first], 1), np.float32(-1e30), np.float32(0))
    half = np.arange(0, HEAD, 2, dtype=np.float32)
    inv_freq = (np.float32(1.0) / np.float32(10000.0) ** (half / np.float32(HEAD))).astype(np.float32)
    t = np.arange(T, dtype=np.float32)
    freqs = t[:, None] * inv_freq[None, :]
    base = (half + np.float32(0.4 * HEAD)) / np.float32(1.4 * HEAD)
    scale = base[None, :] ** ((t - T // 2) / np.float32(WINDOW // 2))[:, None]
    turn = np.zeros((2, T, 2, HEAD), np.float32)
    for n, size in ((0, 8.0 * scale), (1, 1.0 / scale)):
        turn[0, :, n] = np.tile(np.cos(freqs) * size, 2)
        turn[1, :, n] = np.concatenate([-np.sin(freqs) * size, np.sin(freqs) * size], 1)
    turn = turn.reshape(2, TILES, P, 2, HEAD).transpose(2, 0, 1, 3, 4)
    bf16 = mybir.dt.np(BF16)
    order = np.arange(E, 0, -1, dtype=np.float32)[None, :]
    index = np.arange(BLOCKS, dtype=np.float32)[None, :]
    going = np.ones((E, TOKEN_TILES), np.float32)
    going[:, 0] = 0.0
    return {"before": np.triu(np.ones((P, P), np.float32), 1), "index": index, "going": going.reshape(1, -1), "order": order, "eye16": eye.astype(bf16), "mask": mask.astype(bf16), "turn": turn, "ident": eye, "mean": mean, "centre": eye - mean, "pick": pick.astype(mybir.dt.np(BF16))}


def laid_out(i):
    def halves(v):
        return v.reshape(2, P, *v.shape[1:]).swapaxes(0, 1)

    x_proj = i["L1_attn_x_proj_w"].T
    dbc = np.zeros((2 * P, P), x_proj.dtype)
    dbc[:, 32:40] = x_proj[:, 0:8]
    for first in (0, 64, 96):
        dbc[:, first:first + 32] = x_proj[:, 8:40]
    fc2 = i["L1_attn_fc2_w"].T
    b1 = np.zeros((2, 2, 3 * P), i["L1_ffn_b1"].dtype)
    b1[:, :, 0:HID] = i["L1_ffn_b1"].reshape(2, 2, HID)
    return {
        "router_w": i["L0_ffn_router_w"],
        "router_b": i["L0_ffn_router_b"][None, :],
        "moe_w1": i["L0_ffn_W1"],
        "moe_w2": i["L0_ffn_W2"],
        "moe_b1": i["L0_ffn_b1"].reshape(8, 4, P).transpose(2, 0, 1),
        "moe_b2": i["L0_ffn_b2"][None],
        "wqkv": i["L1_ffn_wqkv"],
        "wo": i["L1_ffn_wo"],
        "q_scale": i["L1_ffn_q_scale"],
        "k_scale": i["L1_ffn_k_scale"],
        "ln_g": i["L1_ffn_ln_g"][:, :, None],
        "ln_b": i["L1_ffn_ln_b"][:, :, None],
        "w1": i["L1_ffn_w1"],
        "b1": b1.reshape(2, 2, 3, P).transpose(0, 3, 1, 2),
        "w2": i["L1_ffn_w2"],
        "b2": i["L1_ffn_b2"][:, :, None],
        "in_w": i["L1_attn_in_proj_w"].T,
        "dbc_w": halves(dbc),
        "dt_w": i["L1_attn_dt_proj_w"].T,
        "out_w": halves(i["L1_attn_out_proj_w"].T),
        "rms1": i["L1_attn_rms1_w"][:, None],
        "conv_w": halves(i["L1_attn_conv_w"]),
        "conv_b": halves(i["L1_attn_conv_b"]),
        "dt_b": halves(i["L1_attn_dt_proj_b"]),
        "skip": halves(i["L1_attn_D_skip"]),
        "a_log": halves(i["L1_attn_A_log"]),
        "rms2": i["L1_attn_rms2_w"][:, None],
        "fc1": i["L1_attn_fc1_w"].T.reshape(P, 2, P),
        "fc2": halves(fc2).reshape(P, 2, 2, P),
        "fc3": halves(i["L1_attn_fc3_w"].T),
        "mlp_b": np.concatenate([i["L1_attn_fc1_b"].reshape(2, P), i["L1_attn_fc2_b"].reshape(2, P),
                                 i["L1_attn_fc3_b"].reshape(1, P)]).T,
        "x": i["L0_attn_h"].reshape(ALL, P).T,
        "gru_w0": i["L0_attn_W0"],
        "gru_w1": i["L0_attn_W1"],
    }


def kernel(**inputs):
    import concourse.bacc as bacc
    from concourse.bass_utils import run_bass_kernel_spmd

    arrays = {k: np.ascontiguousarray(v) for k, v in laid_out({k: np.asarray(v) for k, v in inputs.items()}).items()}
    arrays.update(shape_constants())
    arrays = {f"in_{k}": v for k, v in arrays.items()}
    nc = bacc.Bacc("TRN2", target_bir_lowering=False, num_devices=1)
    dram = {k[3:]: nc.dram_tensor(k, v.shape, mybir.dt.from_np(v.dtype), kind="ExternalInput").ap()
            for k, v in arrays.items()}
    out = nc.dram_tensor("out_x", (P, ALL), F32, kind="ExternalOutput").ap()
    program(nc, dram, out)
    result = run_bass_kernel_spmd(nc, [arrays], core_ids=[0]).results[0]["out_x"]
    return np.ascontiguousarray(np.asarray(result).T).reshape(SEQS, T, P)
```
